# Optimizing a Trainium2 kernel written in Bass

```python
import numpy as np
import jax
import jax.numpy as jnp

def _softmax(x, axis=-1):
    return jax.nn.softmax(x, axis=axis)

def _gelu(x):
    return jax.nn.gelu(x, approximate=True)

def _silu(x):
    return jax.nn.silu(x)

def _sigmoid(x):
    return jax.nn.sigmoid(x)

def _layernorm(x, axis=-1, eps=1e-05):
    m = jnp.mean(x, axis=axis, keepdims=True)
    v = jnp.var(x, axis=axis, keepdims=True)
    return (x - m) / jnp.sqrt(v + eps)

def _scatter_add(tgt, idx, src, axis=0):
    return tgt.at[idx].add(src)

def _segment_sum(src, seg, n):
    return jax.ops.segment_sum(src, seg, n)
kernel_name = 'mk_xattn_ffn_d1_seqx_r8_c3f5f6'

def setup_inputs(seed: int=0):
    np.random.seed(seed)
    _w = jnp.asarray

    def _rec_inputs():
        import jax
        import jax.numpy as jnp
        _rk = jax.random.key(seed)
        x = 7.22e-05 + 1 * jax.random.normal(jax.random.fold_in(_rk, 1), (4, 512, 128), jnp.float32)
        _lenS = 512 - jax.random.randint(jax.random.fold_in(_rk, 7), (4,), 0, max(1, 512 // 4) + 1, jnp.int32)
        _lenS2 = 77 - jax.random.randint(jax.random.fold_in(_rk, 8), (4,), 0, max(1, 77 // 4) + 1, jnp.int32)
        _ctx_1024P = jax.random.normal(jax.random.fold_in(_rk, 11), (4, 16, 128), jnp.float32)
        _ctx_1024c = jax.random.dirichlet(jax.random.fold_in(_rk, 511), 0.3 * jnp.ones((16,), jnp.float32), (4, 77))
        _ctx_1024t = jnp.einsum('bsk,bkd->bsd', _ctx_1024c, _ctx_1024P)
        _ctx_1024t = _ctx_1024t * jax.lax.rsqrt(jnp.mean(jnp.square(_ctx_1024t)) + 1e-12) * 0.953939
        ctx_1024 = 4.13588e-05 + 0.999923 * (_ctx_1024t + 0.3 * jax.random.normal(jax.random.fold_in(_rk, 611), (4, 77, 128), jnp.float32))
        _validS = jnp.arange(512)[None, :] < _lenS[:, None]
        _validS2 = jnp.arange(77)[None, :] < _lenS2[:, None]
        _causal = jnp.tril(jnp.ones((512, 512), dtype=bool))
        mask_BxS2_bf0 = jnp.logical_not(jnp.ones((4, 77), dtype=bool))
        return (x, ctx_1024, mask_BxS2_bf0)
    x, ctx_1024, mask_BxS2_bf0 = _rec_inputs()

    def _L0_xattn_setup():
        import jax, jax.numpy as jnp
        import numpy as np
        DIM = 128
        N_HEAD = 16
        BS, QLEN, KLEN = (4, 256, 256)
        key = jax.random.key(seed)
        ks = jax.random.split(key, 12)
        s = 1.0 / np.sqrt(DIM)
        inp = {'q_in': jax.random.normal(ks[0], (BS, QLEN, DIM), jnp.float32), 'k_in': jax.random.normal(ks[1], (BS, KLEN, DIM), jnp.float32), 'v_in': jax.random.normal(ks[2], (BS, KLEN, DIM), jnp.float32), 'key_padding_mask': jnp.zeros((BS, KLEN), dtype=bool), 'Wq': jax.random.normal(ks[3], (DIM, DIM), jnp.float32) * s, 'bq': jnp.zeros((DIM,), jnp.float32), 'Wk': jax.random.normal(ks[4], (DIM, DIM), jnp.float32) * s, 'bk': jnp.zeros((DIM,), jnp.float32), 'Wv': jax.random.normal(ks[5], (DIM, DIM), jnp.float32) * s, 'bv': jnp.zeros((DIM,), jnp.float32), 'Wo': jax.random.normal(ks[6], (DIM, DIM), jnp.float32) * s, 'bo': jnp.zeros((DIM,), jnp.float32)}
        return inp
    _L0_xattn_all = _L0_xattn_setup()
    _L0_xattn_in = {k: v for k, v in _L0_xattn_all.items() if k in ('Wq', 'bq', 'Wk', 'bk', 'Wv', 'bv', 'Wo', 'bo')}
    del _L0_xattn_all

    def _L0_ffn_setup():
        import jax, jax.numpy as jnp
        import numpy as np
        D = 128
        E = 8
        K = 2
        NUM_ITER = 2
        DT = 0.1
        H = 64
        CTX = 2 * D

        def _gelu(t):
            return jax.nn.gelu(t, approximate=False)

        def _inl(ctrl, x, v, mu):
            alpha_raw, beta_raw, gate_raw = jnp.split(ctrl, 3, axis=-1)
            alpha = jax.nn.sigmoid(alpha_raw)
            beta = jax.nn.softplus(beta_raw)
            gate = jax.nn.sigmoid(gate_raw)
            error = x - mu
            v_next = alpha * v - beta * error
            x_next = x + DT * gate * v_next
            return (x_next, v_next)
        key = jax.random.key(seed)
        ks = jax.random.split(key, 20)
        s = 0.02
        inp = {'x': jax.random.normal(ks[0], (4, 512, D), jnp.float32), 'w_r1': jax.random.normal(ks[1], (D, D // 4), jnp.float32) * s, 'b_r1': jnp.zeros((D // 4,), jnp.float32), 'w_r2': jax.random.normal(ks[2], (D // 4, E), jnp.float32) * s, 'b_r2': jnp.zeros((E,), jnp.float32), 'w_h1': jax.random.normal(ks[3], (D, D // 4), jnp.float32) * s, 'b_h1': jnp.zeros((D // 4,), jnp.float32), 'w_h2': jax.random.normal(ks[4], (D // 4, 1), jnp.float32) * s, 'b_h2': jnp.zeros((1,), jnp.float32), 'expert_w1': jax.random.normal(ks[5], (E, CTX, H), jnp.float32) * s, 'expert_b1': jnp.zeros((E, H), jnp.float32), 'expert_w2': jax.random.normal(ks[6], (E, H, 3 * D), jnp.float32) * s, 'expert_b2': jnp.zeros((E, 3 * D), jnp.float32), 'w_s1': jax.random.normal(ks[7], (CTX, H), jnp.float32) * s, 'b_s1': jnp.zeros((H,), jnp.float32), 'w_s2': jax.random.normal(ks[8], (H, 3 * D), jnp.float32) * s, 'b_s2': jnp.zeros((3 * D,), jnp.float32), 'shared_weight': jnp.asarray(0.5, jnp.float32), 'w_f1': jax.random.normal(ks[9], (D, 2 * D), jnp.float32) * s, 'b_f1': jnp.zeros((2 * D,), jnp.float32), 'w_f2': jax.random.normal(ks[10], (2 * D, D), jnp.float32) * s, 'b_f2': jnp.zeros((D,), jnp.float32), 'integration_weight': jnp.full((D,), 0.5, jnp.float32), 'mu': jnp.zeros((D,), jnp.float32)}
        return inp
    _L0_ffn_all = _L0_ffn_setup()
    _L0_ffn_in = {k: v for k, v in _L0_ffn_all.items() if k in ('w_r1', 'b_r1', 'w_r2', 'b_r2', 'w_h1', 'b_h1', 'w_h2', 'b_h2', 'expert_w1', 'expert_b1', 'expert_w2', 'expert_b2', 'w_s1', 'b_s1', 'w_s2', 'b_s2', 'shared_weight', 'w_f1', 'b_f1', 'w_f2', 'b_f2', 'integration_weight', 'mu')}
    del _L0_ffn_all
    return {'x': x, 'ctx_1024': ctx_1024, 'mask_BxS2_bf0': mask_BxS2_bf0, 'L0_xattn_Wq': _L0_xattn_in['Wq'], 'L0_xattn_bq': _L0_xattn_in['bq'], 'L0_xattn_Wk': _L0_xattn_in['Wk'], 'L0_xattn_bk': _L0_xattn_in['bk'], 'L0_xattn_Wv': _L0_xattn_in['Wv'], 'L0_xattn_bv': _L0_xattn_in['bv'], 'L0_xattn_Wo': _L0_xattn_in['Wo'], 'L0_xattn_bo': _L0_xattn_in['bo'], 'L0_ffn_w_r1': _L0_ffn_in['w_r1'], 'L0_ffn_b_r1': _L0_ffn_in['b_r1'], 'L0_ffn_w_r2': _L0_ffn_in['w_r2'], 'L0_ffn_b_r2': _L0_ffn_in['b_r2'], 'L0_ffn_w_h1': _L0_ffn_in['w_h1'], 'L0_ffn_b_h1': _L0_ffn_in['b_h1'], 'L0_ffn_w_h2': _L0_ffn_in['w_h2'], 'L0_ffn_b_h2': _L0_ffn_in['b_h2'], 'L0_ffn_expert_w1': _L0_ffn_in['expert_w1'], 'L0_ffn_expert_b1': _L0_ffn_in['expert_b1'], 'L0_ffn_expert_w2': _L0_ffn_in['expert_w2'], 'L0_ffn_expert_b2': _L0_ffn_in['expert_b2'], 'L0_ffn_w_s1': _L0_ffn_in['w_s1'], 'L0_ffn_b_s1': _L0_ffn_in['b_s1'], 'L0_ffn_w_s2': _L0_ffn_in['w_s2'], 'L0_ffn_b_s2': _L0_ffn_in['b_s2'], 'L0_ffn_shared_weight': _L0_ffn_in['shared_weight'], 'L0_ffn_w_f1': _L0_ffn_in['w_f1'], 'L0_ffn_b_f1': _L0_ffn_in['b_f1'], 'L0_ffn_w_f2': _L0_ffn_in['w_f2'], 'L0_ffn_b_f2': _L0_ffn_in['b_f2'], 'L0_ffn_integration_weight': _L0_ffn_in['integration_weight'], 'L0_ffn_mu': _L0_ffn_in['mu']}

def reference(x, ctx_1024, mask_BxS2_bf0, L0_xattn_Wq, L0_xattn_bq, L0_xattn_Wk, L0_xattn_bk, L0_xattn_Wv, L0_xattn_bv, L0_xattn_Wo, L0_xattn_bo, L0_ffn_w_r1, L0_ffn_b_r1, L0_ffn_w_r2, L0_ffn_b_r2, L0_ffn_w_h1, L0_ffn_b_h1, L0_ffn_w_h2, L0_ffn_b_h2, L0_ffn_expert_w1, L0_ffn_expert_b1, L0_ffn_expert_w2, L0_ffn_expert_b2, L0_ffn_w_s1, L0_ffn_b_s1, L0_ffn_w_s2, L0_ffn_b_s2, L0_ffn_shared_weight, L0_ffn_w_f1, L0_ffn_b_f1, L0_ffn_w_f2, L0_ffn_b_f2, L0_ffn_integration_weight, L0_ffn_mu):
    import jax
    import jax.numpy as jnp

    def _L0_xattn_ref(q_in, k_in, v_in, key_padding_mask, Wq, bq, Wk, bk, Wv, bv, Wo, bo):
        import jax, jax.numpy as jnp
        import numpy as np
        DIM = 128
        N_HEAD = 16
        BS, QLEN, KLEN = (4, 256, 256)
        bs, q_len, _ = q_in.shape
        k_len = k_in.shape[1]
        h = N_HEAD
        d = DIM // h
        q = (q_in @ Wq + bq).reshape(bs, q_len, h, d).transpose(0, 2, 1, 3)
        k = (k_in @ Wk + bk).reshape(bs, k_len, h, d).transpose(0, 2, 1, 3)
        v = (v_in @ Wv + bv).reshape(bs, k_len, h, d).transpose(0, 2, 1, 3)
        score = jnp.einsum('bhqd,bhkd->bhqk', q, k) / jnp.sqrt(jnp.float32(d))
        mask = key_padding_mask[:, None, None, :]
        score = jnp.where(mask, jnp.float32(-1e+30), score)
        attn = jax.nn.softmax(score, axis=-1)
        out = jnp.einsum('bhqk,bhkd->bhqd', attn, v).transpose(0, 2, 1, 3).reshape(bs, q_len, DIM)
        return out @ Wo + bo

    def _L0_ffn_ref(x, w_r1, b_r1, w_r2, b_r2, w_h1, b_h1, w_h2, b_h2, expert_w1, expert_b1, expert_w2, expert_b2, w_s1, b_s1, w_s2, b_s2, shared_weight, w_f1, b_f1, w_f2, b_f2, integration_weight, mu):
        import jax, jax.numpy as jnp
        import numpy as np
        D = 128
        E = 8
        K = 2
        NUM_ITER = 2
        DT = 0.1
        H = 64
        CTX = 2 * D

        def _gelu(t):
            return jax.nn.gelu(t, approximate=False)

        def _inl(ctrl, x, v, mu):
            alpha_raw, beta_raw, gate_raw = jnp.split(ctrl, 3, axis=-1)
            alpha = jax.nn.sigmoid(alpha_raw)
            beta = jax.nn.softplus(beta_raw)
            gate = jax.nn.sigmoid(gate_raw)
            error = x - mu
            v_next = alpha * v - beta * error
            x_next = x + DT * gate * v_next
            return (x_next, v_next)
        B, N, Dm = x.shape
        xf = x.reshape(B * N, Dm)
        logits = _gelu(xf @ w_r1 + b_r1) @ w_r2 + b_r2
        probs = jax.nn.softmax(logits, axis=-1)
        top_p, top_i = jax.lax.top_k(probs, K)
        top_p = top_p / jnp.sum(top_p, axis=-1, keepdims=True)
        flat_idx = top_i.reshape(-1)
        flat_w = top_p.reshape(-1, 1)
        v = jnp.zeros_like(xf)
        integrated = xf
        for _ in range(NUM_ITER):
            ctx = jnp.concatenate([integrated, v], axis=-1)
            shared_ctrl = _gelu(ctx @ w_s1 + b_s1) @ w_s2 + b_s2
            x_shared, v_shared = _inl(shared_ctrl, integrated, v, mu)
            sw = jax.nn.sigmoid(shared_weight)
            ctx_e = jnp.repeat(ctx, K, axis=0)
            x_e = jnp.repeat(integrated, K, axis=0)
            v_e = jnp.repeat(v, K, axis=0)
            w1 = expert_w1[flat_idx]
            b1 = expert_b1[flat_idx]
            w2 = expert_w2[flat_idx]
            b2 = expert_b2[flat_idx]
            hidden = _gelu(jnp.einsum('tc,tch->th', ctx_e, w1) + b1)
            ctrl = jnp.einsum('th,tho->to', hidden, w2) + b2
            x_r, v_r = _inl(ctrl, x_e, v_e, mu)
            x_r = (x_r * flat_w).reshape(B * N, K, Dm).sum(axis=1)
            v_r = (v_r * flat_w).reshape(B * N, K, Dm).sum(axis=1)
            x_next = sw * x_shared + (1.0 - sw) * x_r
            v_next = sw * v_shared + (1.0 - sw) * v_r
            halt = jax.nn.sigmoid(_gelu(x_next @ w_h1 + b_h1) @ w_h2 + b_h2)
            refined = _gelu(x_next @ w_f1 + b_f1) @ w_f2 + b_f2
            integrated = integrated + halt * refined * integration_weight
            v = v_next
        return integrated.reshape(B, N, Dm)
    x = x + _L0_xattn_ref(_layernorm(x, axis=-1), ctx_1024, ctx_1024, mask_BxS2_bf0, L0_xattn_Wq, L0_xattn_bq, L0_xattn_Wk, L0_xattn_bk, L0_xattn_Wv, L0_xattn_bv, L0_xattn_Wo, L0_xattn_bo)
    x = x + _L0_ffn_ref(_layernorm(x, axis=-1), L0_ffn_w_r1, L0_ffn_b_r1, L0_ffn_w_r2, L0_ffn_b_r2, L0_ffn_w_h1, L0_ffn_b_h1, L0_ffn_w_h2, L0_ffn_b_h2, L0_ffn_expert_w1, L0_ffn_expert_b1, L0_ffn_expert_w2, L0_ffn_expert_b2, L0_ffn_w_s1, L0_ffn_b_s1, L0_ffn_w_s2, L0_ffn_b_s2, L0_ffn_shared_weight, L0_ffn_w_f1, L0_ffn_b_f1, L0_ffn_w_f2, L0_ffn_b_f2, L0_ffn_integration_weight, L0_ffn_mu)
    return x

_drawn_inputs = setup_inputs


def setup_inputs(seed=0):
    import zlib

    import numpy as np

    out = dict(_drawn_inputs(seed))
    spreads = {'L0_xattn_bq': (0.0, 0.324),
     'L0_xattn_bk': (0.0, 2.0),
     'L0_xattn_bv': (0.0, 0.1),
     'L0_xattn_bo': (0.0, 0.1),
     'L0_ffn_b_r1': (0.0, 2.0),
     'L0_ffn_b_r2': (0.0, 2.0),
     'L0_ffn_b_h1': (0.0, 0.8),
     'L0_ffn_expert_b1': (0.0, 2.0),
     'L0_ffn_expert_b2': (0.0, 2.0),
     'L0_ffn_b_s1': (0.0, 2.0),
     'L0_ffn_b_s2': (0.0, 2.0),
     'L0_ffn_b_f1': (0.0, 0.8),
     'L0_ffn_b_f2': (0.0, 0.354),
     'L0_ffn_integration_weight': (0.5, 0.6),
     'L0_ffn_mu': (0.0, 0.8)}
    factors = {'L0_ffn_w_r1': 31.628,
     'L0_ffn_w_r2': 8.0,
     'L0_ffn_w_h1': 8.0,
     'L0_ffn_w_h2': 8.0,
     'L0_ffn_expert_w1': 8.0,
     'L0_ffn_expert_w2': 8.0,
     'L0_ffn_w_s1': 8.0,
     'L0_ffn_w_s2': 8.0,
     'L0_ffn_w_f1': 6.673,
     'L0_ffn_w_f2': 6.137}
    for name, (base, spread) in spreads.items():
        noise = np.random.default_rng([zlib.crc32(name.encode()), seed]).standard_normal(out[name].shape)
        drawn = base * np.exp(spread * noise) if base else spread * noise
        out[name] = jnp.asarray(drawn.astype(out[name].dtype))
    for name, factor in factors.items():
        out[name] = (out[name] * factor).astype(out[name].dtype)
    return out
```

```python
from contextlib import ExitStack

import numpy as np

import concourse.bass as bass
from concourse import mybir

F32 = mybir.dt.float32
F32R = mybir.dt.float32r
BF16 = mybir.dt.bfloat16
U32 = mybir.dt.uint32
U8 = mybir.dt.uint8
ACT = mybir.ActivationFunctionType
ALU = mybir.AluOpType
AX_X = mybir.AxisListType.X

P = 128
B, S, D = 4, 512, 128
KL = 77
NH, DH = 16, 8
NG = 4
NS = 4
ROWS = 32
ONE_ROW = 3 * DH
NT = S // P
E, H = 8, 64
NK = E * H // P
NB = B
NEG = -float(2 ** 100)
EPS = 1e-5
DT = 0.1
SOFTPLUS_CAP = 40.0
G_BANKS = 3
POOL_CLEARS = 14

C_IDENT, C_EXPERT, C_ONEHOT, C_NEG_Q, C_NEG_K, C_SPLIT1, C_SPLIT2, C_END = 0, 128, 132, 133, 134, 135, 136, 137

V_B1, V_BS1, V_BF1, V_BF2, V_MU, V_IW, V_BH1, V_BR1, V_BS2, V_END = 0, 4, 5, 7, 8, 9, 10, 11, 12, 16


def shape_constants():
    c = np.zeros((P, C_END), np.float32)
    p = np.arange(P)
    c[:, C_IDENT:C_IDENT + P] = np.eye(P)
    for k in range(NK):
        c[:, C_EXPERT + k] = 2 * k + p // H
    c[:, C_ONEHOT] = np.where(p < 3 * E, p % E, -1)
    part = p % ROWS // DH
    c[:, C_NEG_Q] = np.where(part == 2, -1, 0)
    c[:, C_NEG_K] = np.where(part == 1, -1, 0)
    c[:, C_SPLIT1] = np.where(p >= E, -1, 0)
    c[:, C_SPLIT2] = np.where(p >= 2 * E, -1, 0)
    return c


def attention_order():
    first = [("ln1", 0, 0), ("setup", 0, 0), ("ln1", 1, 0), ("xT", 0, 0)] + [("q", 0, g) for g in range(NG)]
    first += [("S", 0, g) for g in range(NG)] + [("mT", 0, 0)]
    order = list(first)
    for b in range(B):
        n, m = b + 1, b - 1
        if m >= 0:
            order.append(("norm", m, 0))
        if n < B:
            order += [("xT", n, 0)] + [("q", n, g) for g in range(NG)]
        order.append(("lead", b, 0))
        for h in range(NH):
            order.append(("head", b, h))
            if b == 0 and h == 2:
                order.append(("setup2", 0, 0))
            if n < B:
                if h in (4, 6, 8, 10):
                    order.append(("S", n, (h - 4) // 2))
                if h == 13:
                    order.append(("mT", n, 0))
                if h == 14 and n + 1 < B:
                    order.append(("ln1", n + 1, 0))
            if m >= 0:
                stage = {3: "o", 7: "x2T", 9: "r1", 11: "lg", 15: "bc"}.get(h)
                if stage:
                    order += [(stage, m, k) for k in range(4 if stage == "bc" else 1)]
    m = B - 1
    order += [("norm", m, 0), ("o", m, 0), ("x2T", m, 0), ("r1", m, 0), ("lg", m, 0)] + [("bc", m, k) for k in range(4)]
    return order


def ffn_order():
    order = []
    for s in range(2 * NB):
        order.append(("w1", s, 0))
        if s > 0:
            order.append(("tail", s - 1, 0))
        order.append(("w2", s, 0))
        if s > NB:
            order.append(("fin", s - 1, 0))
        order += [("w2", s, 1), ("w2", s, 2)]
    return order + [("tail", 2 * NB - 1, 0), ("fin", 2 * NB - 1, 0)]


def act_steps(stage, i, k):
    if stage == "w2":
        return 3 if i < NB else 4
    return {"ln1": 2, "setup": 5 + 2 * NG, "xT": 1, "q": 2, "mT": 1, "head": 1, "o": 2, "x2T": 1, "r1": 1,
            "lg": 1, "bc": 1, "w1": NK + 1, "tail": 5}.get(stage, 0)


def dve_steps(stage, i, k):
    if stage == "w2":
        return (6, 7, 10 if i < NB else 11)[k]
    if stage == "bc":
        return k % 2
    return {"ln1": 17, "setup": 25 + NG * NS + NG, "setup2": 14, "q": 1, "S": NT, "norm": 2, "o": 18, "lg": 15,
            "w1": 2 * NK, "tail": 2, "fin": 1}.get(stage, 0)


def pool_steps(stage, i, k):
    return {"ln1": 1, "lg": 4}.get(stage, 0)


class Done:

    def __init__(self, order, steps, total=0):
        self.before, self.steps = {}, steps
        for stage in order:
            self.before[stage] = total
            total += steps(*stage)

    def __call__(self, stage, b, k=0, i=None):
        return self.before[(stage, b, k)] + (self.steps(stage, b, k) if i is None else i)


def bank_jobs(att, ffn):
    jobs, used = {}, [0] * G_BANKS

    def put(key, bank):
        jobs[key] = (bank, used[bank])
        used[bank] += 1
    seq = []
    for stage, b, k in att:
        if stage == "setup":
            seq += [("cols",), ("ctxT",)] + [("kproj", g) for g in range(NG)] + [("vproj",)]
        elif stage in ("xT", "q", "mT", "o", "x2T", "r1", "lg", "bc"):
            seq.append((stage, b, k))
        elif stage == "S":
            seq += [("S", b, k, t) for t in range(NT)]
    for i, key in enumerate(seq):
        put(key, i % G_BANKS)
    seq = []
    for stage, s, k in ffn:
        if stage == "w1":
            seq += [("w1", s, j) for j in range(NK + 1)]
        elif stage == "tail":
            seq += [(j, s) for j in ("h1", "f1a", "f1b", "h2", "f2")]
        elif stage == "fin":
            seq.append(("fin", s))
    for i, key in enumerate(seq):
        put(key, i % 2)
    return jobs


def xattn_moe_kernel(nc, x, ctx, mask, Wq, bq, Wk, bk, Wv, bv, Wo, bo, w_r1, b_r1, w_r2, b_r2, w_h1, b_h1,
                     w_h2, b_h2, e_w1, e_b1, e_w2, e_b2, w_s1, b_s1, w_s2, b_s2, shared_weight, w_f1, b_f1,
                     w_f2, b_f2, iw, mu, consts, out):
    att, ffn = attention_order(), ffn_order()
    jobs = bank_jobs(att, ffn)
    act_at, dve_at = Done(att + ffn, act_steps), Done(att + ffn, dve_steps)
    pool_at = Done(att, pool_steps, POOL_CLEARS + 1)
    with ExitStack() as stack:
        def sb(name, shape, dt=F32):
            return stack.enter_context(nc.sbuf_tensor(name, shape, dt))

        def sem(name):
            return stack.enter_context(nc.semaphore(name))

        cst = sb("cst", [P, C_END])
        ident = cst[:, C_IDENT:C_IDENT + P]
        ident_bf = sb("ident_bf", [P, P], BF16)
        ones = sb("ones", [P, P])
        ones_bf = sb("ones_bf", [P, P], BF16)
        x_tok = sb("x_tok", [P, B, NT, D])
        bo_row = sb("bo_row", [P, D])
        stats = sb("stats", [P, 2, NT, 6])
        mv = sb("mv", [P, 2, NT, 2])
        rs = sb("rs", [P, 2, 5, NT])
        xn = sb("xn", [P, 2, NT, D])
        xnT = sb("xnT", [P, 2, S])
        q_full = sb("q_full", [P, 2, S])
        q_hi = sb("q_hi", [P, 2, S], F32R)
        qs = sb("qs", [P, 2, NG, S], F32R)
        KB = sb("KB", [P, B, NG, NS, KL], F32R)
        VB = sb("VB", [P, B, NS, NG, ROWS])
        OB = sb("OB", [P, NG, ROWS])
        ctx_tok = sb("ctx_tok", [KL, B, D])
        ctxT = sb("ctxT", [P, B * KL])
        bv_row = sb("bv_row", [KL, D])
        mask_words = sb("mask_words", [1, B * KL // 4], U32)
        mask_row = sb("mask_row", [1, B * KL])
        sel_mask = sb("sel_mask", [1, NS, ROWS])
        qk_rows = sb("qk_rows", [1, 2, D])
        qk_arr = sb("qk_arr", [1, 2, NG, NS, ROWS])
        qk_cols = sb("qk_cols", [P, 2 * NG])
        Wq_sb, Wk_sb, Wv_sb, Wo_sb = (sb(n, [P, D]) for n in ("Wq_sb", "Wk_sb", "Wv_sb", "Wo_sb"))
        WqA = sb("WqA", [P, NG, NS, ROWS])
        WkA = sb("WkA", [P, NG, NS, ROWS])
        sel_max = sb("sel_max", [P, NH, KL], F32R)
        m_tok = sb("m_tok", [P, 2, NT, P])
        mT = sb("mT", [P, 2, S], F32R)
        PT = sb("PT", [P, 3, S])
        rden = sb("rden", [P, S])
        oT = sb("oT", [P, 2, S])
        w_r1_sb = sb("w_r1_sb", [P, D // 4])
        w_r2_sb = sb("w_r2_sb", [D // 4, E])
        br2_row = sb("br2_row", [P, E])
        hr = sb("hr", [D // 4, S])
        logits = sb("logits", [P, NT, E])
        mx = sb("mx", [P, NT, 8])
        mi = sb("mi", [P, NT, 8], U32)
        wk = sb("wk", [P, 6, NT])
        idxf = sb("idxf", [P, 2, NT])
        diag_w = sb("diag_w", [P, 2, NT, P])
        diag_i = sb("diag_i", [P, 2, NT, P], BF16)
        vec_rows = sb("vec_rows", [V_END, P])
        cols = sb("cols", [P, V_END])
        half = sb("half", [P, 6])
        bh2 = sb("bh2", [P, 1])
        shw = sb("shw", [P, 3])
        w1_sb = sb("w1_sb", [P, 2, E, H])
        ws1_sb = sb("ws1_sb", [P, 2, 2, H])
        w2_sb = sb("w2_sb", [P, NK, 3 * D])
        ws2_sb = sb("ws2_sb", [P, 3 * D])
        b2_rep = sb("b2_rep", [3 * E, 3 * D])
        b2_hi = sb("b2_hi", [3 * E, 3 * D], BF16)
        b2_s = sb("b2_s", [P, 3 * D], BF16)
        wf1_sb = sb("wf1_sb", [P, 2 * D])
        wf2_sb = sb("wf2_sb", [P, 2, D])
        wh1_sb = sb("wh1_sb", [P, P])
        wh2_col = sb("wh2_col", [P, 1])
        wh2_sb = sb("wh2_sb", [P, P])
        xT = sb("xT", [P, NB, S])
        Wb = sb("Wb", [P, 2, NB, S])
        Ib = sb("Ib", [P, 2, NB, S], BF16)
        OH = sb("OH", [P, 2, NB, S], BF16)
        hid = sb("hid", [P, NK + 1, S])
        mh = sb("mh", [P, 2, NK, S])
        vT = VB[:].rearrange("p b j g r -> p b (j g r)")
        st_b, st_g = (t[:].rearrange("p u t d -> p u (t d)") for t in (xn, m_tok))
        st_b, st_g = [st_b[:, u, :] for u in range(2)], [st_g[:, u, :] for u in range(2)]
        st_a = [t[:].rearrange("p g j r -> p (g j r)") for t in (WqA, WkA)]
        acc_g, acc_a = (diag_w[:, u].rearrange("p t d -> p (t d)") for u in range(2))
        nerr, tmp = q_full[:, 0, :], q_full[:, 1, :]
        xnext, hh = xnT[:, 0, :], xnT[:, 1, :]
        fh = oT
        th, rf, zf = rden, PT[:, 0, :], PT[:, 1, :]

        bank = [stack.enter_context(nc.psum_tensor(f"bank{i}", [P, 512], F32)) for i in range(8)]
        G = bank[0:3]
        ST = bank[3:6]
        NUM, DEN = bank[6], bank[7]
        CT = [[bank[3], bank[4], bank[5]], [bank[6], bank[7], bank[2]]]

        const_in, vec_in, attw_in, ctx_in, ffnw_in = (sem(n) for n in ("const_in", "vec_in", "attw_in", "ctx_in", "ffnw_in"))
        x_in = [sem(f"x_in{b}") for b in range(B)]
        out_done = sem("out_done")
        act_done, dve_done, pool_done = sem("act_done"), sem("dve_done"), sem("pool_done")
        bank_full = [sem(f"bank_full{i}") for i in range(G_BANKS)]
        scores_full, pv_done, stream_full = sem("scores_full"), sem("pv_done"), sem("stream_full")

        block = stack.enter_context(nc.Block())
        N_VEC, N_ATT, N_CTX, N_FFN = 11, 6, 5, 18

        def chunks(s):
            return 2 if s < NB else 3

        def chunk_no(s, k, q):
            return sum(3 * chunks(i) for i in range(s)) + k * chunks(s) + q

        def read_by(key):
            kind, *r = key
            act_reads = {"cols": ("setup", 0, 0, 3), "ctxT": ("setup", 0, 0, 4)}
            if kind in act_reads:
                return act_done, act_at(*act_reads[kind])
            if kind == "kproj":
                return act_done, act_at("setup", 0, 0, 4 + 2 * (r[0] + 1))
            if kind == "vproj":
                return dve_done, dve_at("setup", 0)
            if kind == "S":
                return dve_done, dve_at("S", r[0], r[1], r[2] + 1)
            if kind in ("o", "lg"):
                return dve_done, dve_at(kind, r[0], 0, 1)
            if kind == "fin":
                return dve_done, dve_at("fin", r[0])
            if kind == "w1":
                return act_done, act_at("w1", r[0], 0, r[1] + 1)
            if kind in ("h1", "f1a", "f1b", "h2", "f2"):
                return act_done, act_at("tail", r[0], 0, ("h1", "f1a", "f1b", "h2", "f2").index(kind) + 1)
            return act_done, act_at(kind, r[0], r[1])

        before = {}
        for key, (i, n) in jobs.items():
            if n:
                before[key] = next(o for o, at in jobs.items() if at == (i, n - 1))
        last_g2 = next(o for o, at in jobs.items() if at == (2, max(n for i, n in jobs.values() if i == 2)))

        def await_product(eng, key):
            i, n = jobs[key]
            eng.wait_ge(bank_full[i], n + 1)
            return G[i]

        @block.sync
        def _(sp):
            def load(dst, src, signal):
                with nc.allow_non_contiguous_dma(reason="small parameters"):
                    sp.dma_start(dst, src).then_inc(signal, 16)

            def row(v):
                return v.rearrange("(a n) -> a n", a=1)

            load(x_tok[:, 0], x[0].rearrange("(t p) d -> p t d", p=P), x_in[0])
            load(cst[:], consts, const_in)
            load(ctx_tok[:], ctx.rearrange("b k d -> k b d"), ctx_in)
            load(mask_words[:], row(mask), ctx_in)
            load(bv_row[:], bv.partition_broadcast(KL), ctx_in)
            load(Wk_sb[:], Wk, ctx_in)
            load(Wv_sb[:], Wv, ctx_in)
            load(Wq_sb[:], Wq, attw_in)
            load(qk_rows[0:1, 0, :], row(bq), attw_in)
            load(qk_rows[0:1, 1, :], row(bk), attw_in)
            load(Wo_sb[:], Wo, attw_in)
            load(bo_row[:], bo.partition_broadcast(P), attw_in)
            load(br2_row[:], b_r2.partition_broadcast(P), attw_in)
            sp.wait_ge(pool_done, 4)
            load(vec_rows[V_B1:V_B1 + 4, :], e_b1.rearrange("(k e) h -> k (e h)", e=2), vec_in)
            load(vec_rows[V_BS1:V_BS1 + 1, 0:H], row(b_s1), vec_in)
            load(vec_rows[V_BS1:V_BS1 + 1, H:P], row(b_s1), vec_in)
            load(vec_rows[V_BF1:V_BF1 + 2, :], b_f1.rearrange("(a n) -> a n", a=2), vec_in)
            load(vec_rows[V_BF2:V_BF2 + 1, :], row(b_f2), vec_in)
            load(vec_rows[V_MU:V_MU + 1, :], row(mu), vec_in)
            load(vec_rows[V_IW:V_IW + 1, :], row(iw), vec_in)
            load(vec_rows[V_BH1:V_BH1 + 1, 0:D // 4], row(b_h1), vec_in)
            load(vec_rows[V_BR1:V_BR1 + 1, 0:D // 4], row(b_r1), vec_in)
            load(vec_rows[V_BS2:V_BS2 + 3, :], b_s2.rearrange("(a n) -> a n", a=3), vec_in)
            load(shw[:, 0:1], shared_weight.partition_broadcast(P), vec_in)
            for b in range(1, B):
                load(x_tok[:, b], x[b].rearrange("(t p) d -> p t d", p=P), x_in[b])
            load(w_r1_sb[:], w_r1, ffnw_in)
            load(w_r2_sb[:], w_r2, ffnw_in)
            for f in range(2):
                load(w1_sb[:, f], e_w1.rearrange("e (f c) h -> f c e h", f=2)[f], ffnw_in)
                for r in range(2):
                    load(ws1_sb[:, f, r], w_s1.rearrange("(f c) h -> f c h", f=2)[f], ffnw_in)
            load(w2_sb[:], e_w2.rearrange("(k e) h o -> (e h) k o", e=2), ffnw_in)
            load(ws2_sb[0:H], w_s2, ffnw_in)
            for r in range(3):
                load(b2_rep[r * E:(r + 1) * E], e_b2, ffnw_in)
            load(wf1_sb[:], w_f1, ffnw_in)
            load(wf2_sb[:], w_f2.rearrange("(a c) n -> c a n", a=2), ffnw_in)
            load(wh1_sb[:, 0:D // 4], w_h1, ffnw_in)
            load(wh2_col[0:D // 4], w_h2, ffnw_in)
            load(bh2[:], b_h2.partition_broadcast(P), ffnw_in)
            for b in range(B):
                sp.wait_ge(dve_done, dve_at("fin", NB + b))
                sp.dma_start(out[b].rearrange("(t p) d -> p t d", p=P), x_tok[:, b]).then_inc(out_done, 16)
            sp.wait_ge(out_done, 16 * B)

        @block.gpsimd
        def _(pool):
            n = [0]

            def step(ins):
                ins.then_inc(pool_done, 1)
                n[0] += 1
                if n[0] > 1:
                    pool.wait_ge(pool_done, n[0] - 1)

            def clears():
                tiles = [vec_rows[:], ws2_sb[:], wh1_sb[:], wh2_col[:], WqA[:], WkA[:], qk_arr[:], sel_mask[:],
                         VB[:], OB[:], b2_s[:], m_tok[:], PT[:], KB[:].bitcast(F32)]
                assert len(tiles) == POOL_CLEARS
                for t in tiles:
                    step(pool.memset(t, 0.0))
                pool.wait_ge(const_in, 16)
                step(pool.tensor_copy(ident_bf[:], ident))

            clears()
            for stage, b, k in att:
                if stage == "ln1":
                    pool.wait_ge(attw_in, 16 * N_ATT)
                    pool.wait_ge(dve_done, dve_at("ln1", b))
                    step(pool.tensor_tensor(x_tok[:, b], x_tok[:, b], bo_row[:].unsqueeze(1).to_broadcast([P, NT, D]), ALU.add))
                elif stage == "lg":
                    pool.wait_ge(dve_done, dve_at("lg", b))
                    if b > 0:
                        pool.wait_ge(act_done, act_at("bc", b - 1, 3))
                    eye = ident.unsqueeze(1).to_broadcast([P, NT, P])
                    for slot in range(2):
                        w = wk[:, 4 + slot, :].unsqueeze(2).to_broadcast([P, NT, P])
                        e = idxf[:, slot, :].unsqueeze(2).to_broadcast([P, NT, P])
                        step(pool.tensor_tensor(diag_w[:, slot], eye, w, ALU.mult))
                        step(pool.tensor_tensor(diag_i[:, slot], eye, e, ALU.mult))

        @block.tensor
        def _(pe):
            def open_bank(key):
                if key in before:
                    pe.wait_ge(*read_by(before[key]))
                return G[jobs[key][0]]

            def full(key, last):
                last.then_inc(bank_full[jobs[key][0]], 1)

            def scores(b, h):
                g, j = h // NS, h % NS
                n = b * NH + h
                if n >= 3:
                    pe.wait_ge(act_done, act_at("head", (n - 3) // NH, (n - 3) % NH))
                pe.matmul(ST[n % 3][0:KL, :], lhsT=KB[:, b, g, j, :], rhs=qs[:, b % 2, g, :], start=True, stop=False)
                pe.matmul(ST[n % 3][0:KL, :], lhsT=sel_max[:, NG * j + g, :], rhs=mT[:, b % 2, :],
                          start=False, stop=True).then_inc(scores_full, 1)

            for stage, b, k in att:
                if stage == "setup":
                    pe.wait_ge(const_in, 16)
                    pe.wait_ge(dve_done, dve_at("setup", 0, 0, 25))
                    pe.wait_ge(vec_in, 16 * N_VEC)
                    t = open_bank(("cols",))
                    pe.transpose(t[:, 0:V_END], vec_rows[:], ident[0:V_END, 0:V_END])
                    for w in range(2):
                        for g in range(NG):
                            c = V_END + w * NG + g
                            last = pe.matmul(t[:, c:c + 1], lhsT=qk_arr[0:1, w, g], rhs=ones[0:1, 0:1], start=True, stop=True)
                    full(("cols",), last)
                    t = open_bank(("ctxT",))
                    for i in range(B):
                        last = pe.transpose(t[:, i * KL:(i + 1) * KL], ctx_tok[:, i, :], ident[0:KL, 0:KL])
                    full(("ctxT",), last)
                    pe.wait_ge(*read_by(("ctxT",)))
                    for g in range(NG):
                        t = open_bank(("kproj", g))
                        pe.matmul(t[:, 0:B * KL], lhsT=WkA[:, g], rhs=ctxT[:], start=True, stop=False)
                        full(("kproj", g), pe.matmul(t[:, 0:B * KL], lhsT=sel_mask[0:1], rhs=mask_row[0:1], start=False, stop=True))
                    t = open_bank(("vproj",))
                    for i in range(B):
                        last = pe.matmul(t[0:KL, i * D:(i + 1) * D], lhsT=ctxT[:, i * KL:(i + 1) * KL], rhs=Wv_sb[:], start=True, stop=True)
                    full(("vproj",), last)
                elif stage == "xT":
                    t = open_bank((stage, b, k))
                    pe.wait_ge(dve_done, dve_at("ln1", b))
                    for i in range(NT):
                        last = pe.transpose(t[:, i * P:(i + 1) * P], xn[:, 0, i, :], ident)
                    full((stage, b, k), last)
                elif stage == "q":
                    t = open_bank((stage, b, k))
                    pe.wait_ge(act_done, act_at("xT", b))
                    full((stage, b, k), pe.matmul(t[:], lhsT=WqA[:, k], rhs=xnT[:, b % 2, :], start=True, stop=True))
                elif stage == "S":
                    if b == 0:
                        pe.wait_ge(dve_done, dve_at("setup", 0))
                    pe.wait_ge(dve_done, dve_at("q", b, k))
                    for i in range(NT):
                        t = open_bank(("S", b, k, i))
                        full(("S", b, k, i), pe.matmul(t[:, 0:NS * KL], lhsT=qs[:, b % 2, k, i * P:(i + 1) * P],
                                                       rhs=KB[:, b, k], start=True, stop=True))
                elif stage == "mT":
                    t = open_bank((stage, b, k))
                    pe.wait_ge(dve_done, dve_at("S", b, NG - 1))
                    for i in range(NT):
                        last = pe.transpose(t[:, i * P:(i + 1) * P], m_tok[:, b % 2, i, :], ident)
                    full((stage, b, k), last)
                elif stage == "lead":
                    pe.wait_ge(act_done, act_at("mT", b))
                    scores(b, 0)
                    scores(b, 1)
                elif stage == "head":
                    g, j = k // NS, k % NS
                    if k + 2 < NH:
                        scores(b, k + 2)
                    n = b * NH + k
                    if b > 0 and k == 0:
                        pe.wait_ge(dve_done, dve_at("norm", b - 1))
                    pe.wait_ge(act_done, act_at("head", b, k))
                    pe.matmul(NUM[ROWS * j:ROWS * (j + 1), :], lhsT=VB[:, b, j, g, :], rhs=PT[:, n % 3, :],
                              start=(g == 0), stop=(g == NG - 1))
                    pe.matmul(DEN[ROWS * j:ROWS * (j + 1), :], lhsT=OB[:, g, :], rhs=PT[:, n % 3, :],
                              start=(g == 0), stop=(g == NG - 1)).then_inc(pv_done, 1)
                elif stage == "o":
                    t = open_bank((stage, b, k))
                    pe.wait_ge(dve_done, dve_at("norm", b))
                    for i in range(NT):
                        last = pe.matmul(t[:, i * P:(i + 1) * P], lhsT=oT[:, b % 2, i * P:(i + 1) * P], rhs=Wo_sb[:], start=True, stop=True)
                    full((stage, b, k), last)
                elif stage == "x2T":
                    t = open_bank((stage, b, k))
                    pe.wait_ge(dve_done, dve_at("o", b))
                    for i in range(NT):
                        last = pe.transpose(t[:, i * P:(i + 1) * P], xn[:, 1, i, :], ident)
                    full((stage, b, k), last)
                elif stage == "r1":
                    t = open_bank((stage, b, k))
                    if b == 0:
                        pe.wait_ge(ffnw_in, 16 * N_FFN)
                    pe.wait_ge(act_done, act_at("x2T", b))
                    full((stage, b, k), pe.matmul(t[0:D // 4, :], lhsT=w_r1_sb[:], rhs=xT[:, b, :], start=True, stop=True))
                elif stage == "lg":
                    t = open_bank((stage, b, k))
                    pe.wait_ge(act_done, act_at("r1", b))
                    for i in range(NT):
                        last = pe.matmul(t[:, i * E:(i + 1) * E], lhsT=hr[:, i * P:(i + 1) * P], rhs=w_r2_sb[:], start=True, stop=True)
                    full((stage, b, k), last)
                elif stage == "bc":
                    t = open_bank((stage, b, k))
                    pe.wait_ge(pool_done, pool_at("lg", b, 0, k + 1))
                    if k % 2 == 0:
                        last = pe.matmul(t[:], lhsT=ones[:], rhs=diag_w[:, k // 2], start=True, stop=True)
                    else:
                        last = pe.matmul(t[:], lhsT=ones_bf[:], rhs=diag_i[:, k // 2], start=True, stop=True)
                    full((stage, b, k), last)

            for stage, s, k in ffn:
                c, second = s % NB, s >= NB
                if stage == "w1":
                    if second:
                        pe.wait_ge(dve_done, dve_at("tail", c))
                    for j in range(NK + 1):
                        t = open_bank((stage, s, j))
                        for f in range(2 if second else 1):
                            lhsT = w1_sb[:, f, 2 * j:2 * j + 2, :] if j < NK else ws1_sb[:, f]
                            last = pe.matmul(t[:], lhsT=lhsT, rhs=(xT if f == 0 else vT)[:, c, :], start=(f == 0), stop=(f == second))
                        full((stage, s, j), last)
                elif stage == "w2":
                    n = 3 * s + k
                    if n == 0:
                        pe.wait_ge(dve_done, dve_at("norm", B - 1))
                    if n == 1:
                        pe.wait_ge(*read_by(last_g2))
                    if n >= 2:
                        so, ko = (n - 2) // 3, (n - 2) % 3
                        pe.wait_ge(dve_done, dve_at("w2", so, ko, 2))
                        pe.wait_ge(act_done, act_at("w2", so, ko, chunks(so) - 1))
                    if k == 0:
                        pe.wait_ge(act_done, act_at("w1", s))
                    else:
                        pe.wait_ge(dve_done, dve_at("w1", s, 0, NK * k))
                    for q in range(chunks(s)):
                        t = CT[n % 2][q]
                        o = D * (1, 2, 0)[q]
                        if k == 0:
                            last = pe.matmul(t[:], lhsT=ws2_sb[:, o:o + D], rhs=hid[:, NK, :], start=True, stop=True)
                        else:
                            pe.matmul(t[:], lhsT=b2_s[:, o:o + D], rhs=OH[:, k - 1, c, :], start=True, stop=False)
                            for j in range(NK):
                                last = pe.matmul(t[:], lhsT=w2_sb[:, j, o:o + D], rhs=mh[:, k - 1, j, :], start=False, stop=(j == NK - 1))
                        last.then_inc(stream_full, 1)
                elif stage == "tail":
                    pe.wait_ge(dve_done, dve_at("w2", s, 2))
                    t = open_bank(("h1", s))
                    full(("h1", s), pe.matmul(t[:], lhsT=wh1_sb[:], rhs=xnext, start=True, stop=True))
                    for a, name in enumerate(("f1a", "f1b")):
                        t = open_bank((name, s))
                        full((name, s), pe.matmul(t[:], lhsT=wf1_sb[:, a * D:(a + 1) * D], rhs=xnext, start=True, stop=True))
                    t = open_bank(("h2", s))
                    pe.wait_ge(act_done, act_at("tail", s, 0, 1))
                    full(("h2", s), pe.matmul(t[:], lhsT=wh2_sb[:], rhs=hh, start=True, stop=True))
                    t = open_bank(("f2", s))
                    for a in range(2):
                        pe.wait_ge(act_done, act_at("tail", s, 0, 2 + a))
                        last = pe.matmul(t[:], lhsT=wf2_sb[:, a, :], rhs=fh[:, a, :], start=(a == 0), stop=(a == 1))
                    full(("f2", s), last)
                elif stage == "fin":
                    t = open_bank((stage, s))
                    pe.wait_ge(dve_done, dve_at("tail", s))
                    for i in range(NT):
                        last = pe.transpose(t[:, i * P:(i + 1) * P], zf[:, i * P:(i + 1) * P], ident)
                    full((stage, s), last)

        @block.scalar
        def _(act):
            n = [0]

            def step(ins):
                ins.then_inc(act_done, 1)
                n[0] += 1
                if n[0] > 1:
                    act.wait_ge(act_done, n[0] - 1)

            def settle():
                act.wait_ge(act_done, n[0])

            def rstd(r):
                step(act.activation(rs[:, r, 0, :], rs[:, r, 3, :], ACT.Ln))
                settle()
                step(act.activation(rs[:, r, 1, :], rs[:, r, 0, :], ACT.Exp, scale=-0.5))

            for stage, b, k in att + ffn:
                if stage == "ln1":
                    act.wait_ge(dve_done, dve_at("ln1", b, 0, 9))
                    rstd(0)
                elif stage == "setup":
                    act.wait_ge(vec_in, 16 * N_VEC)
                    step(act.activation(shw[:, 1:2], shw[:, 0:1], ACT.Exp, scale=-1.0))
                    t = await_product(act, ("cols",))
                    step(act.activation(qk_cols[:], t[:, V_END:V_END + 2 * NG], ACT.Copy))
                    step(act.activation(cols[:], t[:, 0:V_END], ACT.Copy))
                    t = await_product(act, ("ctxT",))
                    step(act.activation(ctxT[:], t[:, 0:B * KL], ACT.Copy))
                    for g in range(NG):
                        t = await_product(act, ("kproj", g))
                        if g >= 2:
                            act.wait_ge(dve_done, dve_at("setup", 0, 0, 25 + NS * (g - 1)))
                        bias = qk_cols[:, NG + g:NG + g + 1]
                        step(act.activation(q_full[:, g % 2, 0:B * KL], t[:, 0:B * KL], ACT.Identity, bias=bias))
                        step(act.activation(q_hi[:, g % 2, 0:B * KL], t[:, 0:B * KL], ACT.Identity, bias=bias))
                    settle()
                    step(act.activation(shw[:, 2:3], shw[:, 1:2], ACT.Identity, bias=1.0))
                elif stage == "xT":
                    t = await_product(act, (stage, b, k))
                    step(act.activation(xnT[:, b % 2, :], t[:], ACT.Copy))
                elif stage == "q":
                    t = await_product(act, (stage, b, k))
                    if (b, k) < (0, 2):
                        act.wait_ge(dve_done, dve_at("setup", 0))
                    else:
                        act.wait_ge(dve_done, dve_at("q", b if k >= 2 else b - 1, (k - 2) % NG))
                    step(act.activation(q_full[:, k % 2, :], t[:], ACT.Identity, bias=qk_cols[:, k:k + 1]))
                    step(act.activation(q_hi[:, k % 2, :], t[:], ACT.Identity, bias=qk_cols[:, k:k + 1]))
                elif stage == "mT":
                    t = await_product(act, (stage, b, k))
                    if b >= 2:
                        act.wait_ge(scores_full, NH * (b - 1))
                    step(act.activation(mT[:, b % 2, :], t[:], ACT.Copy, scale=-1.0))
                elif stage == "head":
                    i = b * NH + k
                    act.wait_ge(scores_full, i + 1)
                    if i == 0:
                        act.wait_ge(pool_done, POOL_CLEARS)
                    if i >= 3:
                        act.wait_ge(pv_done, i - 2)
                    step(act.activation(PT[0:KL, i % 3, :], ST[i % 3][0:KL, :], ACT.Exp, scale=float(DH) ** -0.5))
                elif stage == "o":
                    act.wait_ge(dve_done, dve_at("o", b, 0, 10))
                    rstd(1)
                elif stage == "x2T":
                    t = await_product(act, (stage, b, k))
                    step(act.activation(xT[:, b, :], t[:], ACT.Copy))
                elif stage == "r1":
                    t = await_product(act, (stage, b, k))
                    if b > 0:
                        act.wait_ge(dve_done, dve_at("lg", b - 1, 0, 1))
                    step(act.activation(hr[:], t[0:D // 4, :], ACT.Gelu, bias=cols[0:D // 4, V_BR1:V_BR1 + 1]))
                elif stage == "lg":
                    act.wait_ge(dve_done, dve_at("lg", b, 0, 10))
                    step(act.activation(wk[:, 1, :], wk[:, 0, :], ACT.Exp))
                elif stage == "bc":
                    t = await_product(act, (stage, b, k))
                    step(act.activation((Wb if k % 2 == 0 else Ib)[:, k // 2, b, :], t[:], ACT.Copy))
                elif stage == "w1":
                    s = b
                    if s > 0:
                        act.wait_ge(dve_done, dve_at("w1", s - 1))
                        act.wait_ge(stream_full, chunk_no(s - 1, 1, 0))
                    for j in range(NK + 1):
                        t = await_product(act, (stage, s, j))
                        step(act.activation(hid[:, j, :], t[:], ACT.Gelu, bias=cols[:, V_B1 + j:V_B1 + j + 1]))
                elif stage == "tail":
                    s = b
                    t = await_product(act, ("h1", s))
                    step(act.activation(hh, t[:], ACT.Gelu, bias=cols[:, V_BH1:V_BH1 + 1]))
                    for a, name in enumerate(("f1a", "f1b")):
                        t = await_product(act, (name, s))
                        step(act.activation(fh[:, a, :], t[:], ACT.Gelu, bias=cols[:, V_BF1 + a:V_BF1 + a + 1]))
                    if s > 0:
                        act.wait_ge(dve_done, dve_at("tail", s - 1))
                    t = await_product(act, ("h2", s))
                    step(act.activation(th[:], t[:], ACT.Tanh, bias=half[:, 2:3], scale=0.5))
                    t = await_product(act, ("f2", s))
                    step(act.activation(rf, t[:], ACT.Identity, bias=cols[:, V_BF2:V_BF2 + 1]))
                elif stage == "w2":
                    s, i = b, 3 * b + k
                    u = i % 2
                    if i >= 2:
                        act.wait_ge(dve_done, dve_at("w2", (i - 2) // 3, (i - 2) % 3))
                    act.wait_ge(stream_full, chunk_no(s, k, 1) + 1)
                    step(act.activation(st_g[u], CT[u][1][:], ACT.Tanh, scale=0.5, **({"bias": half[:, 1:2]} if k == 0 else {})))
                    if s >= NB:
                        act.wait_ge(stream_full, chunk_no(s, k, 2) + 1)
                        step(act.activation(st_a[u], CT[u][2][:], ACT.Tanh, scale=0.5, **({"bias": half[:, 0:1]} if k == 0 else {})))
                    act.wait_ge(dve_done, dve_at("w2", s, k, 1))
                    step(act.activation(st_b[u], st_b[u], ACT.Exp))
                    settle()
                    step(act.activation(st_b[u], st_b[u], ACT.Ln, bias=1.0))
                if (stage, b, k) in act_at.before:
                    assert n[0] == act_at(stage, b, k), (stage, b, k, n[0], act_at(stage, b, k))

        @block.vector
        def _(dve):
            n = [0]

            def step(ins):
                ins.then_inc(dve_done, 1)
                n[0] += 1
                if n[0] > 1:
                    dve.wait_ge(dve_done, n[0] - 1)

            def settle():
                dve.wait_ge(dve_done, n[0])

            def norm_rows(r, b, src, stage, first):
                for t in range(NT):
                    step(dve.bn_stats(stats[:, r, t, :], src[:, t, :]))
                settle()
                for t in range(NT):
                    step(dve.bn_aggr(mv[:, r, t, :], stats[:, r, t, :]))
                settle()
                v, y, s1, y2 = rs[:, r, 3, :], rs[:, r, 1, :], rs[:, r, 2, :], rs[:, r, 4, :]
                step(dve.tensor_scalar(v, mv[:, r, :, 1], EPS, None, ALU.add))
                dve.wait_ge(act_done, act_at(stage, b))
                step(dve.tensor_tensor(s1, y, y, ALU.mult))
                settle()
                step(dve.tensor_tensor(s1, s1, v, ALU.mult))
                settle()
                step(dve.tensor_scalar(s1, s1, -0.5, 1.5, ALU.mult, ALU.add))
                settle()
                step(dve.tensor_tensor(y2, y, s1, ALU.mult))
                settle()
                for t in range(NT):
                    step(dve.tensor_scalar(xn[:, r, t, :], src[:, t, :], mv[:, r, t, 0:1], rs[:, r, 4, t:t + 1],
                                           ALU.subtract, ALU.mult))

            for stage, b, k in att + ffn:
                if stage == "ln1":
                    dve.wait_ge(x_in[b], 16)
                    if b > 0:
                        await_product(dve, ("xT", b - 1, 0))
                    norm_rows(0, b, x_tok[:, b], "ln1", True)
                elif stage == "setup":
                    dve.wait_ge(const_in, 16)
                    dve.wait_ge(attw_in, 16 * N_ATT)
                    dve.wait_ge(ctx_in, 16 * N_CTX)
                    dve.wait_ge(pool_done, POOL_CLEARS)
                    step(dve.memset(ones[:], 1.0))
                    step(dve.memset(ones_bf[:], 1.0))
                    for arr, w in ((WqA, Wq_sb), (WkA, Wk_sb)):
                        wv = w[:].rearrange("p (j g d) -> p g j d", j=NS, g=NG)
                        for part in range(3):
                            step(dve.tensor_copy(arr[:, :, :, part * DH:(part + 1) * DH], wv))
                    for w in range(2):
                        bv_ = qk_rows[0:1, w, :].rearrange("p (j g d) -> p g j d", j=NS, g=NG)
                        for part in range(3):
                            step(dve.tensor_copy(qk_arr[0:1, w, :, :, part * DH:(part + 1) * DH], bv_))
                    step(dve.memset(qk_arr[0:1, 0, :, :, ONE_ROW:ONE_ROW + 1], 1.0))
                    step(dve.memset(sel_mask[0:1, :, ONE_ROW:ONE_ROW + 1], 1.0))
                    step(dve.tensor_scalar(mask_row[:], mask_words[:].bitcast(U8), NEG, None, ALU.mult))
                    for g in range(NG):
                        step(dve.memset(OB[:, g, DH * g:DH * (g + 1)], 1.0))
                    step(dve.tensor_copy(sel_max[:], ident[:, 0:NH].unsqueeze(2).to_broadcast([P, NH, KL])))
                    for w in range(3):
                        step(dve.memset(tmp[:, w:w + 1], 0.0))
                    for g in range(NG):
                        dve.wait_ge(act_done, act_at("setup", 0, 0, 4 + 2 * (g + 1)))
                        for j in range(NS):
                            r = slice(ROWS * j, ROWS * (j + 1))
                            step(dve.scalar_tensor_tensor(
                                KB[r, :, g, j, :], q_hi[r, g % 2, 0:B * KL].bitcast(F32).rearrange("p (b k) -> p b k", b=B),
                                cst[r, C_NEG_K:C_NEG_K + 1], q_full[r, g % 2, 0:B * KL].rearrange("p (b k) -> p b k", b=B),
                                ALU.mult, ALU.add))
                    t = await_product(dve, ("vproj",))
                    for g in range(NG):
                        step(dve.tensor_tensor(
                            VB[0:KL, :, :, g, DH * g:DH * (g + 1)],
                            t[0:KL, :].rearrange("p (b j g d) -> p b j g d", b=B, j=NS, g=NG)[:, :, :, g, :],
                            bv_row[:].rearrange("p (j g d) -> p j g d", j=NS, g=NG)[:, :, g, :].unsqueeze(1).to_broadcast([KL, B, NS, DH]),
                            ALU.add))
                elif stage == "setup2":
                    dve.wait_ge(ffnw_in, 16 * N_FFN)
                    dve.wait_ge(act_done, act_at("setup", 0))
                    step(dve.tensor_scalar(half[:, 0:1], cols[:, V_BS2:V_BS2 + 1], 0.5, None, ALU.mult))
                    step(dve.tensor_scalar(half[:, 1:2], cols[:, V_BS2 + 2:V_BS2 + 3], 0.5, None, ALU.mult))
                    step(dve.tensor_scalar(half[:, 2:3], bh2[:], 0.5, None, ALU.mult))
                    step(dve.tensor_scalar(half[:, 3:4], cols[:, V_IW:V_IW + 1], 0.5, None, ALU.mult))
                    step(dve.reciprocal(half[:, 4:5], shw[:, 2:3]))
                    settle()
                    step(dve.tensor_scalar(half[:, 5:6], half[:, 4:5], -1.0, 1.0, ALU.mult, ALU.add))
                    step(dve.tensor_copy(wh2_sb[:], wh2_col[:].to_broadcast([P, P])))
                    step(dve.tensor_copy(b2_hi[:], b2_rep[:]))
                    settle()
                    step(dve.scalar_tensor_tensor(b2_rep[:], b2_hi[:], cst[0:3 * E, C_SPLIT1:C_SPLIT1 + 1], b2_rep[:], ALU.mult, ALU.add))
                    settle()
                    step(dve.tensor_copy(b2_hi[:], b2_rep[:]))
                    settle()
                    step(dve.scalar_tensor_tensor(b2_s[0:3 * E, :], b2_hi[:], cst[0:3 * E, C_SPLIT2:C_SPLIT2 + 1], b2_rep[:], ALU.mult, ALU.add))
                    for w in range(3):
                        step(dve.memset(logits[:, w, 0:1], 0.0))
                elif stage == "q":
                    if b >= 2 and k == 0:
                        dve.wait_ge(scores_full, NH * (b - 1))
                    dve.wait_ge(act_done, act_at("q", b, k))
                    step(dve.scalar_tensor_tensor(qs[:, b % 2, k, :], q_hi[:, k % 2, :].bitcast(F32), cst[:, C_NEG_Q:C_NEG_Q + 1],
                                                  q_full[:, k % 2, :], ALU.mult, ALU.add))
                elif stage == "S":
                    if b >= 2 and k == 0:
                        await_product(dve, ("mT", b - 2, 0))
                    for i in range(NT):
                        t = await_product(dve, ("S", b, k, i))
                        heads = m_tok[:, b % 2, i, 0:NH].rearrange("p (j g) -> p g j", g=NG)[:, k, :]
                        step(dve.tensor_reduce(heads, t[:, 0:NS * KL].rearrange("p (j k) -> p j k", j=NS), AX_X, ALU.max))
                elif stage == "norm":
                    dve.wait_ge(pv_done, NH * (b + 1))
                    step(dve.reciprocal(rden[:], DEN[:]))
                    settle()
                    step(dve.tensor_tensor(oT[:, b % 2, :], NUM[:], rden[:], ALU.mult))
                elif stage == "o":
                    t = await_product(dve, (stage, b, k))
                    dve.wait_ge(pool_done, pool_at("ln1", b))
                    step(dve.tensor_tensor(x_tok[:, b].rearrange("p t d -> p (t d)"), t[:], x_tok[:, b].rearrange("p t d -> p (t d)"), ALU.add))
                    settle()
                    if b > 0:
                        await_product(dve, ("x2T", b - 1, 0))
                    norm_rows(1, b, x_tok[:, b], "o", False)
                elif stage == "lg":
                    t = await_product(dve, (stage, b, k))
                    step(dve.tensor_tensor(logits[:], t[:, 0:NT * E].rearrange("p (t e) -> p t e", e=E),
                                           br2_row[:].unsqueeze(1).to_broadcast([P, NT, E]), ALU.add))
                    settle()
                    if b > 0:
                        dve.wait_ge(pool_done, pool_at("lg", b - 1))
                    for i in range(NT):
                        step(dve.max(mx[:, i, :], logits[:, i, :]))
                    settle()
                    for i in range(NT):
                        step(dve.max_index(mi[:, i, :], mx[:, i, :], logits[:, i, :]))
                    step(dve.tensor_tensor(wk[:, 0, :], mx[:, :, 1], mx[:, :, 0], ALU.subtract))
                    step(dve.tensor_copy(idxf[:], mi[:, :, 0:2].rearrange("p t s -> p s t")))
                    dve.wait_ge(act_done, act_at("lg", b))
                    step(dve.tensor_scalar(wk[:, 2, :], wk[:, 1, :], 1.0, None, ALU.add))
                    settle()
                    step(dve.reciprocal(wk[:, 3, :], wk[:, 2, :]))
                    settle()
                    step(dve.tensor_scalar(wk[:, 4, :], wk[:, 3, :], half[:, 5:6], None, ALU.mult))
                    settle()
                    step(dve.tensor_tensor(wk[:, 5, :], wk[:, 4, :], wk[:, 1, :], ALU.mult))
                elif stage == "bc" and k % 2:
                    dve.wait_ge(act_done, act_at("bc", b, k))
                    step(dve.tensor_scalar(OH[:, k // 2, b, :], Ib[:, k // 2, b, :], cst[:, C_ONEHOT:C_ONEHOT + 1], None, ALU.is_equal))
                elif stage == "w1":
                    s, c = b, b % NB
                    for slot in range(2):
                        for j in range(NK):
                            if slot == 0:
                                dve.wait_ge(act_done, act_at("w1", s, 0, j + 1))
                            step(dve.scalar_tensor_tensor(mh[:, slot, j, :], Ib[:, slot, c, :], cst[:, C_EXPERT + j:C_EXPERT + j + 1],
                                                          hid[:, j, :], ALU.is_equal, ALU.mult))
                elif stage == "w2":
                    s, c, i = b, b % NB, 3 * b + k
                    u, second = i % 2, b >= NB
                    gate, beta, alpha = st_g[u], st_b[u], st_a[u]
                    w = None if k == 0 else Wb[:, k - 1, c, :]
                    sw = half[:, 4:5]
                    bias = cols[:, V_BS2 + 1:V_BS2 + 2]
                    dve.wait_ge(stream_full, chunk_no(s, k, 0) + 1)
                    if k == 0:
                        step(dve.tensor_scalar(beta, CT[u][0][:], bias, SOFTPLUS_CAP, ALU.add, ALU.min))
                    else:
                        step(dve.tensor_scalar(beta, CT[u][0][:], SOFTPLUS_CAP, None, ALU.min))
                    dve.wait_ge(act_done, act_at("w2", s, k))
                    if k == 0:
                        step(dve.scalar_tensor_tensor(beta, CT[u][0][:], bias, beta, ALU.add, ALU.max))
                        step(dve.tensor_scalar(gate, gate, 1.0, sw, ALU.add, ALU.mult))
                        settle()
                        step(dve.tensor_tensor(acc_g, gate, beta, ALU.mult))
                        if not second:
                            step(dve.tensor_scalar(acc_a, beta, sw, None, ALU.mult))
                        else:
                            step(dve.scalar_tensor_tensor(acc_a, alpha, 1.0, gate, ALU.add, ALU.mult))
                        step(dve.tensor_scalar(nerr, xT[:, c, :], -1.0, cols[:, V_MU:V_MU + 1], ALU.mult, ALU.add))
                    else:
                        step(dve.tensor_tensor(beta, CT[u][0][:], beta, ALU.max))
                        step(dve.scalar_tensor_tensor(gate, gate, 1.0, w, ALU.add, ALU.mult))
                        settle()
                        if not second:
                            step(dve.tensor_tensor(gate, gate, beta, ALU.mult))
                            step(dve.tensor_tensor(tmp, beta, w, ALU.mult))
                            step(dve.tensor_tensor(acc_g, acc_g, gate, ALU.add))
                            step(dve.tensor_tensor(acc_a, acc_a, tmp, ALU.add))
                        else:
                            step(dve.scalar_tensor_tensor(alpha, alpha, 1.0, gate, ALU.add, ALU.mult))
                            step(dve.tensor_tensor(beta, gate, beta, ALU.mult))
                            step(dve.tensor_tensor(acc_a, acc_a, alpha, ALU.add))
                            step(dve.tensor_tensor(acc_g, acc_g, beta, ALU.add))
                    if k == 2 and not second:
                        step(dve.scalar_tensor_tensor(acc_g, acc_g, DT / 2, nerr, ALU.mult, ALU.mult))
                        step(dve.tensor_tensor(vT[:, c, :], acc_a, nerr, ALU.mult))
                        step(dve.tensor_tensor(xnext, acc_g, xT[:, c, :], ALU.add))
                    elif k == 2:
                        step(dve.scalar_tensor_tensor(acc_a, acc_a, 0.25, vT[:, c, :], ALU.mult, ALU.mult))
                        settle()
                        step(dve.scalar_tensor_tensor(acc_g, acc_g, 0.5, nerr, ALU.mult, ALU.mult))
                        settle()
                        step(dve.tensor_tensor(acc_g, acc_g, acc_a, ALU.add))
                        settle()
                        step(dve.scalar_tensor_tensor(xnext, acc_g, DT, xT[:, c, :], ALU.mult, ALU.add))
                elif stage == "tail":
                    s, c = b, b % NB
                    dve.wait_ge(act_done, act_at("tail", s))
                    step(dve.scalar_tensor_tensor(tmp, th[:], 1.0, rf, ALU.add, ALU.mult))
                    settle()
                    step(dve.scalar_tensor_tensor(xT[:, c, :] if s < NB else zf, tmp, half[:, 3:4], xT[:, c, :], ALU.mult, ALU.add))
                elif stage == "fin":
                    c = b % NB
                    t = await_product(dve, (stage, b))
                    step(dve.tensor_tensor(x_tok[:, c].rearrange("p t d -> p (t d)"), t[:], x_tok[:, c].rearrange("p t d -> p (t d)"), ALU.add))
                if (stage, b, k) in dve_at.before:
                    assert n[0] == dve_at(stage, b, k), (stage, b, k, n[0], dve_at(stage, b, k))


INPUTS = ["x", "ctx_1024", "mask_BxS2_bf0", "L0_xattn_Wq", "L0_xattn_bq", "L0_xattn_Wk", "L0_xattn_bk", "L0_xattn_Wv",
          "L0_xattn_bv", "L0_xattn_Wo", "L0_xattn_bo", "L0_ffn_w_r1", "L0_ffn_b_r1", "L0_ffn_w_r2", "L0_ffn_b_r2",
          "L0_ffn_w_h1", "L0_ffn_b_h1", "L0_ffn_w_h2", "L0_ffn_b_h2", "L0_ffn_expert_w1", "L0_ffn_expert_b1",
          "L0_ffn_expert_w2", "L0_ffn_expert_b2", "L0_ffn_w_s1", "L0_ffn_b_s1", "L0_ffn_w_s2", "L0_ffn_b_s2",
          "L0_ffn_shared_weight", "L0_ffn_w_f1", "L0_ffn_b_f1", "L0_ffn_w_f2", "L0_ffn_b_f2",
          "L0_ffn_integration_weight", "L0_ffn_mu"]


def kernel(**inputs):
    import concourse.bacc as bacc
    from concourse.bass_utils import run_bass_kernel_spmd

    nc = bacc.Bacc("TRN2", target_bir_lowering=False, num_devices=1)
    arrays, args = {}, []
    for name in INPUTS + ["shape_constants"]:
        a = np.ascontiguousarray(shape_constants() if name == "shape_constants" else inputs[name])
        if a.dtype == np.bool_:
            a = a.reshape(-1).view(np.uint32)
        if a.ndim == 0:
            a = a.reshape(1)
        arrays[f"in_{name}_dram"] = a
        args.append(nc.dram_tensor(f"in_{name}_dram", a.shape, mybir.dt.from_np(a.dtype), kind="ExternalInput").ap())
    args.append(nc.dram_tensor("out_0_dram", (B, S, D), F32, kind="ExternalOutput").ap())
    xattn_moe_kernel(nc, *args)
    r = run_bass_kernel_spmd(nc, [arrays], core_ids=[0])
    return r.results[0]["out_0_dram"]
```

```python
from contextlib import ExitStack

import numpy as np

import concourse.bass as bass
from concourse import mybir

F32 = mybir.dt.float32
F32R = mybir.dt.float32r
BF16 = mybir.dt.bfloat16
U32 = mybir.dt.uint32
U8 = mybir.dt.uint8
ACT = mybir.ActivationFunctionType
ALU = mybir.AluOpType
AX_X = mybir.AxisListType.X

P = 128
B, S, D = 4, 512, 128
KL = 77
NH, DH = 16, 8
NG = 4
NS = 4
ROWS = 32
ONE_ROW = 3 * DH
NT = S // P
E, H = 8, 64
NK = E * H // P
NB = B
NEG = -float(2 ** 100)
EPS = 1e-5
DT = 0.1
SOFTPLUS_CAP = 40.0
EXP_LN, GELU_TANH = 6, 10
G_BANKS = 3
MASK_ROUNDED = (3, 5, 7, 8)
POOL_CLEARS = 8

C_IDENT, C_EXPERT, C_ONEHOT, C_LO_Q, C_LO_K, C_SPLIT1, C_SPLIT2, C_END = 0, 128, 132, 133, 134, 135, 136, 137

V_B1, V_BS1, V_BF1, V_BF2, V_MU, V_IW, V_BH1, V_BR1, V_BS2, V_END = 0, 4, 5, 7, 8, 9, 10, 11, 12, 16


def shape_constants():
    c = np.zeros((P, C_END), np.float32)
    p = np.arange(P)
    c[:, C_IDENT:C_IDENT + P] = np.eye(P)
    for k in range(NK):
        c[:, C_EXPERT + k] = 2 * k + p // H
    c[:, C_ONEHOT] = np.where(p < 3 * E, p % E, -1)
    part = p % ROWS // DH
    c[:, C_LO_Q] = np.where(part == 2, 1, 0)
    c[:, C_LO_K] = np.where(part == 1, 1, 0)
    c[:, C_SPLIT1] = np.where(p >= E, -1, 0)
    c[:, C_SPLIT2] = np.where(p >= 2 * E, -1, 0)
    return c


PLACES = {
    "ln1": ((None, None, -36.03, None), 0), "ln1r": ((None, -33.76, None, None), 0),
    "ln1x": ((None, None, -35.86, None), 0), "xbo": ((None, None, None, -31.93), 0),
    "xT": ((-30.54, -29.86, None, None), 0), "q": ((-29.33, -28.18, -28, None), 3.55),
    "S": ((-16, None, -15.6, None), 0.75), "mT": ((-3.94, -1.76, None, None), 0),
    "sc": ((-1.92, None, None, None), 1), "exp": ((None, 0, None, None), 1), "pv": ((1.43, None, None, None), 1),
    "ev": ((None, 15.89, 16.72, None), 0), "norm": ((None, None, 17.17, None), 0),
    "o": ((19.63, None, 20.32, None), 0), "o2r": ((None, 21.56, None, None), 0), "o2x": ((None, None, 22.2, None), 0),
    "x2T": ((23.33, 24.2, None, None), 0), "r1": ((25.23, 26.03, None, None), 0),
    "lg": ((27.27, None, 27.65, None), 0), "lge": ((None, 29.48, None, None), 0),
    "lgx": ((None, None, 30.25, 33.38), 0), "bc": ((32.89, 33.49, 34.28, None), 1.47),
}
SETUP = {
    "selmax": ((None, None, -16.06, None), 0), "clear": ((None, None, -60, None), 0),
    "vecs": ((-4.61, -3.97, None, None), 0), "prep": ((None, None, -36.8, None), 0),
    "cols": ((-36, -33.81, None, None), 0), "ctxT": ((-41.13, -34.9, None, None), 0),
    "kproj": ((-34.8, -31.21, -31.74, None), 0.01), "vproj": ((-17.39, None, -20.0, None), 0),
    "setup2": ((None, 2.06, 5.19, None), 0), "w2split": ((None, None, None, 0.14), 0),
}
FIRST_FFN = {
    ("round", 0, 0): (None, None, 71.94, None), ("low", 0, 0): (None, None, None, 74.68),
    ("low", 0, 2): (None, None, None, 75), ("w1", 0, 0): (64.6, 65.09, None, None),
    ("mask", 0, 0): (None, None, 73.5, None), ("mask", 0, 1): (None, None, 79, None),
    ("w2", 0, 0): (76.08, None, None, None),
}
STEP = 24
FFN_PLACES = {
    ("w1", 0): (-7, -6, None, None), ("mask", 0): (None, None, -6.14, None), ("mask", 1): (None, None, 4, None),
    ("round", 0): (None, None, -4, None), ("low", 0): (None, None, None, -5), ("low", 2): (None, None, None, -6.22),
    ("low", 1): (None, None, None, 4.81), ("add", 1): (None, None, None, 11), ("w2", 0): (0.09, None, None, None),
    ("w2", 1): (2, None, None, None), ("w2", 2): (17.05, None, None, None), ("cap", 0): (None, None, 1, None),
    ("cap", 1): (None, None, 3, None), ("cap", 2): (None, None, 23.33, None), ("sp", 0): (None, 1.5, None, None),
    ("sp", 1): (None, 3.22, None, None), ("sp", 2): (None, 20.79, None, None), ("gt", 0): (None, 0.25, None, None),
    ("gt", 1): (None, 11.13, None, None), ("gt", 2): (None, 23, None, None), ("mix", 0): (None, None, 7, None),
    ("mix", 1): (None, None, 9.79, None), ("mix", 2): (None, None, 24.48, None),
    ("tail", 0): (31.96, 32.46, 34.96, None), ("fin", 0): (49.58, None, 51.97, None),
}
ENGINES = ("pe", "act", "dve", "pool")
STAGE_COUNT = {"q": NG, "S": NG * NT, "sc": NH, "exp": NH, "pv": NH, "bc": 4, "kproj": NG}


def engine_order(engine):
    e = ENGINES.index(engine)
    placed = []
    for table, batches in ((PLACES, B), (SETUP, 1)):
        for stage, (at, pitch) in table.items():
            if at[e] is not None:
                placed += [(at[e] + NH * b + pitch * k, (stage, b, k)) for b in range(batches) for k in range(STAGE_COUNT.get(stage, 1))]
    placed += [(at[e], key) for key, at in FIRST_FFN.items() if at[e] is not None]
    placed.sort(key=lambda item: item[0])
    order = [key for at, key in placed]
    placed = [(STEP * s + at[e], (stage, s, k)) for (stage, k), at in FFN_PLACES.items() if at[e] is not None for s in range(2 * NB)]
    placed = [(at, key) for at, key in placed if key not in order and (key[0] != "fin" or key[1] >= NB)]
    placed.sort(key=lambda item: item[0])
    return order + [key for at, key in placed]


def act_steps(stage, i, k):
    if stage == "gt":
        return 1 if i < NB else 2
    return {"ln1r": 2, "cols": 3, "vecs": 2, "clear": 0, "ctxT": 1, "kproj": 1, "setup2": 1, "xT": 1, "q": 1, "mT": 1, "exp": 1, "ev": 1, "o2r": 2,
            "x2T": 1, "r1": 1, "lge": 1, "bc": 1, "w1": NK + 1, "tail": 5, "sp": 2}.get(stage, 0)


def dve_steps(stage, i, k):
    if stage == "mix":
        return (4, 3, 8)[k] if i < NB else (5, 4, 10)[k]
    if stage == "bc":
        return k % 2
    return {"ln1": 9, "ln1x": 8, "clear": 14, "prep": 10, "selmax": 1, "kproj": NS, "vproj": NG, "setup2": 11, "q": 1, "S": 1, "ev": 1, "norm": 2,
            "o": 10, "o2x": 8, "lg": 11, "lgx": 4, "round": 1, "mask": 2 * NK, "cap": 1, "tail": 2, "fin": 1}.get(stage, 0)


def pool_steps(stage, i, k):
    return {"xbo": 1, "lgx": 4, "w2split": 2, "low": NK if k < 2 else 1, "add": 2}.get(stage, 0)


def max_read(s, k):
    return 6 if (s, k) == (2 * NB - 1, 2) else 1


class Done:

    def __init__(self, order, steps, total=0):
        self.before, self.steps = {}, steps
        for stage in order:
            self.before[stage] = total
            total += steps(*stage)

    def __call__(self, stage, b, k=0, i=None):
        return self.before[(stage, b, k)] + (self.steps(stage, b, k) if i is None else i)


def bank_jobs(order):
    jobs, used, turn = {}, [0] * G_BANKS, 0
    for stage, b, k in order:
        if stage == "w1":
            keys = [("w1", b, j) for j in range(NK + 1)]
        elif stage == "tail":
            keys = [(j, b) for j in ("h1", "f1a", "f1b", "h2", "f2")]
        elif stage in ("cols", "vecs", "ctxT", "kproj", "vproj", "xT", "q", "mT", "S", "o", "x2T", "r1", "lg", "bc", "fin"):
            keys = [(stage, b, k)]
        else:
            keys = []
        for key in keys:
            bank = turn % (2 if stage in ("w1", "tail", "fin") and b >= NB - 1 else G_BANKS)
            jobs[key] = (bank, used[bank])
            used[bank] += 1
            turn = bank + 1
    return jobs


def xattn_moe_kernel(nc, x, ctx, mask, Wq, bq, Wk, bk, Wv, bv, Wo, bo, w_r1, b_r1, w_r2, b_r2, w_h1, b_h1,
                     w_h2, b_h2, e_w1, e_b1, e_w2, e_b2, w_s1, b_s1, w_s2, b_s2, shared_weight, w_f1, b_f1,
                     w_f2, b_f2, iw, mu, consts, out):
    order = {e: engine_order(e) for e in ENGINES}
    jobs = bank_jobs(order["pe"])
    act_at, dve_at = Done(order["act"], act_steps), Done(order["dve"], dve_steps)
    pool_at = Done(order["pool"], pool_steps, POOL_CLEARS + 1)
    with ExitStack() as stack:
        def sb(name, shape, dt=F32):
            return stack.enter_context(nc.sbuf_tensor(name, shape, dt))

        def sem(name):
            return stack.enter_context(nc.semaphore(name))

        cst = sb("cst", [P, C_END])
        ident = cst[:, C_IDENT:C_IDENT + P]
        ident_bf = sb("ident_bf", [P, P], BF16)
        ones = sb("ones", [P, P])
        ones_bf = sb("ones_bf", [P, P], BF16)
        x_tok = sb("x_tok", [P, B, NT, D])
        bo_row = sb("bo_row", [P, D])
        stats = sb("stats", [P, 2, NT, 6])
        mv = sb("mv", [P, 2, NT, 2])
        rs = sb("rs", [P, 2, 5, NT])
        xn = sb("xn", [P, 2, NT, D])
        xnT = sb("xnT", [P, 2, S])
        taken = sb("taken", [P, 2, S], F32R)
        qs = sb("qs", [P, 2, NG, S], F32R)
        KB = sb("KB", [P, B, NG, NS, KL], F32R)
        VB = sb("VB", [P, B, NS, NG, ROWS])
        OB = sb("OB", [P, NG, ROWS])
        ctx_tok = sb("ctx_tok", [KL, B, D])
        ctxT = sb("ctxT", [P, B * KL])
        bv_row = sb("bv_row", [KL, D])
        mask_words = sb("mask_words", [1, B * KL // 4], U32)
        mask_row = sb("mask_row", [1, B * KL])
        sel_mask = sb("sel_mask", [1, NS, ROWS])
        qk_rows = sb("qk_rows", [2 * NG, NS, DH])
        qk_arr = sb("qk_arr", [2 * NG, NS, ROWS])
        qk_cols = sb("qk_cols", [P, 2, NG])
        qk_taken = sb("qk_taken", [P, 2, NG])
        Wq_sb, Wk_sb, Wv_sb, Wo_sb = (sb(n, [P, D]) for n in ("Wq_sb", "Wk_sb", "Wv_sb", "Wo_sb"))
        WqA = sb("WqA", [P, NG, NS, ROWS])
        WkA = sb("WkA", [P, NG, NS, ROWS])
        sel_max = sb("sel_max", [P, NH, KL], F32R)
        m_tok = sb("m_tok", [P, 2, NT, P])
        mT = sb("mT", [P, 2, S], F32R)
        PT = sb("PT", [P, 3, S])
        rden = sb("rden", [P, S])
        oT = sb("oT", [P, 2, S])
        w_r1_sb = sb("w_r1_sb", [P, D // 4])
        w_r2_sb = sb("w_r2_sb", [D // 4, E])
        br2_row = sb("br2_row", [P, E])
        hr = sb("hr", [D // 4, S])
        logits = sb("logits", [P, NT, E])
        mx = sb("mx", [P, NT, 8])
        mi = sb("mi", [P, NT, 8], U32)
        wk = sb("wk", [P, 6, NT])
        idxf = sb("idxf", [P, 2, NT])
        diag_w = sb("diag_w", [P, 2, NT, P])
        diag_i = sb("diag_i", [P, 2, NT, P], BF16)
        vec_rows = sb("vec_rows", [V_END, P])
        cols = sb("cols", [P, V_END])
        half = sb("half", [P, 6])
        bh2 = sb("bh2", [P, 1])
        shw = sb("shw", [P, 3])
        w1_sb = sb("w1_sb", [P, 2, E, H])
        ws1_sb = sb("ws1_sb", [P, 2, 2, H])
        w2_hi = sb("w2_hi", [P, NK + 1, 3 * D], F32R)
        w2_lo = sb("w2_lo", [P, NK + 1, 3 * D], F32R)
        b2_rep = sb("b2_rep", [3 * E, 3 * D])
        b2_hi = sb("b2_hi", [3 * E, 3 * D], BF16)
        b2_s = sb("b2_s", [P, 3 * D], BF16)
        wf1_sb = sb("wf1_sb", [P, 2 * D])
        wf2_sb = sb("wf2_sb", [P, 2, D])
        wh1_sb = sb("wh1_sb", [P, P])
        wh2_col = sb("wh2_col", [P, 1])
        wh2_sb = sb("wh2_sb", [P, P])
        xT = sb("xT", [P, NB, S])
        Wb = sb("Wb", [P, 2, NB, S])
        Ib = sb("Ib", [P, 2, NB, S], BF16)
        OH = sb("OH", [P, 2, NB, S], BF16)
        err_tmp = sb("err_tmp", [P, 2, S])
        hid = sb("hid", [P, NK + 1, S])
        w2_in = hid[:].rearrange("p j s -> p (j s)")[:, 0:(NK + 1) * 3 * D].rearrange("p (j o) -> p j o", o=3 * D)
        masked = sb("masked", [P, NK, S])
        shared_hi = sb("shared_hi", [P, S], F32R)
        mask_hi = qs[:].rearrange("p u g s -> p (u g) s")
        mask_lo = KB[:].rearrange("p b g j k -> p (b g j k)")[:, 0:2 * NK * S].rearrange("p (u s) -> p u s", s=S)
        shared_lo = taken[:, 0, :]
        vT = VB[:].rearrange("p b j g r -> p b (j g r)")
        flat = [t[:].rearrange("p u t d -> p u (t d)") for t in (xn, m_tok)]
        st_b, st_g = [flat[0][:, 0, :], xnT[:, 1, :]], [flat[1][:, u, :] for u in range(2)]
        st_a = [t[:].rearrange("p g j r -> p (g j r)") for t in (WqA, WkA)]
        acc_g, acc_a = oT[:, 0, :], xnT[:, 0, :]
        nerr, tmp = err_tmp[:, 0, :], err_tmp[:, 1, :]
        xnext, hh = oT[:, 1, :], flat[0][:, 1, :]
        fh = diag_w[:].rearrange("p u t d -> p u (t d)")
        th, rf, zf = rden, PT[:, 0, :], PT[:, 1, :]

        bank = [stack.enter_context(nc.psum_tensor(f"bank{i}", [P, 512], F32)) for i in range(8)]
        G = bank[0:3]
        ST = bank[3:6]
        NUM, DEN = bank[6], bank[7]
        CT = [[bank[3], bank[4], bank[5]], [bank[6], bank[7], bank[2]]]

        const_in, vec_in, attw_in, ctx_in, proj_in, ffnw_in = (
            sem(n) for n in ("const_in", "vec_in", "attw_in", "ctx_in", "proj_in", "ffnw_in"))
        x_in = [sem(f"x_in{b}") for b in range(B)]
        out_done = sem("out_done")
        act_done, dve_done, pool_done = sem("act_done"), sem("dve_done"), sem("pool_done")
        bank_full = [sem(f"bank_full{i}") for i in range(G_BANKS)]
        scores_full, pv_done, stream_full = sem("scores_full"), sem("pv_done"), sem("stream_full")

        block = stack.enter_context(nc.Block())
        N_VEC, N_ATT, N_CTX, N_PROJ, N_FFN = 11, 5, 1, 5, 18

        def chunks(s):
            return 2 if s < NB else 3

        def chunk_no(s, k, q):
            return sum(3 * chunks(i) for i in range(s)) + k * chunks(s) + q

        def read_by(key):
            kind, b, *k = key
            if kind in ("cols", "vecs", "ctxT", "xT", "mT", "x2T", "r1", "bc"):
                return act_done, act_at(*key)
            if kind in ("kproj", "vproj", "q", "S", "fin"):
                return dve_done, dve_at(*key)
            if kind in ("o", "lg"):
                return dve_done, dve_at(kind, b, 0, 1)
            if kind == "w1":
                return act_done, act_at("w1", b, 0, k[0] + 1)
            return act_done, act_at("tail", b, 0, ("h1", "f1a", "f1b", "h2", "f2").index(kind) + 1)

        before = {}
        for key, (i, n) in jobs.items():
            if n:
                before[key] = next(o for o, at in jobs.items() if at == (i, n - 1))
        last_g2 = next(o for o, at in jobs.items() if at == (2, max(n for i, n in jobs.values() if i == 2)))
        splits = [("kproj", 0, g) for g in range(NG)] + [("q", b, g) for b in range(B) for g in range(NG)]

        def await_product(eng, key):
            i, n = jobs[key]
            eng.wait_ge(bank_full[i], n + 1)
            return G[i]

        @block.sync
        def _(sp):
            def load(dst, src, signal):
                with nc.allow_non_contiguous_dma(reason="small parameters"):
                    sp.dma_start(dst, src).then_inc(signal, 16)

            def row(v):
                return v.rearrange("(a n) -> a n", a=1)

            load(x_tok[:, 0], x[0].rearrange("(t p) d -> p t d", p=P), x_in[0])
            load(cst[:], consts, const_in)
            load(ctx_tok[:], ctx.rearrange("b k d -> k b d"), ctx_in)
            load(Wk_sb[:], Wk, attw_in)
            load(Wq_sb[:], Wq, attw_in)
            load(qk_rows[0:NG], bq.rearrange("(j g d) -> g j d", j=NS, g=NG), attw_in)
            load(qk_rows[NG:2 * NG], bk.rearrange("(j g d) -> g j d", j=NS, g=NG), attw_in)
            load(mask_words[:], row(mask), attw_in)
            load(Wv_sb[:], Wv, proj_in)
            load(bv_row[:], bv.partition_broadcast(KL), proj_in)
            load(Wo_sb[:], Wo, proj_in)
            load(bo_row[:], bo.partition_broadcast(P), proj_in)
            load(br2_row[:], b_r2.partition_broadcast(P), proj_in)
            load(x_tok[:, 1], x[1].rearrange("(t p) d -> p t d", p=P), x_in[1])
            sp.wait_ge(pool_done, 4)
            load(vec_rows[V_B1:V_B1 + 4, :], e_b1.rearrange("(k e) h -> k (e h)", e=2), vec_in)
            load(vec_rows[V_BS1:V_BS1 + 1, 0:H], row(b_s1), vec_in)
            load(vec_rows[V_BS1:V_BS1 + 1, H:P], row(b_s1), vec_in)
            load(vec_rows[V_BF1:V_BF1 + 2, :], b_f1.rearrange("(a n) -> a n", a=2), vec_in)
            load(vec_rows[V_BF2:V_BF2 + 1, :], row(b_f2), vec_in)
            load(vec_rows[V_MU:V_MU + 1, :], row(mu), vec_in)
            load(vec_rows[V_IW:V_IW + 1, :], row(iw), vec_in)
            load(vec_rows[V_BH1:V_BH1 + 1, 0:D // 4], row(b_h1), vec_in)
            load(vec_rows[V_BR1:V_BR1 + 1, 0:D // 4], row(b_r1), vec_in)
            load(vec_rows[V_BS2:V_BS2 + 3, :], b_s2.rearrange("(a n) -> a n", a=3), vec_in)
            load(shw[:, 0:1], shared_weight.partition_broadcast(P), vec_in)
            for b in range(2, B):
                load(x_tok[:, b], x[b].rearrange("(t p) d -> p t d", p=P), x_in[b])
            load(w_r1_sb[:], w_r1, ffnw_in)
            load(w_r2_sb[:], w_r2, ffnw_in)
            for f in range(2):
                load(w1_sb[:, f], e_w1.rearrange("e (f c) h -> f c e h", f=2)[f], ffnw_in)
                for r in range(2):
                    load(ws1_sb[:, f, r], w_s1.rearrange("(f c) h -> f c h", f=2)[f], ffnw_in)
            load(w2_in[:, 0:NK], e_w2.rearrange("(k e) h o -> (e h) k o", e=2), ffnw_in)
            load(w2_in[0:H, NK], w_s2, ffnw_in)
            for r in range(3):
                load(b2_rep[r * E:(r + 1) * E], e_b2, ffnw_in)
            load(wf1_sb[:], w_f1, ffnw_in)
            load(wf2_sb[:], w_f2.rearrange("(a c) n -> c a n", a=2), ffnw_in)
            load(wh1_sb[:, 0:D // 4], w_h1, ffnw_in)
            load(wh2_col[0:D // 4], w_h2, ffnw_in)
            load(bh2[:], b_h2.partition_broadcast(P), ffnw_in)
            for b in range(B):
                sp.wait_ge(dve_done, dve_at("fin", NB + b))
                sp.dma_start(out[b].rearrange("(t p) d -> p t d", p=P), x_tok[:, b]).then_inc(out_done, 16)
            sp.wait_ge(out_done, 16 * B)

        @block.gpsimd
        def _(pool):
            n = [0]

            def step(ins):
                ins.then_inc(pool_done, 1)
                n[0] += 1
                if n[0] > 1:
                    pool.wait_ge(pool_done, n[0] - 1)

            def clears():
                tiles = [vec_rows[:], w2_in[:, NK], wh1_sb[:], wh2_col[:], VB[:], m_tok[:], PT[:], b2_s[:]]
                assert len(tiles) == POOL_CLEARS
                for t in tiles:
                    step(pool.memset(t, 0.0))
                pool.wait_ge(const_in, 16)
                step(pool.tensor_copy(ident_bf[:], ident))

            clears()
            for stage, b, k in order["pool"]:
                if stage == "w2split":
                    pool.wait_ge(ffnw_in, 16 * N_FFN)
                    step(pool.tensor_copy(w2_hi[:], w2_in))
                    pool.wait_ge(pool_done, n[0])
                    step(pool.tensor_tensor(w2_lo[:], w2_in, w2_hi[:].bitcast(F32), ALU.subtract))
                elif stage == "low" and k < 2:
                    if b == 0:
                        pool.wait_ge(scores_full, B * NH)
                    else:
                        pool.wait_ge(stream_full, chunk_no(b - 1, k + 1, chunks(b - 1)))
                    for j in range(NK):
                        pool.wait_ge(dve_done, dve_at("mask", b, k, MASK_ROUNDED[j]))
                        step(pool.tensor_tensor(mask_lo[:, k * NK + j, :], masked[:, j, :], mask_hi[:, k * NK + j, :].bitcast(F32), ALU.subtract))
                elif stage == "low":
                    pool.wait_ge(dve_done, dve_at("round", b))
                    if b > 0:
                        pool.wait_ge(stream_full, chunk_no(b - 1, 1, 0))
                    step(pool.tensor_tensor(shared_lo, hid[:, NK, :], shared_hi[:].bitcast(F32), ALU.subtract))
                elif stage == "add":
                    u = (3 * b + k) % 2
                    pool.wait_ge(dve_done, dve_at("mix", b, k))
                    step(pool.tensor_tensor(acc_a, acc_a, st_b[u] if b < NB else st_a[u], ALU.add))
                    step(pool.tensor_tensor(acc_g, acc_g, st_g[u] if b < NB else st_b[u], ALU.add))
                elif stage == "xbo":
                    pool.wait_ge(proj_in, 16 * N_PROJ)
                    pool.wait_ge(dve_done, dve_at("ln1x", b))
                    step(pool.tensor_tensor(x_tok[:, b], x_tok[:, b], bo_row[:].unsqueeze(1).to_broadcast([P, NT, D]), ALU.add))
                elif stage == "lgx":
                    pool.wait_ge(dve_done, dve_at("lgx", b))
                    if b > 0:
                        pool.wait_ge(act_done, act_at("bc", b - 1, 3))
                    eye = ident.unsqueeze(1).to_broadcast([P, NT, P])
                    for slot in range(2):
                        w = wk[:, 4 + slot, :].unsqueeze(2).to_broadcast([P, NT, P])
                        e = idxf[:, slot, :].unsqueeze(2).to_broadcast([P, NT, P])
                        step(pool.tensor_tensor(diag_w[:, slot], eye, w, ALU.mult))
                        step(pool.tensor_tensor(diag_i[:, slot], eye, e, ALU.mult))

        @block.tensor
        def _(pe):
            def open_bank(key):
                if key in before:
                    pe.wait_ge(*read_by(before[key]))
                return G[jobs[key][0]]

            def full(key, last):
                last.then_inc(bank_full[jobs[key][0]], 1)

            def ffn_stage(stage, s, k):
                c, second = s % NB, s >= NB
                if stage == "w1":
                    if second:
                        pe.wait_ge(dve_done, dve_at("tail", c))
                    for j in range(NK + 1):
                        t = open_bank((stage, s, j))
                        for f in range(2 if second else 1):
                            lhsT = w1_sb[:, f, 2 * j:2 * j + 2, :] if j < NK else ws1_sb[:, f]
                            last = pe.matmul(t[:], lhsT=lhsT, rhs=(xT if f == 0 else vT)[:, c, :], start=(f == 0), stop=(f == second))
                        full((stage, s, j), last)
                elif stage == "w2":
                    n = 3 * s + k
                    if n == 0:
                        pe.wait_ge(act_done, act_at("exp", B - 1, NH - 1))
                    if n == 1:
                        pe.wait_ge(act_done, act_at("ev", B - 1))
                        pe.wait_ge(dve_done, dve_at("ev", B - 1))
                    if n == 3 * NB + 1:
                        pe.wait_ge(*read_by(last_g2))
                    if n >= 2:
                        so, ko = (n - 2) // 3, (n - 2) % 3
                        pe.wait_ge(dve_done, dve_at("mix", so, ko, max_read(so, ko)))
                        pe.wait_ge(act_done, act_at("gt", so, ko))
                    if k == 0:
                        pe.wait_ge(pool_done, pool_at("low", s, 2))
                    else:
                        pe.wait_ge(dve_done, dve_at("mask", s, k - 1))
                    for q in range(chunks(s)):
                        t = CT[n % 2][q]
                        o = D * (1, 2, 0)[q]
                        if k > 0:
                            pe.matmul(t[:], lhsT=b2_s[:, o:o + D], rhs=OH[:, k - 1, c, :], start=True, stop=False)
                            units = [(j, mask_hi[:, (k - 1) * NK + j, :], mask_lo[:, (k - 1) * NK + j, :]) for j in range(NK)]
                        else:
                            units = [(NK, shared_hi[:], shared_lo)]
                        for j, hi, lo in units:
                            pe.matmul(t[:], lhsT=w2_hi[:, j, o:o + D], rhs=hi, start=(k == 0), stop=False)
                            pe.matmul(t[:], lhsT=w2_lo[:, j, o:o + D], rhs=hi, start=False, stop=False)
                        if k > 0 and q == 0:
                            pe.wait_ge(pool_done, pool_at("low", s, k - 1))
                        for j, hi, lo in units:
                            last = pe.matmul(t[:], lhsT=w2_hi[:, j, o:o + D], rhs=lo, start=False, stop=(j == units[-1][0]))
                        last.then_inc(stream_full, 1)
                elif stage == "tail":
                    pe.wait_ge(dve_done, dve_at("mix", s, 2))
                    t = open_bank(("h1", s))
                    full(("h1", s), pe.matmul(t[:], lhsT=wh1_sb[:], rhs=xnext, start=True, stop=True))
                    for a, name in enumerate(("f1a", "f1b")):
                        t = open_bank((name, s))
                        full((name, s), pe.matmul(t[:], lhsT=wf1_sb[:, a * D:(a + 1) * D], rhs=xnext, start=True, stop=True))
                    t = open_bank(("h2", s))
                    pe.wait_ge(act_done, act_at("tail", s, 0, 1))
                    full(("h2", s), pe.matmul(t[:], lhsT=wh2_sb[:], rhs=hh, start=True, stop=True))
                    t = open_bank(("f2", s))
                    for a in range(2):
                        pe.wait_ge(act_done, act_at("tail", s, 0, 2 + a))
                        last = pe.matmul(t[:], lhsT=wf2_sb[:, a, :], rhs=fh[:, a, :], start=(a == 0), stop=(a == 1))
                    full(("f2", s), last)
                elif stage == "fin":
                    t = open_bank((stage, s, 0))
                    pe.wait_ge(dve_done, dve_at("tail", s))
                    for i in range(NT):
                        last = pe.transpose(t[:, i * P:(i + 1) * P], zf[:, i * P:(i + 1) * P], ident)
                    full((stage, s, 0), last)

            for stage, b, k in order["pe"]:
                if (stage, b, k) in jobs and stage in PLACES | SETUP:
                    t = open_bank((stage, b, k))
                if stage == "cols":
                    pe.wait_ge(dve_done, dve_at("prep", 0))
                    pe.wait_ge(const_in, 16)
                    full((stage, b, k), pe.transpose(t[:, 0:2 * NG], qk_arr[:].rearrange("p j r -> p (j r)"), ident[0:2 * NG, 0:2 * NG]))
                elif stage == "vecs":
                    pe.wait_ge(vec_in, 16 * N_VEC)
                    full((stage, b, k), pe.transpose(t[:, 0:V_END], vec_rows[:], ident[0:V_END, 0:V_END]))
                elif stage == "ctxT":
                    pe.wait_ge(const_in, 16)
                    pe.wait_ge(ctx_in, 16 * N_CTX)
                    for i in range(B):
                        last = pe.transpose(t[:, i * KL:(i + 1) * KL], ctx_tok[:, i, :], ident[0:KL, 0:KL])
                    full((stage, b, k), last)
                elif stage == "kproj":
                    pe.wait_ge(act_done, act_at("ctxT", 0))
                    pe.wait_ge(dve_done, dve_at("prep", 0))
                    pe.matmul(t[:, 0:B * KL], lhsT=WkA[:, k], rhs=ctxT[:], start=True, stop=False)
                    full((stage, b, k), pe.matmul(t[:, 0:B * KL], lhsT=sel_mask[0:1], rhs=mask_row[0:1], start=False, stop=True))
                elif stage == "vproj":
                    pe.wait_ge(proj_in, 16 * N_PROJ)
                    for i in range(B):
                        last = pe.matmul(t[0:KL, i * D:(i + 1) * D], lhsT=ctxT[:, i * KL:(i + 1) * KL], rhs=Wv_sb[:], start=True, stop=True)
                    full((stage, b, k), last)
                elif stage == "xT":
                    pe.wait_ge(dve_done, dve_at("ln1x", b))
                    for i in range(NT):
                        last = pe.transpose(t[:, i * P:(i + 1) * P], xn[:, 0, i, :], ident)
                    full((stage, b, k), last)
                elif stage == "q":
                    pe.wait_ge(act_done, act_at("xT", b))
                    full((stage, b, k), pe.matmul(t[:], lhsT=WqA[:, k], rhs=xnT[:, b % 2, :], start=True, stop=True))
                elif stage == "S":
                    g, i = k // NT, k % NT
                    if b == 0 and k == 0:
                        pe.wait_ge(dve_done, dve_at("kproj", 0, NG - 1))
                    if i == 0:
                        pe.wait_ge(dve_done, dve_at("q", b, g))
                    full((stage, b, k), pe.matmul(t[:, 0:NS * KL], lhsT=qs[:, b % 2, g, i * P:(i + 1) * P],
                                                  rhs=KB[:, b, g], start=True, stop=True))
                elif stage == "mT":
                    pe.wait_ge(dve_done, dve_at("S", b, NG * NT - 1))
                    for i in range(NT):
                        last = pe.transpose(t[:, i * P:(i + 1) * P], m_tok[:, b % 2, i, :], ident)
                    full((stage, b, k), last)
                elif stage == "sc":
                    g, j, n = k // NS, k % NS, b * NH + k
                    if k == 0:
                        pe.wait_ge(act_done, act_at("mT", b))
                        pe.wait_ge(dve_done, dve_at("selmax", 0))
                    if n >= 3:
                        pe.wait_ge(act_done, act_at("exp", (n - 3) // NH, (n - 3) % NH))
                    pe.matmul(ST[n % 3][0:KL, :], lhsT=KB[:, b, g, j, :], rhs=qs[:, b % 2, g, :], start=True, stop=False)
                    pe.matmul(ST[n % 3][0:KL, :], lhsT=sel_max[:, NG * j + g, :], rhs=mT[:, b % 2, :],
                              start=False, stop=True).then_inc(scores_full, 1)
                elif stage == "pv":
                    g, j, n = k // NS, k % NS, b * NH + k
                    if b == 0 and k == 0:
                        pe.wait_ge(dve_done, dve_at("vproj", 0))
                    if b > 0 and k == 0:
                        pe.wait_ge(act_done, act_at("ev", b - 1))
                        pe.wait_ge(dve_done, dve_at("ev", b - 1))
                    pe.wait_ge(act_done, act_at("exp", b, k))
                    pe.matmul(NUM[ROWS * j:ROWS * (j + 1), :], lhsT=VB[:, b, j, g, :], rhs=PT[:, n % 3, :],
                              start=(g == 0), stop=(g == NG - 1))
                    pe.matmul(DEN[ROWS * j:ROWS * (j + 1), :], lhsT=OB[:, g, :], rhs=PT[:, n % 3, :],
                              start=(g == 0), stop=(g == NG - 1)).then_inc(pv_done, 1)
                elif stage == "o":
                    pe.wait_ge(dve_done, dve_at("norm", b))
                    for i in range(NT):
                        last = pe.matmul(t[:, i * P:(i + 1) * P], lhsT=oT[:, b % 2, i * P:(i + 1) * P], rhs=Wo_sb[:], start=True, stop=True)
                    full((stage, b, k), last)
                elif stage == "x2T":
                    pe.wait_ge(dve_done, dve_at("o2x", b))
                    for i in range(NT):
                        last = pe.transpose(t[:, i * P:(i + 1) * P], xn[:, 1, i, :], ident)
                    full((stage, b, k), last)
                elif stage == "r1":
                    if b == 0:
                        pe.wait_ge(ffnw_in, 16 * N_FFN)
                    pe.wait_ge(act_done, act_at("x2T", b))
                    full((stage, b, k), pe.matmul(t[0:D // 4, :], lhsT=w_r1_sb[:], rhs=xT[:, b, :], start=True, stop=True))
                elif stage == "lg":
                    pe.wait_ge(act_done, act_at("r1", b))
                    for i in range(NT):
                        last = pe.matmul(t[:, i * E:(i + 1) * E], lhsT=hr[:, i * P:(i + 1) * P], rhs=w_r2_sb[:], start=True, stop=True)
                    full((stage, b, k), last)
                elif stage == "bc":
                    pe.wait_ge(pool_done, pool_at("lgx", b, 0, k + 1))
                    if k % 2 == 0:
                        last = pe.matmul(t[:], lhsT=ones[:], rhs=diag_w[:, k // 2], start=True, stop=True)
                    else:
                        last = pe.matmul(t[:], lhsT=ones_bf[:], rhs=diag_i[:, k // 2], start=True, stop=True)
                    full((stage, b, k), last)
                else:
                    ffn_stage(stage, b, k)

        @block.scalar
        def _(act):
            n = [0]

            def step(ins):
                ins.then_inc(act_done, 1)
                n[0] += 1
                if n[0] > 1:
                    act.wait_ge(act_done, n[0] - 1)

            def settle():
                act.wait_ge(act_done, n[0])

            def rstd(r):
                step(act.activation(rs[:, r, 0, :], rs[:, r, 3, :], ACT.Ln))
                settle()
                step(act.activation(rs[:, r, 1, :], rs[:, r, 0, :], ACT.Exp, scale=-0.5))

            loaded = [None]

            def functions(chosen):
                if loaded[0] != chosen:
                    act.add_instruction(mybir.InstLoadActFuncSet(name=nc.get_next_instruction_name(), act_func_set_id=chosen, ins=[], outs=[]))
                    loaded[0] = chosen

            needs = {"ln1r": EXP_LN, "vecs": EXP_LN, "exp": EXP_LN, "o2r": EXP_LN, "r1": GELU_TANH, "lge": EXP_LN,
                     "w1": GELU_TANH, "tail": GELU_TANH, "gt": GELU_TANH, "sp": EXP_LN}
            functions(EXP_LN)
            for stage, b, k in order["act"]:
                if stage in needs:
                    functions(needs[stage])
                if stage == "ln1r":
                    act.wait_ge(dve_done, dve_at("ln1", b))
                    rstd(0)
                elif stage == "cols":
                    t = await_product(act, (stage, b, k))
                    qk = t[:, 0:2 * NG].rearrange("p (w g) -> p w g", w=2)
                    step(act.activation(qk_cols[:], qk, ACT.Copy))
                    for w, c in ((0, C_LO_Q), (1, C_LO_K)):
                        step(act.activation(qk_taken[:, w], qk[:, w], ACT.Copy, scale=cst[:, c:c + 1]))
                elif stage == "vecs":
                    t = await_product(act, (stage, b, k))
                    step(act.activation(cols[:], t[:, 0:V_END], ACT.Copy))
                    step(act.activation(shw[:, 1:2], shw[:, 0:1], ACT.Exp, scale=-1.0))
                elif stage == "ctxT":
                    t = await_product(act, (stage, b, k))
                    step(act.activation(ctxT[:], t[:, 0:B * KL], ACT.Copy))
                elif stage == "setup2":
                    settle()
                    step(act.activation(shw[:, 2:3], shw[:, 1:2], ACT.Identity, bias=1.0))
                elif stage in ("kproj", "q"):
                    t = await_product(act, (stage, b, k))
                    use = splits.index((stage, b, k))
                    if use >= 2:
                        act.wait_ge(dve_done, dve_at(*splits[use - 2]))
                    w = 0 if stage == "q" else 1
                    c, width = (C_LO_Q, C_LO_K)[w], (S, B * KL)[w]
                    step(act.activation(taken[:, use % 2, 0:width], t[:, 0:width], ACT.Identity,
                                        bias=qk_taken[:, w, k:k + 1], scale=cst[:, c:c + 1]))
                elif stage == "xT":
                    t = await_product(act, (stage, b, k))
                    if b >= 2:
                        await_product(act, ("q", b - 2, NG - 1))
                    step(act.activation(xnT[:, b % 2, :], t[:], ACT.Copy))
                elif stage == "ev":
                    act.wait_ge(pv_done, NH * (b + 1))
                    if b >= 2:
                        await_product(act, ("o", b - 2, 0))
                    step(act.activation(oT[:, b % 2, :], NUM[:], ACT.Copy))
                elif stage == "mT":
                    t = await_product(act, (stage, b, k))
                    if b >= 2:
                        act.wait_ge(scores_full, NH * (b - 1))
                    step(act.activation(mT[:, b % 2, :], t[:], ACT.Copy, scale=-1.0))
                elif stage == "exp":
                    i = b * NH + k
                    act.wait_ge(scores_full, i + 1)
                    if i == 0:
                        act.wait_ge(pool_done, POOL_CLEARS)
                    if i >= 3:
                        act.wait_ge(pv_done, i - 2)
                    step(act.activation(PT[0:KL, i % 3, :], ST[i % 3][0:KL, :], ACT.Exp, scale=float(DH) ** -0.5))
                elif stage == "o2r":
                    act.wait_ge(dve_done, dve_at("o", b))
                    rstd(1)
                elif stage == "x2T":
                    t = await_product(act, (stage, b, k))
                    step(act.activation(xT[:, b, :], t[:], ACT.Copy))
                elif stage == "r1":
                    t = await_product(act, (stage, b, k))
                    if b > 0:
                        act.wait_ge(dve_done, dve_at("lg", b - 1, 0, 1))
                    step(act.activation(hr[:], t[0:D // 4, :], ACT.Gelu, bias=cols[0:D // 4, V_BR1:V_BR1 + 1]))
                elif stage == "lge":
                    act.wait_ge(dve_done, dve_at("lg", b))
                    step(act.activation(wk[:, 1, :], wk[:, 0, :], ACT.Exp))
                elif stage == "bc":
                    t = await_product(act, (stage, b, k))
                    step(act.activation((Wb if k % 2 == 0 else Ib)[:, k // 2, b, :], t[:], ACT.Copy))
                elif stage == "w1":
                    s = b
                    if s > 0:
                        act.wait_ge(dve_done, dve_at("mask", s - 1, 1))
                        act.wait_ge(pool_done, pool_at("low", s - 1, 2))
                    else:
                        act.wait_ge(pool_done, pool_at("w2split", 0))
                    for j in range(NK + 1):
                        t = await_product(act, (stage, s, j))
                        step(act.activation(hid[:, j, :], t[:], ACT.Gelu, bias=cols[:, V_B1 + j:V_B1 + j + 1]))
                elif stage == "tail":
                    s = b
                    t = await_product(act, ("h1", s))
                    step(act.activation(hh, t[:], ACT.Gelu, bias=cols[:, V_BH1:V_BH1 + 1]))
                    for a, name in enumerate(("f1a", "f1b")):
                        t = await_product(act, (name, s))
                        step(act.activation(fh[:, a, :], t[:], ACT.Gelu, bias=cols[:, V_BF1 + a:V_BF1 + a + 1]))
                    if s > 0:
                        act.wait_ge(dve_done, dve_at("tail", s - 1))
                    t = await_product(act, ("h2", s))
                    step(act.activation(th[:], t[:], ACT.Tanh, bias=half[:, 2:3], scale=0.5))
                    t = await_product(act, ("f2", s))
                    step(act.activation(rf, t[:], ACT.Identity, bias=cols[:, V_BF2:V_BF2 + 1]))
                elif stage == "gt":
                    s, u = b, (3 * b + k) % 2
                    if 3 * s + k >= 2:
                        act.wait_ge(dve_done, dve_at("mix", (3 * s + k - 2) // 3, (3 * s + k - 2) % 3))
                    if k == 0 and s > 0:
                        act.wait_ge(pool_done, pool_at("add", s - 1, 1))
                    act.wait_ge(stream_full, chunk_no(s, k, 1) + 1)
                    step(act.activation(st_g[u], CT[u][1][:], ACT.Tanh, scale=0.5, **({"bias": half[:, 1:2]} if k == 0 else {})))
                    if s >= NB:
                        act.wait_ge(stream_full, chunk_no(s, k, 2) + 1)
                        step(act.activation(st_a[u], CT[u][2][:], ACT.Tanh, scale=0.5, **({"bias": half[:, 0:1]} if k == 0 else {})))
                elif stage == "sp":
                    u = (3 * b + k) % 2
                    act.wait_ge(dve_done, dve_at("cap", b, k))
                    step(act.activation(st_b[u], st_b[u], ACT.Exp))
                    settle()
                    step(act.activation(st_b[u], st_b[u], ACT.Ln, bias=1.0))
                if (stage, b, k) in act_at.before:
                    assert n[0] == act_at(stage, b, k), (stage, b, k, n[0], act_at(stage, b, k))

        @block.vector
        def _(dve):
            n = [0]

            def step(ins):
                ins.then_inc(dve_done, 1)
                n[0] += 1
                if n[0] > 1:
                    dve.wait_ge(dve_done, n[0] - 1)

            def settle():
                dve.wait_ge(dve_done, n[0])

            def row_stats(r, src):
                for t in range(NT):
                    step(dve.bn_stats(stats[:, r, t, :], src[:, t, :]))
                settle()
                for t in range(NT):
                    step(dve.bn_aggr(mv[:, r, t, :], stats[:, r, t, :]))
                settle()
                step(dve.tensor_scalar(rs[:, r, 3, :], mv[:, r, :, 1], EPS, None, ALU.add))

            def norm_rows(r, src):
                v, y, s1, y2 = rs[:, r, 3, :], rs[:, r, 1, :], rs[:, r, 2, :], rs[:, r, 4, :]
                step(dve.tensor_tensor(s1, y, y, ALU.mult))
                settle()
                step(dve.tensor_tensor(s1, s1, v, ALU.mult))
                settle()
                step(dve.tensor_scalar(s1, s1, -0.5, 1.5, ALU.mult, ALU.add))
                settle()
                step(dve.tensor_tensor(y2, y, s1, ALU.mult))
                settle()
                for t in range(NT):
                    step(dve.tensor_scalar(xn[:, r, t, :], src[:, t, :], mv[:, r, t, 0:1], rs[:, r, 4, t:t + 1],
                                           ALU.subtract, ALU.mult))

            for stage, b, k in order["dve"]:
                if stage == "ln1":
                    dve.wait_ge(x_in[b], 16)
                    row_stats(0, x_tok[:, b])
                elif stage == "ln1x":
                    dve.wait_ge(act_done, act_at("ln1r", b))
                    if b > 0:
                        await_product(dve, ("xT", b - 1, 0))
                    norm_rows(0, x_tok[:, b])
                elif stage == "clear":
                    for t in (WqA[:], WkA[:], qk_arr[:], sel_mask[:], KB[:].bitcast(F32), OB[:]):
                        step(dve.memset(t, 0.0))
                    step(dve.memset(ones[:], 1.0))
                    step(dve.memset(ones_bf[:], 1.0))
                    step(dve.memset(qk_arr[0:NG, :, ONE_ROW:ONE_ROW + 1], 1.0))
                    step(dve.memset(sel_mask[0:1, :, ONE_ROW:ONE_ROW + 1], 1.0))
                    for g in range(NG):
                        step(dve.memset(OB[:, g, DH * g:DH * (g + 1)], 1.0))
                elif stage == "prep":
                    dve.wait_ge(attw_in, 16 * N_ATT)
                    settle()
                    for arr, w in ((WkA, Wk_sb), (WqA, Wq_sb)):
                        wv = w[:].rearrange("p (j g d) -> p g j d", j=NS, g=NG)
                        for part in range(3):
                            step(dve.tensor_copy(arr[:, :, :, part * DH:(part + 1) * DH], wv))
                    for part in range(3):
                        step(dve.tensor_copy(qk_arr[:, :, part * DH:(part + 1) * DH], qk_rows[:]))
                    step(dve.tensor_scalar(mask_row[:], mask_words[:].bitcast(U8), NEG, None, ALU.mult))
                elif stage == "selmax":
                    dve.wait_ge(const_in, 16)
                    step(dve.tensor_copy(sel_max[:], ident[:, 0:NH].unsqueeze(2).to_broadcast([P, NH, KL])))
                elif stage in ("kproj", "q"):
                    t = await_product(dve, (stage, b, k))
                    dve.wait_ge(act_done, act_at(stage, b, k))
                    high = taken[:, splits.index((stage, b, k)) % 2, :].bitcast(F32)
                    if stage == "q":
                        if b >= 2:
                            dve.wait_ge(scores_full, NH * (b - 2) + NS * (k + 1))
                        step(dve.scalar_tensor_tensor(qs[:, b % 2, k, :], t[:], qk_cols[:, 0, k:k + 1], high, ALU.add, ALU.subtract))
                    else:
                        for j in range(NS):
                            r = slice(ROWS * j, ROWS * (j + 1))
                            step(dve.scalar_tensor_tensor(
                                KB[r, :, k, j, :], t[r, 0:B * KL].rearrange("p (b k) -> p b k", b=B), qk_cols[r, 1, k:k + 1],
                                high[r, 0:B * KL].rearrange("p (b k) -> p b k", b=B), ALU.add, ALU.subtract))
                elif stage == "vproj":
                    t = await_product(dve, (stage, b, k))
                    dve.wait_ge(pool_done, POOL_CLEARS)
                    for g in range(NG):
                        step(dve.tensor_tensor(
                            VB[0:KL, :, :, g, DH * g:DH * (g + 1)],
                            t[0:KL, :].rearrange("p (b j g d) -> p b j g d", b=B, j=NS, g=NG)[:, :, :, g, :],
                            bv_row[:].rearrange("p (j g d) -> p j g d", j=NS, g=NG)[:, :, g, :].unsqueeze(1).to_broadcast([KL, B, NS, DH]),
                            ALU.add))
                elif stage == "setup2":
                    dve.wait_ge(ffnw_in, 16 * N_FFN)
                    dve.wait_ge(act_done, act_at("setup2", 0))
                    step(dve.tensor_scalar(half[:, 0:1], cols[:, V_BS2:V_BS2 + 1], 0.5, None, ALU.mult))
                    step(dve.tensor_scalar(half[:, 1:2], cols[:, V_BS2 + 2:V_BS2 + 3], 0.5, None, ALU.mult))
                    step(dve.tensor_scalar(half[:, 2:3], bh2[:], 0.5, None, ALU.mult))
                    step(dve.tensor_scalar(half[:, 3:4], cols[:, V_IW:V_IW + 1], 0.5, None, ALU.mult))
                    step(dve.reciprocal(half[:, 4:5], shw[:, 2:3]))
                    settle()
                    step(dve.tensor_scalar(half[:, 5:6], half[:, 4:5], -1.0, 1.0, ALU.mult, ALU.add))
                    step(dve.tensor_copy(wh2_sb[:], wh2_col[:].to_broadcast([P, P])))
                    step(dve.tensor_copy(b2_hi[:], b2_rep[:]))
                    settle()
                    step(dve.scalar_tensor_tensor(b2_rep[:], b2_hi[:], cst[0:3 * E, C_SPLIT1:C_SPLIT1 + 1], b2_rep[:], ALU.mult, ALU.add))
                    settle()
                    step(dve.tensor_copy(b2_hi[:], b2_rep[:]))
                    settle()
                    step(dve.scalar_tensor_tensor(b2_s[0:3 * E, :], b2_hi[:], cst[0:3 * E, C_SPLIT2:C_SPLIT2 + 1], b2_rep[:], ALU.mult, ALU.add))
                elif stage == "S":
                    g, i = k // NT, k % NT
                    if b >= 2 and k == 0:
                        await_product(dve, ("mT", b - 2, 0))
                    elif k == 0:
                        dve.wait_ge(pool_done, POOL_CLEARS)
                    t = await_product(dve, (stage, b, k))
                    heads = m_tok[:, b % 2, i, 0:NH].rearrange("p (j g) -> p g j", g=NG)[:, g, :]
                    step(dve.tensor_reduce(heads, t[:, 0:NS * KL].rearrange("p (j k) -> p j k", j=NS), AX_X, ALU.max))
                elif stage == "ev":
                    dve.wait_ge(pv_done, NH * (b + 1))
                    step(dve.tensor_copy(rden[:], DEN[:]))
                elif stage == "norm":
                    settle()
                    step(dve.reciprocal(rden[:], rden[:]))
                    settle()
                    dve.wait_ge(act_done, act_at("ev", b))
                    step(dve.tensor_tensor(oT[:, b % 2, :], oT[:, b % 2, :], rden[:], ALU.mult))
                elif stage == "o":
                    t = await_product(dve, (stage, b, k))
                    dve.wait_ge(pool_done, pool_at("xbo", b))
                    step(dve.tensor_tensor(x_tok[:, b].rearrange("p t d -> p (t d)"), t[:], x_tok[:, b].rearrange("p t d -> p (t d)"), ALU.add))
                    settle()
                    row_stats(1, x_tok[:, b])
                elif stage == "o2x":
                    dve.wait_ge(act_done, act_at("o2r", b))
                    if b > 0:
                        await_product(dve, ("x2T", b - 1, 0))
                    norm_rows(1, x_tok[:, b])
                elif stage == "lg":
                    t = await_product(dve, (stage, b, k))
                    step(dve.tensor_tensor(logits[:], t[:, 0:NT * E].rearrange("p (t e) -> p t e", e=E),
                                           br2_row[:].unsqueeze(1).to_broadcast([P, NT, E]), ALU.add))
                    settle()
                    if b > 0:
                        dve.wait_ge(pool_done, pool_at("lgx", b - 1))
                    for i in range(NT):
                        step(dve.max(mx[:, i, :], logits[:, i, :]))
                    settle()
                    for i in range(NT):
                        step(dve.max_index(mi[:, i, :], mx[:, i, :], logits[:, i, :]))
                    step(dve.tensor_tensor(wk[:, 0, :], mx[:, :, 1], mx[:, :, 0], ALU.subtract))
                    step(dve.tensor_copy(idxf[:], mi[:, :, 0:2].rearrange("p t s -> p s t")))
                elif stage == "lgx":
                    dve.wait_ge(act_done, act_at("lge", b))
                    step(dve.tensor_scalar(wk[:, 2, :], wk[:, 1, :], 1.0, None, ALU.add))
                    settle()
                    step(dve.reciprocal(wk[:, 3, :], wk[:, 2, :]))
                    settle()
                    step(dve.tensor_scalar(wk[:, 4, :], wk[:, 3, :], half[:, 5:6], None, ALU.mult))
                    settle()
                    step(dve.tensor_tensor(wk[:, 5, :], wk[:, 4, :], wk[:, 1, :], ALU.mult))
                elif stage == "bc" and k % 2:
                    dve.wait_ge(act_done, act_at("bc", b, k))
                    step(dve.tensor_scalar(OH[:, k // 2, b, :], Ib[:, k // 2, b, :], cst[:, C_ONEHOT:C_ONEHOT + 1], None, ALU.is_equal))
                elif stage == "round":
                    if b > 0:
                        dve.wait_ge(stream_full, chunk_no(b - 1, 1, 0))
                        dve.wait_ge(pool_done, pool_at("low", b - 1, 2))
                    dve.wait_ge(act_done, act_at("w1", b))
                    step(dve.tensor_copy(shared_hi[:], hid[:, NK, :]))
                elif stage == "mask":
                    s, c = b, b % NB
                    if s > 0:
                        dve.wait_ge(stream_full, chunk_no(s - 1, k + 1, chunks(s - 1)))
                    else:
                        dve.wait_ge(scores_full, B * NH)
                    if (s, k) > (0, 0):
                        dve.wait_ge(pool_done, pool_at("low", s if k else s - 1, 1 - k))

                    def rounded(j):
                        step(dve.tensor_copy(mask_hi[:, k * NK + j, :], masked[:, j, :]))
                    for j in range(NK):
                        if k == 0:
                            dve.wait_ge(act_done, act_at("w1", s, 0, j + 1))
                        step(dve.scalar_tensor_tensor(masked[:, j, :], Ib[:, k, c, :], cst[:, C_EXPERT + j:C_EXPERT + j + 1],
                                                      hid[:, j, :], ALU.is_equal, ALU.mult))
                        if j > 0:
                            rounded(j - 1)
                    rounded(NK - 1)
                elif stage == "cap":
                    u = (3 * b + k) % 2
                    dve.wait_ge(stream_full, chunk_no(b, k, 0) + 1)
                    if k == 0:
                        if b > 0:
                            dve.wait_ge(pool_done, pool_at("add", b - 1, 1))
                        step(dve.tensor_scalar(st_b[u], CT[u][0][:], cols[:, V_BS2 + 1:V_BS2 + 2], SOFTPLUS_CAP, ALU.add, ALU.min))
                    else:
                        step(dve.tensor_scalar(st_b[u], CT[u][0][:], SOFTPLUS_CAP, None, ALU.min))
                elif stage == "mix":
                    s, c, i = b, b % NB, 3 * b + k
                    u, second = i % 2, b >= NB
                    gate, beta, alpha = st_g[u], st_b[u], st_a[u]
                    w = None if k == 0 else Wb[:, k - 1, c, :]
                    sw = half[:, 4:5]
                    bias = cols[:, V_BS2 + 1:V_BS2 + 2]
                    if k == 0:
                        dve.wait_ge(act_done, act_at("sp", s, k))
                        step(dve.scalar_tensor_tensor(beta, CT[u][0][:], bias, beta, ALU.add, ALU.max))
                        step(dve.tensor_scalar(nerr, xT[:, c, :], -1.0, cols[:, V_MU:V_MU + 1], ALU.mult, ALU.add))
                        dve.wait_ge(act_done, act_at("gt", s, k))
                        if not second:
                            step(dve.tensor_scalar(acc_a, beta, sw, None, ALU.mult))
                            settle()
                            step(dve.scalar_tensor_tensor(acc_g, gate, 1.0, acc_a, ALU.add, ALU.mult))
                        else:
                            step(dve.tensor_scalar(gate, gate, 1.0, sw, ALU.add, ALU.mult))
                            settle()
                            step(dve.tensor_tensor(acc_g, gate, beta, ALU.mult))
                            step(dve.scalar_tensor_tensor(acc_a, alpha, 1.0, gate, ALU.add, ALU.mult))
                    elif not second:
                        dve.wait_ge(act_done, act_at("sp", s, k))
                        step(dve.tensor_tensor(beta, CT[u][0][:], beta, ALU.max))
                        settle()
                        step(dve.tensor_tensor(beta, beta, w, ALU.mult))
                        settle()
                        dve.wait_ge(act_done, act_at("gt", s, k))
                        step(dve.scalar_tensor_tensor(gate, gate, 1.0, beta, ALU.add, ALU.mult))
                        if k == 2:
                            dve.wait_ge(pool_done, pool_at("add", s, 1))
                            step(dve.tensor_tensor(acc_a, acc_a, beta, ALU.add))
                            step(dve.tensor_tensor(acc_g, acc_g, gate, ALU.add))
                            step(dve.tensor_tensor(vT[:, c, :], acc_a, nerr, ALU.mult))
                            step(dve.scalar_tensor_tensor(acc_g, acc_g, DT / 2, nerr, ALU.mult, ALU.mult))
                            settle()
                            step(dve.tensor_tensor(xnext, acc_g, xT[:, c, :], ALU.add))
                    else:
                        def softplus():
                            dve.wait_ge(act_done, act_at("sp", s, k))
                            step(dve.tensor_tensor(beta, CT[u][0][:], beta, ALU.max))
                        if max_read(s, k) == 1:
                            softplus()
                        dve.wait_ge(act_done, act_at("gt", s, k))
                        step(dve.scalar_tensor_tensor(gate, gate, 1.0, w, ALU.add, ALU.mult))
                        settle()
                        step(dve.scalar_tensor_tensor(alpha, alpha, 1.0, gate, ALU.add, ALU.mult))
                        if k == 2:
                            dve.wait_ge(pool_done, pool_at("add", s, 1))
                            settle()
                            step(dve.tensor_tensor(acc_a, acc_a, alpha, ALU.add))
                            settle()
                            step(dve.scalar_tensor_tensor(acc_a, acc_a, DT / 4, vT[:, c, :], ALU.mult, ALU.mult))
                            settle()
                            step(dve.tensor_tensor(acc_a, acc_a, xT[:, c, :], ALU.add))
                        if max_read(s, k) > 1:
                            softplus()
                        settle()
                        step(dve.tensor_tensor(beta, gate, beta, ALU.mult))
                        if k == 2:
                            settle()
                            step(dve.tensor_tensor(acc_g, acc_g, beta, ALU.add))
                            settle()
                            step(dve.scalar_tensor_tensor(acc_g, acc_g, DT / 2, nerr, ALU.mult, ALU.mult))
                            settle()
                            step(dve.tensor_tensor(xnext, acc_g, acc_a, ALU.add))
                elif stage == "tail":
                    s, c = b, b % NB
                    dve.wait_ge(act_done, act_at("tail", s))
                    settle()
                    step(dve.scalar_tensor_tensor(tmp, th[:], 1.0, rf, ALU.add, ALU.mult))
                    settle()
                    step(dve.scalar_tensor_tensor(xT[:, c, :] if s < NB else zf, tmp, half[:, 3:4], xT[:, c, :], ALU.mult, ALU.add))
                elif stage == "fin":
                    c = b % NB
                    t = await_product(dve, (stage, b, k))
                    step(dve.tensor_tensor(x_tok[:, c].rearrange("p t d -> p (t d)"), t[:], x_tok[:, c].rearrange("p t d -> p (t d)"), ALU.add))
                if (stage, b, k) in dve_at.before:
                    assert n[0] == dve_at(stage, b, k), (stage, b, k, n[0], dve_at(stage, b, k))


INPUTS = ["x", "ctx_1024", "mask_BxS2_bf0", "L0_xattn_Wq", "L0_xattn_bq", "L0_xattn_Wk", "L0_xattn_bk", "L0_xattn_Wv",
          "L0_xattn_bv", "L0_xattn_Wo", "L0_xattn_bo", "L0_ffn_w_r1", "L0_ffn_b_r1", "L0_ffn_w_r2", "L0_ffn_b_r2",
          "L0_ffn_w_h1", "L0_ffn_b_h1", "L0_ffn_w_h2", "L0_ffn_b_h2", "L0_ffn_expert_w1", "L0_ffn_expert_b1",
          "L0_ffn_expert_w2", "L0_ffn_expert_b2", "L0_ffn_w_s1", "L0_ffn_b_s1", "L0_ffn_w_s2", "L0_ffn_b_s2",
          "L0_ffn_shared_weight", "L0_ffn_w_f1", "L0_ffn_b_f1", "L0_ffn_w_f2", "L0_ffn_b_f2",
          "L0_ffn_integration_weight", "L0_ffn_mu"]


def kernel(**inputs):
    import concourse.bacc as bacc
    from concourse.bass_utils import run_bass_kernel_spmd

    nc = bacc.Bacc("TRN2", target_bir_lowering=False, num_devices=1)
    arrays, args = {}, []
    for name in INPUTS + ["shape_constants"]:
        a = np.ascontiguousarray(shape_constants() if name == "shape_constants" else inputs[name])
        if a.dtype == np.bool_:
            a = a.reshape(-1).view(np.uint32)
        if a.ndim == 0:
            a = a.reshape(1)
        arrays[f"in_{name}_dram"] = a
        args.append(nc.dram_tensor(f"in_{name}_dram", a.shape, mybir.dt.from_np(a.dtype), kind="ExternalInput").ap())
    args.append(nc.dram_tensor("out_0_dram", (B, S, D), F32, kind="ExternalOutput").ap())
    xattn_moe_kernel(nc, *args)
    r = run_bass_kernel_spmd(nc, [arrays], core_ids=[0])
    return r.results[0]["out_0_dram"]
```

```python
from contextlib import ExitStack

import numpy as np

import concourse.bass as bass
from concourse import mybir

F32 = mybir.dt.float32
F32R = mybir.dt.float32r
BF16 = mybir.dt.bfloat16
U32 = mybir.dt.uint32
U8 = mybir.dt.uint8
ACT = mybir.ActivationFunctionType
ALU = mybir.AluOpType
AX_X = mybir.AxisListType.X

P = 128
B, S, D = 4, 512, 128
KL = 77
NH, DH = 16, 8
NG = 4
NS = 4
ROWS = 32
ONE_ROW = 3 * DH
NT = S // P
E, H = 8, 64
NK = E * H // P
NB = B
LAST = 2 * NB - 1
NEG = -float(2 ** 100)
EPS = 1e-5
DT = 0.1
SOFTPLUS_CAP = 40.0
EXP_LN, GELU_TANH = 6, 10
G_BANKS = 3
MASK_ROUNDED = (3, 5, 7, 8)
POOL_CLEARS = 8

C_IDENT, C_EXPERT, C_ONEHOT, C_LO_Q, C_LO_K, C_SPLIT1, C_SPLIT2, C_END = 0, 128, 132, 133, 134, 135, 136, 137

V_B1, V_BS1, V_BF1, V_BF2, V_MU, V_IW, V_BH1, V_BR1, V_BS2, V_END = 0, 4, 5, 7, 8, 9, 10, 11, 12, 16


def shape_constants():
    c = np.zeros((P, C_END), np.float32)
    p = np.arange(P)
    c[:, C_IDENT:C_IDENT + P] = np.eye(P)
    for k in range(NK):
        c[:, C_EXPERT + k] = 2 * k + p // H
    c[:, C_ONEHOT] = np.where(p < 3 * E, p % E, -1)
    part = p % ROWS // DH
    c[:, C_LO_Q] = np.where(part == 2, 1, 0)
    c[:, C_LO_K] = np.where(part == 1, 1, 0)
    c[:, C_SPLIT1] = np.where(p >= E, -1, 0)
    c[:, C_SPLIT2] = np.where(p >= 2 * E, -1, 0)
    return c


PLACES = {
    "ln1": ((None, None, -38.33, None), 0), "ln1r": ((None, -34.38, None, None), 0),
    "ln1x": ((None, None, -35.65, None), 0), "xbo": ((None, None, None, -35.18), 0),
    "xT": ((-30.94, -29.86, None, None), 0), "q": ((-29.33, -28.18, -28, None), 3.55),
    "S": ((-16, None, -15.6, None), 0.75), "mT": ((-2.68, -2.18, None, None), 0),
    "sc": ((-1.87, None, None, None), 1), "exp": ((None, 0, None, None), 1), "pv": ((1.53, None, None, None), 1),
    "ev": ((None, 15.87, 16.7, None), 0), "norm": ((None, None, 17.18, None), 0),
    "o": ((19.71, None, 20.67, None), 0), "o2r": ((None, 20.0, None, None), 0), "o2x": ((None, None, 21.76, None), 0),
    "x2T": ((23.44, 24.51, None, None), 0), "r1": ((25.21, 26.73, None, None), 0),
    "lg": ((27.27, None, 27.65, None), 0), "lge": ((None, 30.03, None, None), 0),
    "lgx": ((None, None, 29.53, 33.17), 0), "bc": ((33.12, 33.72, 34.51, None), 1.47),
}
SETUP = {
    "selmax": ((None, None, -16.06, None), 0), "clear": ((None, None, -61.93, None), 0),
    "vecs": ((-4.61, -3.97, None, None), 0), "prep": ((None, None, -38.69, None), 0),
    "cols": ((-36, -33.14, None, None), 0), "ctxT": ((-41.13, -34.9, None, None), 0),
    "kput": ((None, -30.294999999999998, None, None), 0.01), "kproj": ((-33.99, -30.31, -30.84, None), 0.01),
    "vproj": ((-17.39, None, -16.97, None), 0), "setup2": ((None, 2.53, 2.39, None), 0),
    "w2split": ((None, None, None, -3.23), 0), "w1split": ((None, None, None, 6.31), 0),
}
FIRST_FFN = {
    ("halves", 0, 0): (None, 62.4, None, 63.27), ("round", 0, 0): (None, None, 75.16, None),
    ("low", 0, 0): (None, None, None, 74), ("low", 0, 2): (None, None, None, 75.4),
    ("w1", 0, 0): (64.57, 65.2, None, None), ("mask", 0, 0): (None, None, 73.44, None),
    ("mask", 0, 1): (None, None, 80.85, None), ("w2", 0, 0): (75.48, None, None, None),
}
STEP = 24
FFN_PLACES = {
    ("halves", 0): (None, -23.08, None, -22.08), ("w1", 0): (-16.58, -15.58, None, None),
    ("mask", 0): (None, None, -12.64, None), ("mask", 1): (None, None, 3.09, None),
    ("round", 0): (None, None, -9.58, None), ("low", 0): (None, None, None, -3.39),
    ("low", 2): (None, None, None, -6.88), ("low", 1): (None, None, None, 6), ("add", 1): (None, None, None, 18.74),
    ("w2", 0): (1.2, None, None, None), ("w2", 1): (2.24, None, None, None), ("w2", 2): (16.33, None, None, None),
    ("cap", 0): (None, None, 0.6, None), ("cap", 1): (None, None, 6.61, None), ("cap", 2): (None, None, 19.57, None),
    ("sp", 0): (None, 2.8, None, None), ("sp", 1): (None, 9.03, None, None), ("sp", 2): (None, 20.25, None, None),
    ("gt", 0): (None, 7.4, None, None), ("gt", 1): (None, 7.67, None, None), ("gt", 2): (None, 12.64, None, None),
    ("mix", 0): (None, None, 8.69, None), ("mix", 1): (None, None, 15.38, None),
    ("mix", 2): (None, None, 25.07, None), ("tail", 0): (28.64, 31.76, None, None),
    ("tail", 1): (36.41, 34.46, 40.81, None), ("fin", 0): (46.94, None, 49.93, None),
}
TAIL = (("h1", "f1a", "f1b"), ("h2", "f2"))
LAST_FFN = {
    ("sp", 7, 2): (None, 182.97, None, None), ("gt", 7, 2): (None, 185.95, None, None),
    ("mix", 7, 2): (None, None, 192.87, None), ("fin", 6, 0): (194.02, None, 195.02, None),
}
ENGINES = ("pe", "act", "dve", "pool")
STAGE_COUNT = {"q": NG, "S": NG * NT, "sc": NH, "exp": NH, "pv": NH, "bc": 4, "kproj": NG, "kput": NG}


def engine_order(engine):
    e = ENGINES.index(engine)
    placed = []
    for table, batches in ((PLACES, B), (SETUP, 1)):
        for stage, (at, pitch) in table.items():
            if at[e] is not None:
                placed += [(at[e] + NH * b + pitch * k, (stage, b, k)) for b in range(batches) for k in range(STAGE_COUNT.get(stage, 1))]
    placed += [(at[e], key) for key, at in FIRST_FFN.items() if at[e] is not None]
    placed.sort(key=lambda item: item[0])
    order = [key for at, key in placed]
    placed = [(STEP * s + at[e], (stage, s, k)) for (stage, k), at in FFN_PLACES.items() if at[e] is not None for s in range(2 * NB)]
    placed = [(LAST_FFN[key][e] if key in LAST_FFN else at, key) for at, key in placed]
    placed = [(at, key) for at, key in placed if key not in order and (key[0] != "fin" or key[1] >= NB)]
    placed.sort(key=lambda item: item[0])
    return order + [key for at, key in placed]


def act_steps(stage, i, k):
    if stage == "tail":
        return len(TAIL[k]) * len(parts(i))
    if stage in ("gt", "halves"):
        return 1 if i < NB else 3 if (stage, i, k) == ("gt", LAST, 2) else 2
    return {"ln1r": 2, "cols": 3, "vecs": 2, "ctxT": 1, "kput": 2, "kproj": 1, "setup2": 1, "xT": 1, "q": 1, "mT": 1, "exp": 1, "ev": 1, "o2r": 2,
            "x2T": 1, "r1": 1, "lge": 1, "bc": 1, "w1": NK + 1, "sp": 2}.get(stage, 0)


def dve_steps(stage, i, k):
    if stage == "mix":
        return (4, 3, 8)[k] if i < NB else (5, 4, 10 if i < LAST else 13)[k]
    if stage == "fin":
        return len(parts(i))
    if stage == "tail":
        return 2 * len(parts(i))
    if stage == "bc":
        return k % 2
    return {"ln1": 9, "ln1x": 8, "clear": 14, "prep": 10, "selmax": 1, "kproj": 3, "vproj": NG, "setup2": 11, "q": 1, "S": 1, "ev": 1, "norm": 2,
            "o": 10, "o2x": 8, "lg": 11, "lgx": 4, "round": 1, "mask": 2 * NK, "cap": 1}.get(stage, 0)


def pool_steps(stage, i, k):
    if stage == "halves":
        return 1 if i < NB else 2
    return {"xbo": 1, "w1split": 2, "lgx": 4, "w2split": 2, "low": NK if k < 2 else 1, "add": 2}.get(stage, 0)


def max_read(s, k):
    return 5 if (s, k) == (LAST, 2) else 1


def parts(s):
    return [slice(0, S)] if s < 2 * NB - 1 else [slice(0, S // 2), slice(S // 2, S)]


class Done:

    def __init__(self, order, steps, total=0):
        self.before, self.steps = {}, steps
        for stage in order:
            self.before[stage] = total
            total += steps(*stage)

    def __call__(self, stage, b, k=0, i=None):
        return self.before[(stage, b, k)] + (self.steps(stage, b, k) if i is None else i)


def bank_jobs(order):
    jobs, used, turn = {}, [0] * G_BANKS, 0
    for stage, b, k in order:
        if stage == "w1":
            keys = [("w1", b, j) for j in range(NK + 1)]
        elif stage == "tail":
            keys = [(j, b, h) for h in range(len(parts(b))) for j in TAIL[k]]
        elif stage == "fin":
            keys = [("fin", b, h) for h in range(len(parts(b)))]
        elif stage in ("cols", "vecs", "ctxT", "kproj", "vproj", "xT", "q", "mT", "S", "o", "x2T", "r1", "lg", "bc"):
            keys = [(stage, b, k)]
        else:
            keys = []
        for key in keys:
            bank = turn % (2 if stage in ("w1", "tail", "fin") and b >= NB - 1 else G_BANKS)
            jobs[key] = (bank, used[bank])
            used[bank] += 1
            turn = bank + 1
    return jobs


def xattn_moe_kernel(nc, x, ctx, mask, Wq, bq, Wk, bk, Wv, bv, Wo, bo, w_r1, b_r1, w_r2, b_r2, w_h1, b_h1,
                     w_h2, b_h2, e_w1, e_b1, e_w2, e_b2, w_s1, b_s1, w_s2, b_s2, shared_weight, w_f1, b_f1,
                     w_f2, b_f2, iw, mu, consts, out):
    order = {e: engine_order(e) for e in ENGINES}
    jobs = bank_jobs(order["pe"])
    act_at, dve_at = Done(order["act"], act_steps), Done(order["dve"], dve_steps)
    pool_at = Done(order["pool"], pool_steps, POOL_CLEARS + 1)
    with ExitStack() as stack:
        def sb(name, shape, dt=F32):
            return stack.enter_context(nc.sbuf_tensor(name, shape, dt))

        def sem(name):
            return stack.enter_context(nc.semaphore(name))

        cst = sb("cst", [P, C_END])
        ident = cst[:, C_IDENT:C_IDENT + P]
        ident_bf = sb("ident_bf", [P, P], BF16)
        ones = sb("ones", [P, P])
        ones_bf = sb("ones_bf", [P, P], BF16)
        x_tok = sb("x_tok", [P, B, NT, D])
        bo_row = sb("bo_row", [P, D])
        stats = sb("stats", [P, 2, NT, 6])
        mv = sb("mv", [P, 2, NT, 2])
        rs = sb("rs", [P, 2, 5, NT])
        xn = sb("xn", [P, 2, NT, D])
        xnT = sb("xnT", [P, 2, S])
        taken = sb("taken", [P, 2, S], F32R)
        qs = sb("qs", [P, 2, NG, S], F32R)
        KB = sb("KB", [P, B, NG, NS, KL], F32R)
        VB = sb("VB", [P, B, NS, NG, ROWS])
        OB = sb("OB", [P, NG, ROWS])
        ctx_tok = sb("ctx_tok", [P, B, D])
        ctxT = sb("ctxT", [P, B * KL])
        bv_row = sb("bv_row", [KL, D])
        mask_words = sb("mask_words", [1, B * KL // 4], U32)
        mask_row = sb("mask_row", [1, B * KL])
        sel_mask = sb("sel_mask", [1, NS, ROWS])
        qk_rows = sb("qk_rows", [2 * NG, NS, DH])
        qk_arr = sb("qk_arr", [2 * NG, NS, ROWS])
        qk_cols = sb("qk_cols", [P, 2, NG])
        qk_taken = sb("qk_taken", [P, 2, NG])
        W_att = sb("W_att", [P, 4, D])
        Wq_sb, Wk_sb, Wv_sb, Wo_sb = (W_att[:, i, :] for i in range(4))
        WqA = sb("WqA", [P, NG, NS, ROWS])
        WkA = sb("WkA", [P, NG, NS, ROWS])
        sel_max = sb("sel_max", [P, NH, KL], F32R)
        m_tok = sb("m_tok", [P, 2, NT, P])
        mT = sb("mT", [P, 2, S], F32R)
        PT = sb("PT", [P, 3, S])
        rden = sb("rden", [P, S])
        oT = sb("oT", [P, 2, S])
        w_r1_sb = sb("w_r1_sb", [P, D // 4])
        w_r2_sb = sb("w_r2_sb", [D // 4, E])
        br2_row = sb("br2_row", [P, E])
        hr = sb("hr", [D // 4, S])
        logits = sb("logits", [P, NT, E])
        mx = sb("mx", [P, NT, 8])
        mi = sb("mi", [P, NT, 8], U32)
        wk = sb("wk", [P, 6, NT])
        idxf = sb("idxf", [P, 2, NT])
        diag_w = sb("diag_w", [P, 2, NT, P])
        diag_i = sb("diag_i", [P, 2, NT, P], BF16)
        vec_rows = sb("vec_rows", [V_END, P])
        cols = sb("cols", [P, V_END])
        half = sb("half", [P, 6])
        bh2 = sb("bh2", [P, 1])
        shw = sb("shw", [P, 3])
        w1_hi = sb("w1_hi", [P, 2, NK + 1, P], F32R)
        w1_lo = sb("w1_lo", [P, 2, NK + 1, P], F32R)
        w2_hi = sb("w2_hi", [P, NK + 1, 3 * D], F32R)
        w2_lo = sb("w2_lo", [P, NK + 1, 3 * D], F32R)
        b2_hi = sb("b2_hi", [3 * E, 3 * D], BF16)
        b2_s = sb("b2_s", [P, 3 * D], BF16)
        wf1_sb = sb("wf1_sb", [P, 2 * D])
        wf2_sb = sb("wf2_sb", [P, 2, D])
        wh1_sb = sb("wh1_sb", [P, P])
        wh2_col = sb("wh2_col", [P, 1])
        wh2_sb = sb("wh2_sb", [P, P])
        xT = sb("xT", [P, NB, S])
        Wb = sb("Wb", [P, 2, NB, S])
        Ib = sb("Ib", [P, 2, NB, S], BF16)
        OH = sb("OH", [P, 2, NB, S], BF16)
        hid = sb("hid", [P, NK + 1, S])
        w2_in = hid[:].rearrange("p j s -> p (j s)")[:, 0:(NK + 1) * 3 * D].rearrange("p (j o) -> p j o", o=3 * D)
        masked = sb("masked", [P, NK, S])
        staged = masked[:].rearrange("p j s -> p (j s)")
        w1_in = staged[:, 0:2 * (NK + 1) * P].rearrange("p (f j n) -> p f j n", f=2, j=NK + 1)
        b2_rep = staged[0:3 * E, 3 * S:3 * S + 3 * D]
        shared_hi = sb("shared_hi", [P, S], F32R)
        keys_split = Wb[:].rearrange("p u b s -> p (u b s)")[:, 0:2 * B * KL].rearrange("p (i b k) -> p i b k", i=2, b=B)
        mask_hi = qs[:].rearrange("p u g s -> p (u g) s")
        mask_lo = KB[:].rearrange("p b g j k -> p (b g j k)")[:, 0:2 * NK * S].rearrange("p (u s) -> p u s", s=S)
        shared_lo = taken[:, 0, :]
        vT = VB[:].rearrange("p b j g r -> p b (j g r)")
        flat = [t[:].rearrange("p u t d -> p u (t d)") for t in (xn, m_tok)]
        st_b, st_g = [flat[0][:, 0, :], xnT[:, 1, :]], [flat[1][:, u, :] for u in range(2)]
        st_a = [t[:].rearrange("p g j r -> p (g j r)") for t in (WqA, WkA)]
        acc_g, acc_a = oT[:, 0, :], xnT[:, 0, :]
        nerr, tmp = ctx_tok[:].rearrange("p b d -> p (b d)"), W_att[:].rearrange("p w d -> p (w d)")
        x_hi, x_lo = (sel_max[:].rearrange("p h k -> p (h k)")[:, i * S:(i + 1) * S] for i in range(2))
        v_hi, v_lo = taken[:, 1, :], mT[:, 0, :]
        xnext, hh = oT[:, 1, :], flat[0][:, 1, :]
        fh = diag_w[:].rearrange("p u t d -> p u (t d)")
        th, rf, zf = rden, PT[:, 0, :], PT[:, 1, :]

        bank = [stack.enter_context(nc.psum_tensor(f"bank{i}", [P, 512], F32)) for i in range(8)]
        G = bank[0:3]
        ST = bank[3:6]
        NUM, DEN = bank[6], bank[7]
        CT = [[bank[3], bank[4], bank[5]], [bank[6], bank[7], bank[2]]]

        const_in, vec_in, attw_in, ctx_in, proj_in, ffnw_in = (
            sem(n) for n in ("const_in", "vec_in", "attw_in", "ctx_in", "proj_in", "ffnw_in"))
        x_in = [sem(f"x_in{b}") for b in range(B)]
        out_done = sem("out_done")
        act_done, dve_done, pool_done = sem("act_done"), sem("dve_done"), sem("pool_done")
        bank_full = [sem(f"bank_full{i}") for i in range(G_BANKS)]
        scores_full, pv_done, stream_full = sem("scores_full"), sem("pv_done"), sem("stream_full")

        block = stack.enter_context(nc.Block())
        N_VEC, N_ATT, N_CTX, N_PROJ, N_FFN = 11, 5, 1, 5, 18

        def chunks(s):
            return 2 if s < NB else 3

        def chunk_order(s, k):
            return [0, 2, 1] if (s, k) == (LAST, 2) else [0, 1, 2][:chunks(s)] if k < 2 else [1, 2, 0] if s >= NB else [1, 0]

        def chunk_no(s, k, q):
            if k == 2 and q < chunks(s):
                q = chunk_order(s, k).index(q)
            return sum(3 * chunks(i) for i in range(s)) + k * chunks(s) + q

        def read_by(key):
            kind, b, *k = key
            if kind in ("cols", "vecs", "ctxT", "xT", "mT", "x2T", "r1", "bc"):
                return act_done, act_at(*key)
            if kind in ("kproj", "vproj", "q", "S"):
                return dve_done, dve_at(*key)
            if kind == "fin":
                return dve_done, dve_at("fin", b, 0, k[0] + 1)
            if kind in ("o", "lg"):
                return dve_done, dve_at(kind, b, 0, 1)
            if kind == "w1":
                return act_done, act_at("w1", b, 0, k[0] + 1)
            part = int(kind in TAIL[1])
            return act_done, act_at("tail", b, part, k[0] * len(TAIL[part]) + TAIL[part].index(kind) + 1)

        before = {}
        for key, (i, n) in jobs.items():
            if n:
                before[key] = next(o for o, at in jobs.items() if at == (i, n - 1))
        last_g2 = next(o for o, at in jobs.items() if at == (2, max(n for i, n in jobs.values() if i == 2)))
        splits = [("kproj", 0, g) for g in range(NG)] + [("q", b, g) for b in range(B) for g in range(NG)]

        def await_product(eng, key):
            i, n = jobs[key]
            eng.wait_ge(bank_full[i], n + 1)
            return G[i]

        @block.sync
        def _(sp):
            def load(dst, src, signal):
                with nc.allow_non_contiguous_dma(reason="small parameters"):
                    sp.dma_start(dst, src).then_inc(signal, 16)

            def row(v):
                return v.rearrange("(a n) -> a n", a=1)

            load(x_tok[:, 0], x[0].rearrange("(t p) d -> p t d", p=P), x_in[0])
            load(cst[:], consts, const_in)
            load(ctx_tok[0:KL], ctx.rearrange("b k d -> k b d"), ctx_in)
            load(Wk_sb, Wk, attw_in)
            load(Wq_sb, Wq, attw_in)
            load(qk_rows[0:NG], bq.rearrange("(j g d) -> g j d", j=NS, g=NG), attw_in)
            load(qk_rows[NG:2 * NG], bk.rearrange("(j g d) -> g j d", j=NS, g=NG), attw_in)
            load(mask_words[:], row(mask), attw_in)
            load(Wv_sb, Wv, proj_in)
            load(bv_row[:], bv.partition_broadcast(KL), proj_in)
            load(Wo_sb, Wo, proj_in)
            load(bo_row[:], bo.partition_broadcast(P), proj_in)
            load(br2_row[:], b_r2.partition_broadcast(P), proj_in)
            load(x_tok[:, 1], x[1].rearrange("(t p) d -> p t d", p=P), x_in[1])
            sp.wait_ge(pool_done, 4)
            load(vec_rows[V_B1:V_B1 + 4, :], e_b1.rearrange("(k e) h -> k (e h)", e=2), vec_in)
            load(vec_rows[V_BS1:V_BS1 + 1, 0:H], row(b_s1), vec_in)
            load(vec_rows[V_BS1:V_BS1 + 1, H:P], row(b_s1), vec_in)
            load(vec_rows[V_BF1:V_BF1 + 2, :], b_f1.rearrange("(a n) -> a n", a=2), vec_in)
            load(vec_rows[V_BF2:V_BF2 + 1, :], row(b_f2), vec_in)
            load(vec_rows[V_MU:V_MU + 1, :], row(mu), vec_in)
            load(vec_rows[V_IW:V_IW + 1, :], row(iw), vec_in)
            load(vec_rows[V_BH1:V_BH1 + 1, 0:D // 4], row(b_h1), vec_in)
            load(vec_rows[V_BR1:V_BR1 + 1, 0:D // 4], row(b_r1), vec_in)
            load(vec_rows[V_BS2:V_BS2 + 3, :], b_s2.rearrange("(a n) -> a n", a=3), vec_in)
            load(shw[:, 0:1], shared_weight.partition_broadcast(P), vec_in)
            for b in range(2, B):
                load(x_tok[:, b], x[b].rearrange("(t p) d -> p t d", p=P), x_in[b])
            load(w_r1_sb[:], w_r1, ffnw_in)
            load(w_r2_sb[:], w_r2, ffnw_in)
            for f in range(2):
                load(w1_in[:, f, 0:NK].rearrange("c j (e h) -> c (j e) h", e=2), e_w1.rearrange("e (f c) h -> f c e h", f=2)[f], ffnw_in)
                for r in range(2):
                    load(w1_in[:, f, NK, r * H:(r + 1) * H], w_s1.rearrange("(f c) h -> f c h", f=2)[f], ffnw_in)
            load(w2_in[:, 0:NK], e_w2.rearrange("(k e) h o -> (e h) k o", e=2), ffnw_in)
            load(w2_in[0:H, NK], w_s2, ffnw_in)
            for r in range(3):
                load(b2_rep[r * E:(r + 1) * E], e_b2, ffnw_in)
            load(wf1_sb[:], w_f1, ffnw_in)
            load(wf2_sb[:], w_f2.rearrange("(a c) n -> c a n", a=2), ffnw_in)
            load(wh1_sb[:, 0:D // 4], w_h1, ffnw_in)
            load(wh2_col[0:D // 4], w_h2, ffnw_in)
            load(bh2[:], b_h2.partition_broadcast(P), ffnw_in)
            for b in range(B):
                cut = parts(NB + b)
                for h, part in enumerate(cut):
                    sp.wait_ge(dve_done, dve_at("fin", NB + b, 0, h + 1))
                    tiles = slice(part.start // P, part.stop // P)
                    sp.dma_start(out[b].rearrange("(t p) d -> p t d", p=P)[:, tiles], x_tok[:, b, tiles]).then_inc(out_done, 16)
            sp.wait_ge(out_done, 16 * sum(len(parts(NB + b)) for b in range(B)))

        @block.gpsimd
        def _(pool):
            n = [0]

            def step(ins):
                ins.then_inc(pool_done, 1)
                n[0] += 1
                if n[0] > 1:
                    pool.wait_ge(pool_done, n[0] - 1)

            def clears():
                tiles = [vec_rows[:], w2_in[:, NK], wh1_sb[:], wh2_col[:], VB[:], m_tok[:], PT[:], b2_s[:]]
                assert len(tiles) == POOL_CLEARS
                for t in tiles:
                    step(pool.memset(t, 0.0))
                pool.wait_ge(const_in, 16)
                step(pool.tensor_copy(ident_bf[:], ident))

            clears()
            for stage, b, k in order["pool"]:
                if stage == "w1split":
                    pool.wait_ge(ffnw_in, 16 * N_FFN)
                    step(pool.tensor_copy(w1_hi[:], w1_in))
                    pool.wait_ge(pool_done, n[0])
                    step(pool.tensor_tensor(w1_lo[:], w1_in, w1_hi[:].bitcast(F32), ALU.subtract))
                elif stage == "halves":
                    pool.wait_ge(act_done, act_at("halves", b))
                    step(pool.tensor_tensor(x_lo, xT[:, b % NB, :], x_hi.bitcast(F32), ALU.subtract))
                    if b >= NB:
                        step(pool.tensor_tensor(v_lo, vT[:, b % NB, :], v_hi.bitcast(F32), ALU.subtract))
                elif stage == "w2split":
                    pool.wait_ge(ffnw_in, 16 * N_FFN)
                    step(pool.tensor_copy(w2_hi[:], w2_in))
                    pool.wait_ge(pool_done, n[0])
                    step(pool.tensor_tensor(w2_lo[:], w2_in, w2_hi[:].bitcast(F32), ALU.subtract))
                elif stage == "low" and k < 2:
                    if b == 0:
                        pool.wait_ge(scores_full, B * NH)
                    else:
                        pool.wait_ge(stream_full, chunk_no(b - 1, k + 1, chunks(b - 1)))
                    for j in range(NK):
                        pool.wait_ge(dve_done, dve_at("mask", b, k, MASK_ROUNDED[j]))
                        step(pool.tensor_tensor(mask_lo[:, k * NK + j, :], masked[:, j, :], mask_hi[:, k * NK + j, :].bitcast(F32), ALU.subtract))
                elif stage == "low":
                    pool.wait_ge(dve_done, dve_at("round", b))
                    if b > 0:
                        pool.wait_ge(stream_full, chunk_no(b - 1, 1, 0))
                    step(pool.tensor_tensor(shared_lo, hid[:, NK, :], shared_hi[:].bitcast(F32), ALU.subtract))
                elif stage == "add":
                    u = (3 * b + k) % 2
                    pool.wait_ge(dve_done, dve_at("mix", b, k))
                    step(pool.tensor_tensor(acc_a, acc_a, st_b[u] if b < NB else st_a[u], ALU.add))
                    step(pool.tensor_tensor(acc_g, acc_g, st_g[u] if b < NB else st_b[u], ALU.add))
                elif stage == "xbo":
                    pool.wait_ge(proj_in, 16 * N_PROJ)
                    pool.wait_ge(dve_done, dve_at("ln1x", b))
                    step(pool.tensor_tensor(x_tok[:, b], x_tok[:, b], bo_row[:].unsqueeze(1).to_broadcast([P, NT, D]), ALU.add))
                elif stage == "lgx":
                    pool.wait_ge(dve_done, dve_at("lgx", b))
                    if b > 0:
                        pool.wait_ge(act_done, act_at("bc", b - 1, 3))
                    eye = ident.unsqueeze(1).to_broadcast([P, NT, P])
                    for slot in range(2):
                        w = wk[:, 4 + slot, :].unsqueeze(2).to_broadcast([P, NT, P])
                        e = idxf[:, slot, :].unsqueeze(2).to_broadcast([P, NT, P])
                        step(pool.tensor_tensor(diag_w[:, slot], eye, w, ALU.mult))
                        step(pool.tensor_tensor(diag_i[:, slot], eye, e, ALU.mult))

        @block.tensor
        def _(pe):
            def open_bank(key):
                if key in before:
                    pe.wait_ge(*read_by(before[key]))
                return G[jobs[key][0]]

            def full(key, last):
                last.then_inc(bank_full[jobs[key][0]], 1)

            def ffn_stage(stage, s, k):
                c, second = s % NB, s >= NB
                if stage == "w1":
                    if s == 0:
                        pe.wait_ge(pool_done, pool_at("w1split", 0))
                    pe.wait_ge(pool_done, pool_at("halves", s))
                    for j in range(NK + 1):
                        t = open_bank((stage, s, j))
                        for f in range(2 if second else 1):
                            hi, lo = (x_hi, x_lo) if f == 0 else (v_hi, v_lo)
                            pe.matmul(t[:], lhsT=w1_hi[:, f, j], rhs=hi, start=(f == 0), stop=False)
                            pe.matmul(t[:], lhsT=w1_lo[:, f, j], rhs=hi, start=False, stop=False)
                            last = pe.matmul(t[:], lhsT=w1_hi[:, f, j], rhs=lo, start=False, stop=(f == second))
                        full((stage, s, j), last)
                elif stage == "w2":
                    n = 3 * s + k
                    if n == 0:
                        pe.wait_ge(act_done, act_at("exp", B - 1, NH - 1))
                    if n == 1:
                        pe.wait_ge(act_done, act_at("ev", B - 1))
                        pe.wait_ge(dve_done, dve_at("ev", B - 1))
                    if n == 3 * NB + 1:
                        pe.wait_ge(*read_by(last_g2))
                    if n >= 2:
                        so, ko = (n - 2) // 3, (n - 2) % 3
                        pe.wait_ge(dve_done, dve_at("mix", so, ko, max_read(so, ko)))
                        pe.wait_ge(act_done, act_at("gt", so, ko))
                    if k == 0:
                        pe.wait_ge(pool_done, pool_at("low", s, 2))
                    else:
                        pe.wait_ge(dve_done, dve_at("mask", s, k - 1))
                    for q in chunk_order(s, k):
                        t = CT[n % 2][q]
                        o = D * (1, 2, 0)[q]
                        if k > 0:
                            pe.matmul(t[:], lhsT=b2_s[:, o:o + D], rhs=OH[:, k - 1, c, :], start=True, stop=False)
                            units = [(j, mask_hi[:, (k - 1) * NK + j, :], mask_lo[:, (k - 1) * NK + j, :]) for j in range(NK)]
                        else:
                            units = [(NK, shared_hi[:], shared_lo)]
                        for j, hi, lo in units:
                            pe.matmul(t[:], lhsT=w2_hi[:, j, o:o + D], rhs=hi, start=(k == 0), stop=False)
                            pe.matmul(t[:], lhsT=w2_lo[:, j, o:o + D], rhs=hi, start=False, stop=False)
                        if k > 0 and q == chunk_order(s, k)[0]:
                            pe.wait_ge(pool_done, pool_at("low", s, k - 1))
                        for j, hi, lo in units:
                            last = pe.matmul(t[:], lhsT=w2_hi[:, j, o:o + D], rhs=lo, start=False, stop=(j == units[-1][0]))
                        last.then_inc(stream_full, 1)
                elif stage == "tail" and k == 0:
                    for h, part in enumerate(parts(s)):
                        pe.wait_ge(dve_done, dve_at("mix", s, 2) - len(parts(s)) + h + 1)
                        for name, lhsT in (("h1", wh1_sb[:]), ("f1a", wf1_sb[:, 0:D]), ("f1b", wf1_sb[:, D:2 * D])):
                            t = open_bank((name, s, h))
                            full((name, s, h), pe.matmul(t[:, part], lhsT=lhsT, rhs=xnext[:, part], start=True, stop=True))
                elif stage == "tail":
                    for h, part in enumerate(parts(s)):
                        t = open_bank(("h2", s, h))
                        pe.wait_ge(act_done, act_at("tail", s, 0, 3 * h + 1))
                        full(("h2", s, h), pe.matmul(t[:, part], lhsT=wh2_sb[:], rhs=hh[:, part], start=True, stop=True))
                        t = open_bank(("f2", s, h))
                        for a in range(2):
                            pe.wait_ge(act_done, act_at("tail", s, 0, 3 * h + 2 + a))
                            last = pe.matmul(t[:, part], lhsT=wf2_sb[:, a, :], rhs=fh[:, a, part], start=(a == 0), stop=(a == 1))
                        full(("f2", s, h), last)
                elif stage == "fin":
                    for h, part in enumerate(parts(s)):
                        t = open_bank((stage, s, h))
                        pe.wait_ge(dve_done, dve_at("tail", s, 1, len(parts(s)) + h + 1))
                        for i in range(part.start, part.stop, P):
                            last = pe.transpose(t[:, i:i + P], zf[:, i:i + P], ident)
                        full((stage, s, h), last)

            for stage, b, k in order["pe"]:
                if (stage, b, k) in jobs and stage in PLACES | SETUP:
                    t = open_bank((stage, b, k))
                if stage == "cols":
                    pe.wait_ge(dve_done, dve_at("prep", 0))
                    pe.wait_ge(const_in, 16)
                    full((stage, b, k), pe.transpose(t[:, 0:2 * NG], qk_arr[:].rearrange("p j r -> p (j r)"), ident[0:2 * NG, 0:2 * NG]))
                elif stage == "vecs":
                    pe.wait_ge(vec_in, 16 * N_VEC)
                    full((stage, b, k), pe.transpose(t[:, 0:V_END], vec_rows[:], ident[0:V_END, 0:V_END]))
                elif stage == "ctxT":
                    pe.wait_ge(const_in, 16)
                    pe.wait_ge(ctx_in, 16 * N_CTX)
                    for i in range(B):
                        last = pe.transpose(t[:, i * KL:(i + 1) * KL], ctx_tok[0:KL, i, :], ident[0:KL, 0:KL])
                    full((stage, b, k), last)
                elif stage == "kproj":
                    pe.wait_ge(act_done, act_at("ctxT", 0))
                    pe.wait_ge(dve_done, dve_at("prep", 0))
                    pe.matmul(t[:, 0:B * KL], lhsT=WkA[:, k], rhs=ctxT[:], start=True, stop=False)
                    full((stage, b, k), pe.matmul(t[:, 0:B * KL], lhsT=sel_mask[0:1], rhs=mask_row[0:1], start=False, stop=True))
                elif stage == "vproj":
                    pe.wait_ge(proj_in, 16 * N_PROJ)
                    for i in range(B):
                        last = pe.matmul(t[0:KL, i * D:(i + 1) * D], lhsT=ctxT[:, i * KL:(i + 1) * KL], rhs=Wv_sb, start=True, stop=True)
                    full((stage, b, k), last)
                elif stage == "xT":
                    pe.wait_ge(dve_done, dve_at("ln1x", b))
                    for i in range(NT):
                        last = pe.transpose(t[:, i * P:(i + 1) * P], xn[:, 0, i, :], ident)
                    full((stage, b, k), last)
                elif stage == "q":
                    pe.wait_ge(act_done, act_at("xT", b))
                    full((stage, b, k), pe.matmul(t[:], lhsT=WqA[:, k], rhs=xnT[:, b % 2, :], start=True, stop=True))
                elif stage == "S":
                    g, i = k // NT, k % NT
                    if b == 0 and k == 0:
                        pe.wait_ge(dve_done, dve_at("kproj", 0, NG - 1))
                        pe.wait_ge(act_done, act_at("kput", 0, NG - 1))
                    if i == 0:
                        pe.wait_ge(dve_done, dve_at("q", b, g))
                    full((stage, b, k), pe.matmul(t[:, 0:NS * KL], lhsT=qs[:, b % 2, g, i * P:(i + 1) * P],
                                                  rhs=KB[:, b, g], start=True, stop=True))
                elif stage == "mT":
                    pe.wait_ge(dve_done, dve_at("S", b, NG * NT - 1))
                    for i in range(NT):
                        last = pe.transpose(t[:, i * P:(i + 1) * P], m_tok[:, b % 2, i, :], ident)
                    full((stage, b, k), last)
                elif stage == "sc":
                    g, j, n = k // NS, k % NS, b * NH + k
                    if k == 0:
                        pe.wait_ge(act_done, act_at("mT", b))
                        pe.wait_ge(dve_done, dve_at("selmax", 0))
                    if n >= 3:
                        pe.wait_ge(act_done, act_at("exp", (n - 3) // NH, (n - 3) % NH))
                    pe.matmul(ST[n % 3][0:KL, :], lhsT=KB[:, b, g, j, :], rhs=qs[:, b % 2, g, :], start=True, stop=False)
                    pe.matmul(ST[n % 3][0:KL, :], lhsT=sel_max[:, NG * j + g, :], rhs=mT[:, b % 2, :],
                              start=False, stop=True).then_inc(scores_full, 1)
                elif stage == "pv":
                    g, j, n = k // NS, k % NS, b * NH + k
                    if b == 0 and k == 0:
                        pe.wait_ge(dve_done, dve_at("vproj", 0))
                    if b > 0 and k == 0:
                        pe.wait_ge(act_done, act_at("ev", b - 1))
                        pe.wait_ge(dve_done, dve_at("ev", b - 1))
                    pe.wait_ge(act_done, act_at("exp", b, k))
                    pe.matmul(NUM[ROWS * j:ROWS * (j + 1), :], lhsT=VB[:, b, j, g, :], rhs=PT[:, n % 3, :],
                              start=(g == 0), stop=(g == NG - 1))
                    pe.matmul(DEN[ROWS * j:ROWS * (j + 1), :], lhsT=OB[:, g, :], rhs=PT[:, n % 3, :],
                              start=(g == 0), stop=(g == NG - 1)).then_inc(pv_done, 1)
                elif stage == "o":
                    pe.wait_ge(dve_done, dve_at("norm", b))
                    for i in range(NT):
                        last = pe.matmul(t[:, i * P:(i + 1) * P], lhsT=oT[:, b % 2, i * P:(i + 1) * P], rhs=Wo_sb, start=True, stop=True)
                    full((stage, b, k), last)
                elif stage == "x2T":
                    pe.wait_ge(dve_done, dve_at("o2x", b))
                    for i in range(NT):
                        last = pe.transpose(t[:, i * P:(i + 1) * P], xn[:, 1, i, :], ident)
                    full((stage, b, k), last)
                elif stage == "r1":
                    if b == 0:
                        pe.wait_ge(ffnw_in, 16 * N_FFN)
                    pe.wait_ge(act_done, act_at("x2T", b))
                    full((stage, b, k), pe.matmul(t[0:D // 4, :], lhsT=w_r1_sb[:], rhs=xT[:, b, :], start=True, stop=True))
                elif stage == "lg":
                    pe.wait_ge(act_done, act_at("r1", b))
                    for i in range(NT):
                        last = pe.matmul(t[:, i * E:(i + 1) * E], lhsT=hr[:, i * P:(i + 1) * P], rhs=w_r2_sb[:], start=True, stop=True)
                    full((stage, b, k), last)
                elif stage == "bc":
                    pe.wait_ge(pool_done, pool_at("lgx", b, 0, k + 1))
                    if k % 2 == 0:
                        last = pe.matmul(t[:], lhsT=ones[:], rhs=diag_w[:, k // 2], start=True, stop=True)
                    else:
                        last = pe.matmul(t[:], lhsT=ones_bf[:], rhs=diag_i[:, k // 2], start=True, stop=True)
                    full((stage, b, k), last)
                else:
                    ffn_stage(stage, b, k)

        @block.scalar
        def _(act):
            n = [0]

            def step(ins):
                ins.then_inc(act_done, 1)
                n[0] += 1
                if n[0] > 1:
                    act.wait_ge(act_done, n[0] - 1)

            def settle():
                act.wait_ge(act_done, n[0])

            def rstd(r):
                step(act.activation(rs[:, r, 0, :], rs[:, r, 3, :], ACT.Ln))
                settle()
                step(act.activation(rs[:, r, 1, :], rs[:, r, 0, :], ACT.Exp, scale=-0.5))

            loaded = [None]

            def functions(chosen):
                if loaded[0] != chosen:
                    act.add_instruction(mybir.InstLoadActFuncSet(name=nc.get_next_instruction_name(), act_func_set_id=chosen, ins=[], outs=[]))
                    loaded[0] = chosen

            needs = {"ln1r": EXP_LN, "vecs": EXP_LN, "exp": EXP_LN, "o2r": EXP_LN, "r1": GELU_TANH, "lge": EXP_LN,
                     "w1": GELU_TANH, "tail": GELU_TANH, "gt": GELU_TANH, "sp": EXP_LN}
            functions(EXP_LN)
            for stage, b, k in order["act"]:
                if stage in needs:
                    functions(needs[stage])
                if stage == "ln1r":
                    act.wait_ge(dve_done, dve_at("ln1", b))
                    rstd(0)
                elif stage == "cols":
                    t = await_product(act, (stage, b, k))
                    qk = t[:, 0:2 * NG].rearrange("p (w g) -> p w g", w=2)
                    step(act.activation(qk_cols[:], qk, ACT.Copy))
                    for w, c in ((0, C_LO_Q), (1, C_LO_K)):
                        step(act.activation(qk_taken[:, w], qk[:, w], ACT.Copy, scale=cst[:, c:c + 1]))
                elif stage == "vecs":
                    t = await_product(act, (stage, b, k))
                    step(act.activation(cols[:], t[:, 0:V_END], ACT.Copy))
                    step(act.activation(shw[:, 1:2], shw[:, 0:1], ACT.Exp, scale=-1.0))
                elif stage == "ctxT":
                    t = await_product(act, (stage, b, k))
                    step(act.activation(ctxT[:], t[:, 0:B * KL], ACT.Copy))
                elif stage == "setup2":
                    settle()
                    step(act.activation(shw[:, 2:3], shw[:, 1:2], ACT.Identity, bias=1.0))
                elif stage in ("kproj", "q"):
                    t = await_product(act, (stage, b, k))
                    act.wait_ge(act_done, act_at("cols", 0))
                    use = splits.index((stage, b, k))
                    if use >= 2:
                        act.wait_ge(dve_done, dve_at(*splits[use - 2]))
                    w = 0 if stage == "q" else 1
                    c, width = (C_LO_Q, C_LO_K)[w], (S, B * KL)[w]
                    step(act.activation(taken[:, use % 2, 0:width], t[:, 0:width], ACT.Identity,
                                        bias=qk_taken[:, w, k:k + 1], scale=cst[:, c:c + 1]))
                elif stage == "kput":
                    act.wait_ge(dve_done, dve_at("kproj", 0, k, 1))
                    for j in (0, 1):
                        r = slice(ROWS * j, ROWS * (j + 1))
                        step(act.activation(KB[r, :, k, j, :], keys_split[r, k % 2], ACT.Copy))
                elif stage == "xT":
                    t = await_product(act, (stage, b, k))
                    if b >= 2:
                        await_product(act, ("q", b - 2, NG - 1))
                    step(act.activation(xnT[:, b % 2, :], t[:], ACT.Copy))
                elif stage == "ev":
                    act.wait_ge(pv_done, NH * (b + 1))
                    if b >= 2:
                        await_product(act, ("o", b - 2, 0))
                    step(act.activation(oT[:, b % 2, :], NUM[:], ACT.Copy))
                elif stage == "mT":
                    t = await_product(act, (stage, b, k))
                    if b >= 2:
                        act.wait_ge(scores_full, NH * (b - 1))
                    step(act.activation(mT[:, b % 2, :], t[:], ACT.Copy, scale=-1.0))
                elif stage == "exp":
                    i = b * NH + k
                    act.wait_ge(scores_full, i + 1)
                    if i == 0:
                        act.wait_ge(pool_done, POOL_CLEARS)
                    if i >= 3:
                        act.wait_ge(pv_done, i - 2)
                    step(act.activation(PT[0:KL, i % 3, :], ST[i % 3][0:KL, :], ACT.Exp, scale=float(DH) ** -0.5))
                elif stage == "o2r":
                    act.wait_ge(dve_done, dve_at("o", b))
                    rstd(1)
                elif stage == "x2T":
                    t = await_product(act, (stage, b, k))
                    step(act.activation(xT[:, b, :], t[:], ACT.Copy))
                elif stage == "r1":
                    t = await_product(act, (stage, b, k))
                    if b > 0:
                        act.wait_ge(dve_done, dve_at("lg", b - 1, 0, 1))
                    step(act.activation(hr[:], t[0:D // 4, :], ACT.Gelu, bias=cols[0:D // 4, V_BR1:V_BR1 + 1]))
                elif stage == "lge":
                    act.wait_ge(dve_done, dve_at("lg", b))
                    step(act.activation(wk[:, 1, :], wk[:, 0, :], ACT.Exp))
                elif stage == "bc":
                    t = await_product(act, (stage, b, k))
                    step(act.activation((Wb if k % 2 == 0 else Ib)[:, k // 2, b, :], t[:], ACT.Copy))
                elif stage == "halves":
                    s, c = b, b % NB
                    if s == 0:
                        act.wait_ge(scores_full, B * NH)
                        act.wait_ge(dve_done, dve_at("q", B - 1, NG - 1))
                    else:
                        await_product(act, ("w1", s - 1, NK))
                    if s >= NB:
                        act.wait_ge(dve_done, dve_at("tail", c, 1))
                    step(act.activation(x_hi, xT[:, c, :], ACT.Copy))
                    if s >= NB:
                        step(act.activation(v_hi, vT[:, c, :], ACT.Copy))
                elif stage == "w1":
                    s = b
                    if s > 0:
                        act.wait_ge(dve_done, dve_at("mask", s - 1, 1))
                        act.wait_ge(pool_done, pool_at("low", s - 1, 2))
                    else:
                        act.wait_ge(pool_done, pool_at("w2split", 0))
                    for j in range(NK + 1):
                        t = await_product(act, (stage, s, j))
                        step(act.activation(hid[:, j, :], t[:], ACT.Gelu, bias=cols[:, V_B1 + j:V_B1 + j + 1]))
                elif stage == "tail" and k == 0:
                    s = b
                    if s > 0:
                        await_product(act, ("f2", s - 1, 0))
                    for h, part in enumerate(parts(s)):
                        t = await_product(act, ("h1", s, h))
                        step(act.activation(hh[:, part], t[:, part], ACT.Gelu, bias=cols[:, V_BH1:V_BH1 + 1]))
                        for a, name in enumerate(("f1a", "f1b")):
                            t = await_product(act, (name, s, h))
                            step(act.activation(fh[:, a, part], t[:, part], ACT.Gelu, bias=cols[:, V_BF1 + a:V_BF1 + a + 1]))
                elif stage == "tail":
                    s = b
                    if s > 0:
                        act.wait_ge(dve_done, dve_at("tail", s - 1, 1))
                    for h, part in enumerate(parts(s)):
                        t = await_product(act, ("h2", s, h))
                        step(act.activation(th[:, part], t[:, part], ACT.Tanh, bias=half[:, 2:3], scale=0.5))
                        t = await_product(act, ("f2", s, h))
                        step(act.activation(rf[:, part], t[:, part], ACT.Identity, bias=cols[:, V_BF2:V_BF2 + 1]))
                elif stage == "gt":
                    s, u = b, (3 * b + k) % 2
                    if 3 * s + k >= 2:
                        act.wait_ge(dve_done, dve_at("mix", (3 * s + k - 2) // 3, (3 * s + k - 2) % 3))
                    if k == 0 and s > 0:
                        act.wait_ge(pool_done, pool_at("add", s - 1, 1))
                    if (s, k) == (LAST, 2):
                        act.wait_ge(stream_full, chunk_no(s, k, 2) + 1)
                        step(act.activation(st_a[u], CT[u][2][:], ACT.Tanh, scale=0.5))
                        act.wait_ge(stream_full, chunk_no(s, k, 1) + 1)
                        for part in parts(s):
                            step(act.activation(st_g[u][:, part], CT[u][1][:, part], ACT.Tanh, scale=0.5))
                        continue
                    act.wait_ge(stream_full, chunk_no(s, k, 1) + 1)
                    step(act.activation(st_g[u], CT[u][1][:], ACT.Tanh, scale=0.5, **({"bias": half[:, 1:2]} if k == 0 else {})))
                    if s >= NB:
                        act.wait_ge(stream_full, chunk_no(s, k, 2) + 1)
                        step(act.activation(st_a[u], CT[u][2][:], ACT.Tanh, scale=0.5, **({"bias": half[:, 0:1]} if k == 0 else {})))
                elif stage == "sp":
                    u = (3 * b + k) % 2
                    act.wait_ge(dve_done, dve_at("cap", b, k))
                    step(act.activation(st_b[u], st_b[u], ACT.Exp))
                    settle()
                    step(act.activation(st_b[u], st_b[u], ACT.Ln, bias=1.0))
                if (stage, b, k) in act_at.before:
                    assert n[0] == act_at(stage, b, k), (stage, b, k, n[0], act_at(stage, b, k))

        @block.vector
        def _(dve):
            n = [0]

            def step(ins):
                ins.then_inc(dve_done, 1)
                n[0] += 1
                if n[0] > 1:
                    dve.wait_ge(dve_done, n[0] - 1)

            def settle():
                dve.wait_ge(dve_done, n[0])

            def row_stats(r, src):
                for t in range(NT):
                    step(dve.bn_stats(stats[:, r, t, :], src[:, t, :]))
                settle()
                for t in range(NT):
                    step(dve.bn_aggr(mv[:, r, t, :], stats[:, r, t, :]))
                settle()
                step(dve.tensor_scalar(rs[:, r, 3, :], mv[:, r, :, 1], EPS, None, ALU.add))

            def norm_rows(r, src):
                v, y, s1, y2 = rs[:, r, 3, :], rs[:, r, 1, :], rs[:, r, 2, :], rs[:, r, 4, :]
                step(dve.tensor_tensor(s1, y, y, ALU.mult))
                settle()
                step(dve.tensor_tensor(s1, s1, v, ALU.mult))
                settle()
                step(dve.tensor_scalar(s1, s1, -0.5, 1.5, ALU.mult, ALU.add))
                settle()
                step(dve.tensor_tensor(y2, y, s1, ALU.mult))
                settle()
                for t in range(NT):
                    step(dve.tensor_scalar(xn[:, r, t, :], src[:, t, :], mv[:, r, t, 0:1], rs[:, r, 4, t:t + 1],
                                           ALU.subtract, ALU.mult))

            for stage, b, k in order["dve"]:
                if stage == "ln1":
                    dve.wait_ge(x_in[b], 16)
                    row_stats(0, x_tok[:, b])
                elif stage == "ln1x":
                    dve.wait_ge(act_done, act_at("ln1r", b))
                    if b > 0:
                        await_product(dve, ("xT", b - 1, 0))
                    norm_rows(0, x_tok[:, b])
                elif stage == "clear":
                    for t in (WqA[:], WkA[:], qk_arr[:], sel_mask[:], KB[:].bitcast(F32), OB[:]):
                        step(dve.memset(t, 0.0))
                    step(dve.memset(ones[:], 1.0))
                    step(dve.memset(ones_bf[:], 1.0))
                    step(dve.memset(qk_arr[0:NG, :, ONE_ROW:ONE_ROW + 1], 1.0))
                    step(dve.memset(sel_mask[0:1, :, ONE_ROW:ONE_ROW + 1], 1.0))
                    for g in range(NG):
                        step(dve.memset(OB[:, g, DH * g:DH * (g + 1)], 1.0))
                elif stage == "prep":
                    dve.wait_ge(attw_in, 16 * N_ATT)
                    settle()
                    for arr, w in ((WkA, Wk_sb), (WqA, Wq_sb)):
                        wv = w[:].rearrange("p (j g d) -> p g j d", j=NS, g=NG)
                        for part in range(3):
                            step(dve.tensor_copy(arr[:, :, :, part * DH:(part + 1) * DH], wv))
                    for part in range(3):
                        step(dve.tensor_copy(qk_arr[:, :, part * DH:(part + 1) * DH], qk_rows[:]))
                    step(dve.tensor_scalar(mask_row[:], mask_words[:].bitcast(U8), NEG, None, ALU.mult))
                elif stage == "selmax":
                    dve.wait_ge(const_in, 16)
                    step(dve.tensor_copy(sel_max[:], ident[:, 0:NH].unsqueeze(2).to_broadcast([P, NH, KL])))
                elif stage in ("kproj", "q"):
                    t = await_product(dve, (stage, b, k))
                    dve.wait_ge(act_done, act_at(stage, b, k))
                    high = taken[:, splits.index((stage, b, k)) % 2, :].bitcast(F32)
                    if stage == "q":
                        if b >= 2:
                            dve.wait_ge(scores_full, NH * (b - 2) + NS * (k + 1))
                        step(dve.scalar_tensor_tensor(qs[:, b % 2, k, :], t[:], qk_cols[:, 0, k:k + 1], high, ALU.add, ALU.subtract))
                    else:
                        if k >= 2:
                            dve.wait_ge(act_done, act_at("kput", 0, k - 2))
                        step(dve.scalar_tensor_tensor(
                            keys_split[:, k % 2], t[:, 0:B * KL].rearrange("p (b k) -> p b k", b=B), qk_cols[:, 1, k:k + 1],
                            high[:, 0:B * KL].rearrange("p (b k) -> p b k", b=B), ALU.add, ALU.subtract))
                        settle()
                        for j in (2, 3):
                            r = slice(ROWS * j, ROWS * (j + 1))
                            step(dve.tensor_copy(KB[r, :, k, j, :], keys_split[r, k % 2]))
                elif stage == "vproj":
                    t = await_product(dve, (stage, b, k))
                    dve.wait_ge(pool_done, POOL_CLEARS)
                    for g in range(NG):
                        step(dve.tensor_tensor(
                            VB[0:KL, :, :, g, DH * g:DH * (g + 1)],
                            t[0:KL, :].rearrange("p (b j g d) -> p b j g d", b=B, j=NS, g=NG)[:, :, :, g, :],
                            bv_row[:].rearrange("p (j g d) -> p j g d", j=NS, g=NG)[:, :, g, :].unsqueeze(1).to_broadcast([KL, B, NS, DH]),
                            ALU.add))
                elif stage == "setup2":
                    dve.wait_ge(ffnw_in, 16 * N_FFN)
                    dve.wait_ge(act_done, act_at("setup2", 0))
                    step(dve.tensor_scalar(half[:, 0:1], cols[:, V_BS2:V_BS2 + 1], 0.5, None, ALU.mult))
                    step(dve.tensor_scalar(half[:, 1:2], cols[:, V_BS2 + 2:V_BS2 + 3], 0.5, None, ALU.mult))
                    step(dve.tensor_scalar(half[:, 2:3], bh2[:], 0.5, None, ALU.mult))
                    step(dve.tensor_scalar(half[:, 3:4], cols[:, V_IW:V_IW + 1], 0.5, None, ALU.mult))
                    step(dve.reciprocal(half[:, 4:5], shw[:, 2:3]))
                    settle()
                    step(dve.tensor_scalar(half[:, 5:6], half[:, 4:5], -1.0, 1.0, ALU.mult, ALU.add))
                    step(dve.tensor_copy(wh2_sb[:], wh2_col[:].to_broadcast([P, P])))
                    step(dve.tensor_copy(b2_hi[:], b2_rep))
                    settle()
                    step(dve.scalar_tensor_tensor(b2_rep, b2_hi[:], cst[0:3 * E, C_SPLIT1:C_SPLIT1 + 1], b2_rep, ALU.mult, ALU.add))
                    settle()
                    step(dve.tensor_copy(b2_hi[:], b2_rep))
                    settle()
                    step(dve.scalar_tensor_tensor(b2_s[0:3 * E, :], b2_hi[:], cst[0:3 * E, C_SPLIT2:C_SPLIT2 + 1], b2_rep, ALU.mult, ALU.add))
                elif stage == "S":
                    g, i = k // NT, k % NT
                    if b >= 2 and k == 0:
                        await_product(dve, ("mT", b - 2, 0))
                    elif k == 0:
                        dve.wait_ge(pool_done, POOL_CLEARS)
                    t = await_product(dve, (stage, b, k))
                    heads = m_tok[:, b % 2, i, 0:NH].rearrange("p (j g) -> p g j", g=NG)[:, g, :]
                    step(dve.tensor_reduce(heads, t[:, 0:NS * KL].rearrange("p (j k) -> p j k", j=NS), AX_X, ALU.max))
                elif stage == "ev":
                    dve.wait_ge(pv_done, NH * (b + 1))
                    step(dve.tensor_copy(rden[:], DEN[:]))
                elif stage == "norm":
                    settle()
                    step(dve.reciprocal(rden[:], rden[:]))
                    settle()
                    dve.wait_ge(act_done, act_at("ev", b))
                    step(dve.tensor_tensor(oT[:, b % 2, :], oT[:, b % 2, :], rden[:], ALU.mult))
                elif stage == "o":
                    t = await_product(dve, (stage, b, k))
                    dve.wait_ge(pool_done, pool_at("xbo", b))
                    step(dve.tensor_tensor(x_tok[:, b].rearrange("p t d -> p (t d)"), t[:], x_tok[:, b].rearrange("p t d -> p (t d)"), ALU.add))
                    settle()
                    row_stats(1, x_tok[:, b])
                elif stage == "o2x":
                    dve.wait_ge(act_done, act_at("o2r", b))
                    if b > 0:
                        await_product(dve, ("x2T", b - 1, 0))
                    norm_rows(1, x_tok[:, b])
                elif stage == "lg":
                    t = await_product(dve, (stage, b, k))
                    step(dve.tensor_tensor(logits[:], t[:, 0:NT * E].rearrange("p (t e) -> p t e", e=E),
                                           br2_row[:].unsqueeze(1).to_broadcast([P, NT, E]), ALU.add))
                    settle()
                    if b > 0:
                        dve.wait_ge(pool_done, pool_at("lgx", b - 1))
                    for i in range(NT):
                        step(dve.max(mx[:, i, :], logits[:, i, :]))
                    settle()
                    for i in range(NT):
                        step(dve.max_index(mi[:, i, :], mx[:, i, :], logits[:, i, :]))
                    step(dve.tensor_tensor(wk[:, 0, :], mx[:, :, 1], mx[:, :, 0], ALU.subtract))
                    step(dve.tensor_copy(idxf[:], mi[:, :, 0:2].rearrange("p t s -> p s t")))
                elif stage == "lgx":
                    dve.wait_ge(act_done, act_at("lge", b))
                    step(dve.tensor_scalar(wk[:, 2, :], wk[:, 1, :], 1.0, None, ALU.add))
                    settle()
                    step(dve.reciprocal(wk[:, 3, :], wk[:, 2, :]))
                    settle()
                    step(dve.tensor_scalar(wk[:, 4, :], wk[:, 3, :], half[:, 5:6], None, ALU.mult))
                    settle()
                    step(dve.tensor_tensor(wk[:, 5, :], wk[:, 4, :], wk[:, 1, :], ALU.mult))
                elif stage == "bc" and k % 2:
                    dve.wait_ge(act_done, act_at("bc", b, k))
                    step(dve.tensor_scalar(OH[:, k // 2, b, :], Ib[:, k // 2, b, :], cst[:, C_ONEHOT:C_ONEHOT + 1], None, ALU.is_equal))
                elif stage == "round":
                    if b > 0:
                        dve.wait_ge(stream_full, chunk_no(b - 1, 1, 0))
                        dve.wait_ge(pool_done, pool_at("low", b - 1, 2))
                    dve.wait_ge(act_done, act_at("w1", b))
                    step(dve.tensor_copy(shared_hi[:], hid[:, NK, :]))
                elif stage == "mask":
                    s, c = b, b % NB
                    if s > 0:
                        dve.wait_ge(stream_full, chunk_no(s - 1, k + 1, chunks(s - 1)))
                    else:
                        dve.wait_ge(scores_full, B * NH)
                    if (s, k) > (0, 0):
                        dve.wait_ge(pool_done, pool_at("low", s if k else s - 1, 1 - k))

                    def rounded(j):
                        step(dve.tensor_copy(mask_hi[:, k * NK + j, :], masked[:, j, :]))
                    for j in range(NK):
                        if k == 0:
                            dve.wait_ge(act_done, act_at("w1", s, 0, j + 1))
                        step(dve.scalar_tensor_tensor(masked[:, j, :], Ib[:, k, c, :], cst[:, C_EXPERT + j:C_EXPERT + j + 1],
                                                      hid[:, j, :], ALU.is_equal, ALU.mult))
                        if j > 0:
                            rounded(j - 1)
                    rounded(NK - 1)
                elif stage == "cap":
                    u = (3 * b + k) % 2
                    dve.wait_ge(stream_full, chunk_no(b, k, 0) + 1)
                    if k == 0:
                        if b > 0:
                            dve.wait_ge(pool_done, pool_at("add", b - 1, 1))
                        step(dve.tensor_scalar(st_b[u], CT[u][0][:], cols[:, V_BS2 + 1:V_BS2 + 2], SOFTPLUS_CAP, ALU.add, ALU.min))
                    else:
                        step(dve.tensor_scalar(st_b[u], CT[u][0][:], SOFTPLUS_CAP, None, ALU.min))
                elif stage == "mix":
                    s, c, i = b, b % NB, 3 * b + k
                    u, second = i % 2, b >= NB
                    gate, beta, alpha = st_g[u], st_b[u], st_a[u]
                    w = None if k == 0 else Wb[:, k - 1, c, :]
                    sw = half[:, 4:5]
                    bias = cols[:, V_BS2 + 1:V_BS2 + 2]
                    if k == 0:
                        dve.wait_ge(act_done, act_at("sp", s, k))
                        step(dve.scalar_tensor_tensor(beta, CT[u][0][:], bias, beta, ALU.add, ALU.max))
                        step(dve.tensor_scalar(nerr, xT[:, c, :], -1.0, cols[:, V_MU:V_MU + 1], ALU.mult, ALU.add))
                        dve.wait_ge(act_done, act_at("gt", s, k))
                        if not second:
                            step(dve.tensor_scalar(acc_a, beta, sw, None, ALU.mult))
                            settle()
                            step(dve.scalar_tensor_tensor(acc_g, gate, 1.0, acc_a, ALU.add, ALU.mult))
                        else:
                            step(dve.tensor_scalar(gate, gate, 1.0, sw, ALU.add, ALU.mult))
                            settle()
                            step(dve.tensor_tensor(acc_g, gate, beta, ALU.mult))
                            step(dve.scalar_tensor_tensor(acc_a, alpha, 1.0, gate, ALU.add, ALU.mult))
                    elif not second:
                        dve.wait_ge(act_done, act_at("sp", s, k))
                        step(dve.tensor_tensor(beta, CT[u][0][:], beta, ALU.max))
                        settle()
                        step(dve.tensor_tensor(beta, beta, w, ALU.mult))
                        settle()
                        dve.wait_ge(act_done, act_at("gt", s, k))
                        step(dve.scalar_tensor_tensor(gate, gate, 1.0, beta, ALU.add, ALU.mult))
                        if k == 2:
                            dve.wait_ge(pool_done, pool_at("add", s, 1))
                            step(dve.tensor_tensor(acc_a, acc_a, beta, ALU.add))
                            step(dve.tensor_tensor(acc_g, acc_g, gate, ALU.add))
                            step(dve.tensor_tensor(vT[:, c, :], acc_a, nerr, ALU.mult))
                            step(dve.scalar_tensor_tensor(acc_g, acc_g, DT / 2, nerr, ALU.mult, ALU.mult))
                            settle()
                            step(dve.tensor_tensor(xnext, acc_g, xT[:, c, :], ALU.add))
                    elif (s, k) == (LAST, 2):
                        v, known = vT[:, c, :], acc_a
                        dve.wait_ge(pool_done, pool_at("add", s, 1))
                        step(dve.scalar_tensor_tensor(known, acc_a, DT / 4, v, ALU.mult, ALU.mult))
                        step(dve.scalar_tensor_tensor(acc_g, acc_g, DT / 2, nerr, ALU.mult, ALU.mult))
                        settle()
                        step(dve.tensor_tensor(known, known, acc_g, ALU.add))
                        settle()
                        step(dve.tensor_tensor(known, known, xT[:, c, :], ALU.add))
                        dve.wait_ge(act_done, act_at("sp", s, k))
                        step(dve.tensor_tensor(beta, CT[u][0][:], beta, ALU.max))
                        settle()
                        step(dve.scalar_tensor_tensor(beta, beta, 2.0, nerr, ALU.mult, ALU.mult))
                        dve.wait_ge(act_done, act_at("gt", s, k, 1))
                        step(dve.scalar_tensor_tensor(alpha, alpha, 1.0, v, ALU.add, ALU.mult))
                        settle()
                        step(dve.tensor_tensor(alpha, alpha, beta, ALU.add))
                        settle()
                        step(dve.scalar_tensor_tensor(alpha, alpha, DT / 4, w, ALU.mult, ALU.mult))
                        settle()
                        for h, part in enumerate(parts(s)):
                            dve.wait_ge(act_done, act_at("gt", s, k, h + 2))
                            step(dve.scalar_tensor_tensor(gate[:, part], gate[:, part], 1.0, alpha[:, part], ALU.add, ALU.mult))
                        for part in parts(s):
                            settle()
                            step(dve.tensor_tensor(xnext[:, part], known[:, part], gate[:, part], ALU.add))
                    else:
                        dve.wait_ge(act_done, act_at("sp", s, k))
                        step(dve.tensor_tensor(beta, CT[u][0][:], beta, ALU.max))
                        dve.wait_ge(act_done, act_at("gt", s, k))
                        step(dve.scalar_tensor_tensor(gate, gate, 1.0, w, ALU.add, ALU.mult))
                        settle()
                        step(dve.scalar_tensor_tensor(alpha, alpha, 1.0, gate, ALU.add, ALU.mult))
                        step(dve.tensor_tensor(beta, gate, beta, ALU.mult))
                        if k == 2:
                            dve.wait_ge(pool_done, pool_at("add", s, 1))
                            step(dve.tensor_tensor(acc_a, acc_a, alpha, ALU.add))
                            step(dve.tensor_tensor(acc_g, acc_g, beta, ALU.add))
                            step(dve.scalar_tensor_tensor(acc_a, acc_a, DT / 4, vT[:, c, :], ALU.mult, ALU.mult))
                            step(dve.scalar_tensor_tensor(acc_g, acc_g, DT / 2, nerr, ALU.mult, ALU.mult))
                            step(dve.tensor_tensor(acc_a, acc_a, xT[:, c, :], ALU.add))
                            settle()
                            step(dve.tensor_tensor(xnext, acc_g, acc_a, ALU.add))
                elif stage == "tail":
                    s, c = b, b % NB
                    settle()
                    for h, part in enumerate(parts(s)):
                        dve.wait_ge(act_done, act_at("tail", s, 1, 2 * h + 2))
                        step(dve.scalar_tensor_tensor(tmp[:, part], th[:, part], 1.0, rf[:, part], ALU.add, ALU.mult))
                    for part in parts(s):
                        settle()
                        to = xT[:, c, part] if s < NB else zf[:, part]
                        step(dve.scalar_tensor_tensor(to, tmp[:, part], half[:, 3:4], xT[:, c, part], ALU.mult, ALU.add))
                elif stage == "fin":
                    rows = x_tok[:, b % NB].rearrange("p t d -> p (t d)")
                    for h, part in enumerate(parts(b)):
                        t = await_product(dve, (stage, b, h))
                        step(dve.tensor_tensor(rows[:, part], t[:, part], rows[:, part], ALU.add))
                if (stage, b, k) in dve_at.before:
                    assert n[0] == dve_at(stage, b, k), (stage, b, k, n[0], dve_at(stage, b, k))


INPUTS = ["x", "ctx_1024", "mask_BxS2_bf0", "L0_xattn_Wq", "L0_xattn_bq", "L0_xattn_Wk", "L0_xattn_bk", "L0_xattn_Wv",
          "L0_xattn_bv", "L0_xattn_Wo", "L0_xattn_bo", "L0_ffn_w_r1", "L0_ffn_b_r1", "L0_ffn_w_r2", "L0_ffn_b_r2",
          "L0_ffn_w_h1", "L0_ffn_b_h1", "L0_ffn_w_h2", "L0_ffn_b_h2", "L0_ffn_expert_w1", "L0_ffn_expert_b1",
          "L0_ffn_expert_w2", "L0_ffn_expert_b2", "L0_ffn_w_s1", "L0_ffn_b_s1", "L0_ffn_w_s2", "L0_ffn_b_s2",
          "L0_ffn_shared_weight", "L0_ffn_w_f1", "L0_ffn_b_f1", "L0_ffn_w_f2", "L0_ffn_b_f2",
          "L0_ffn_integration_weight", "L0_ffn_mu"]


def kernel(**inputs):
    import concourse.bacc as bacc
    from concourse.bass_utils import run_bass_kernel_spmd

    nc = bacc.Bacc("TRN2", target_bir_lowering=False, num_devices=1)
    arrays, args = {}, []
    for name in INPUTS + ["shape_constants"]:
        a = np.ascontiguousarray(shape_constants() if name == "shape_constants" else inputs[name])
        if a.dtype == np.bool_:
            a = a.reshape(-1).view(np.uint32)
        if a.ndim == 0:
            a = a.reshape(1)
        arrays[f"in_{name}_dram"] = a
        args.append(nc.dram_tensor(f"in_{name}_dram", a.shape, mybir.dt.from_np(a.dtype), kind="ExternalInput").ap())
    args.append(nc.dram_tensor("out_0_dram", (B, S, D), F32, kind="ExternalOutput").ap())
    xattn_moe_kernel(nc, *args)
    r = run_bass_kernel_spmd(nc, [arrays], core_ids=[0])
    return r.results[0]["out_0_dram"]
```
